# Optimizing a Trainium2 kernel written in Bass

```python
import numpy as np
import jax
import jax.numpy as jnp

def _softmax(x, axis=-1):
    return jax.nn.softmax(x, axis=axis)

def _gelu(x):
    return jax.nn.gelu(x, approximate=True)

def _silu(x):
    return jax.nn.silu(x)

def _sigmoid(x):
    return jax.nn.sigmoid(x)

def _layernorm(x, axis=-1, eps=1e-05):
    m = jnp.mean(x, axis=axis, keepdims=True)
    v = jnp.var(x, axis=axis, keepdims=True)
    return (x - m) / jnp.sqrt(v + eps)

def _scatter_add(tgt, idx, src, axis=0):
    return tgt.at[idx].add(src)

def _segment_sum(src, seg, n):
    return jax.ops.segment_sum(src, seg, n)
kernel_name = 'mk_decoder_postln_d1_seqx_r4_4f0264'

def setup_inputs(seed: int=0):
    np.random.seed(seed)
    _w = jnp.asarray

    def _rec_inputs():
        import jax
        import jax.numpy as jnp
        _rk = jax.random.key(seed)
        x = 7.22e-05 + 1 * jax.random.normal(jax.random.fold_in(_rk, 1), (1, 2048, 256), jnp.float32)
        _lenS = 2048 - jax.random.randint(jax.random.fold_in(_rk, 7), (1,), 0, max(1, 2048 // 4) + 1, jnp.int32)
        _lenS2 = 1601 - jax.random.randint(jax.random.fold_in(_rk, 8), (1,), 0, max(1, 1601 // 4) + 1, jnp.int32)
        _ctx_1024P = jax.random.normal(jax.random.fold_in(_rk, 11), (1, 16, 256), jnp.float32)
        _ctx_1024c = jax.random.dirichlet(jax.random.fold_in(_rk, 511), 0.3 * jnp.ones((16,), jnp.float32), (1, 1601))
        _ctx_1024t = jnp.einsum('bsk,bkd->bsd', _ctx_1024c, _ctx_1024P)
        _ctx_1024t = _ctx_1024t * jax.lax.rsqrt(jnp.mean(jnp.square(_ctx_1024t)) + 1e-12) * 0.953939
        ctx_1024 = 4.13588e-05 + 0.999923 * (_ctx_1024t + 0.3 * jax.random.normal(jax.random.fold_in(_rk, 611), (1, 1601, 256), jnp.float32))
        return (x, ctx_1024)
    x, ctx_1024 = _rec_inputs()

    def _L0_attn_setup():
        import jax, jax.numpy as jnp
        import numpy as np
        EMBED_DIM = 256
        NUM_HEADS = 16
        HEAD_DIM = EMBED_DIM // NUM_HEADS
        key = jax.random.key(seed)
        k1, k2, k3 = jax.random.split(key, 3)
        inputs = jax.random.normal(k1, (4, 512, EMBED_DIM), dtype=jnp.float32)
        rotation_params = jax.random.normal(k2, (NUM_HEADS, HEAD_DIM), dtype=jnp.float32)
        entangle_params = jax.random.normal(k3, (NUM_HEADS, HEAD_DIM), dtype=jnp.float32)
        return {'inputs': inputs, 'rotation_params': rotation_params, 'entangle_params': entangle_params}
    _L0_attn_all = _L0_attn_setup()
    _L0_attn_in = {k: v for k, v in _L0_attn_all.items() if k in ('rotation_params', 'entangle_params')}
    del _L0_attn_all

    def _L0_xattn_setup():
        import math
        import jax, jax.numpy as jnp
        import numpy as np
        H = 16
        D_MODEL = 256
        DK = D_MODEL // H
        K_FACTOR = 2

        def _time_delay_agg_inference(v, corr):
            B, _, _, L = v.shape
            top_k = min(int(K_FACTOR * math.log(L)), L)
            mean_value = jnp.mean(corr, axis=(1, 2))
            weights, delay = jax.lax.top_k(mean_value, top_k)
            tmp_corr = jax.nn.softmax(weights, axis=-1)
            idx = (delay[:, :, None] + jnp.arange(L)) % L
            gathered = jnp.take_along_axis(v[:, None], idx[:, :, None, None, :], axis=-1)
            return jnp.einsum('bk,bkhdl->bhdl', tmp_corr, gathered)
        key = jax.random.key(seed)
        ks = jax.random.split(key, 11)
        B, L, D = (4, 512, D_MODEL)
        s = 1.0 / math.sqrt(D)
        return {'queries': jax.random.normal(ks[0], (B, L, D), jnp.float32), 'keys': jax.random.normal(ks[1], (B, L, D), jnp.float32), 'values': jax.random.normal(ks[2], (B, L, D), jnp.float32), 'Wq': jax.random.normal(ks[3], (D, H * DK), jnp.float32) * s, 'bq': jnp.zeros((H * DK,), jnp.float32), 'Wk': jax.random.normal(ks[4], (D, H * DK), jnp.float32) * s, 'bk': jnp.zeros((H * DK,), jnp.float32), 'Wv': jax.random.normal(ks[5], (D, H * DK), jnp.float32) * s, 'bv': jnp.zeros((H * DK,), jnp.float32), 'Wo': jax.random.normal(ks[6], (H * DK, D), jnp.float32) * s, 'bo': jnp.zeros((D,), jnp.float32)}
    _L0_xattn_all = _L0_xattn_setup()
    _L0_xattn_in = {k: v for k, v in _L0_xattn_all.items() if k in ('Wq', 'bq', 'Wk', 'bk', 'Wv', 'bv', 'Wo', 'bo')}
    del _L0_xattn_all

    def _L0_ffn_setup():
        import jax, jax.numpy as jnp
        import numpy as np
        B, S, IN, OUT = (4, 2048, 256, 256)
        EPS = 1e-06

        def _xla_quantized_matmul(x2d, weight_q, weight_scale):
            amax = jnp.max(jnp.abs(x2d), axis=-1, keepdims=True)
            x_scale = jnp.maximum(amax, EPS) / 127.0
            x_q = jnp.clip(jnp.round(x2d / x_scale), -128, 127).astype(jnp.int8)
            acc = jax.lax.dot_general(x_q, weight_q, (((1,), (1,)), ((), ())), preferred_element_type=jnp.int32)
            return acc.astype(jnp.float32) * x_scale * weight_scale[None, :]
        key = jax.random.key(seed)
        k1, k2, k3, k4 = jax.random.split(key, 4)
        x = jax.random.normal(k1, (B, S, IN), dtype=jnp.float32)
        weight_q = jax.random.randint(k2, (OUT, IN), -128, 128, dtype=jnp.int32).astype(jnp.int8)
        weight_scale = jax.random.uniform(k3, (OUT,), dtype=jnp.float32, minval=0.001, maxval=0.01)
        bias = jax.random.normal(k4, (OUT,), dtype=jnp.float32) * 0.01
        return {'x': x, 'weight_q': weight_q, 'weight_scale': weight_scale, 'bias': bias}
    _L0_ffn_all = _L0_ffn_setup()
    _L0_ffn_in = {k: v for k, v in _L0_ffn_all.items() if k in ('weight_q', 'weight_scale', 'bias')}
    del _L0_ffn_all
    return {'x': x, 'ctx_1024': ctx_1024, 'L0_attn_rotation_params': _L0_attn_in['rotation_params'], 'L0_attn_entangle_params': _L0_attn_in['entangle_params'], 'L0_xattn_Wq': _L0_xattn_in['Wq'], 'L0_xattn_bq': _L0_xattn_in['bq'], 'L0_xattn_Wk': _L0_xattn_in['Wk'], 'L0_xattn_bk': _L0_xattn_in['bk'], 'L0_xattn_Wv': _L0_xattn_in['Wv'], 'L0_xattn_bv': _L0_xattn_in['bv'], 'L0_xattn_Wo': _L0_xattn_in['Wo'], 'L0_xattn_bo': _L0_xattn_in['bo'], 'L0_ffn_weight_q': _L0_ffn_in['weight_q'], 'L0_ffn_weight_scale': _L0_ffn_in['weight_scale'], 'L0_ffn_bias': _L0_ffn_in['bias']}

def reference(x, ctx_1024, L0_attn_rotation_params, L0_attn_entangle_params, L0_xattn_Wq, L0_xattn_bq, L0_xattn_Wk, L0_xattn_bk, L0_xattn_Wv, L0_xattn_bv, L0_xattn_Wo, L0_xattn_bo, L0_ffn_weight_q, L0_ffn_weight_scale, L0_ffn_bias):
    import jax
    import jax.numpy as jnp

    def _L0_attn_ref(inputs, rotation_params, entangle_params):
        import jax, jax.numpy as jnp
        import numpy as np
        EMBED_DIM = 256
        NUM_HEADS = 16
        HEAD_DIM = EMBED_DIM // NUM_HEADS
        B, T, _ = inputs.shape
        x = inputs.reshape(B, T, NUM_HEADS, HEAD_DIM).transpose(0, 2, 1, 3)
        q = x * rotation_params[None, :, None, :]
        k = x * entangle_params[None, :, None, :]
        v = x
        scale = 1.0 / np.sqrt(HEAD_DIM).astype(np.float32)
        attn_scores = jnp.einsum('bhid,bhjd->bhij', q, k) * scale
        attn_weights = jax.nn.softmax(attn_scores, axis=-1)
        out = jnp.einsum('bhij,bhjd->bhid', attn_weights, v)
        out = out.transpose(0, 2, 1, 3).reshape(B, T, EMBED_DIM)
        return out

    def _L0_xattn_ref(queries, keys, values, Wq, bq, Wk, bk, Wv, bv, Wo, bo):
        import math
        import jax, jax.numpy as jnp
        import numpy as np
        H = 16
        D_MODEL = 256
        DK = D_MODEL // H
        K_FACTOR = 2

        def _time_delay_agg_inference(v, corr):
            B, _, _, L = v.shape
            top_k = min(int(K_FACTOR * math.log(L)), L)
            mean_value = jnp.mean(corr, axis=(1, 2))
            weights, delay = jax.lax.top_k(mean_value, top_k)
            tmp_corr = jax.nn.softmax(weights, axis=-1)
            idx = (delay[:, :, None] + jnp.arange(L)) % L
            gathered = jnp.take_along_axis(v[:, None], idx[:, :, None, None, :], axis=-1)
            return jnp.einsum('bk,bkhdl->bhdl', tmp_corr, gathered)
        B, Lq, _ = queries.shape
        Lk = keys.shape[1]
        q = (queries @ Wq + bq).reshape(B, Lq, H, DK)
        k = (keys @ Wk + bk).reshape(B, Lk, H, DK)
        v = (values @ Wv + bv).reshape(B, Lk, H, DK)
        if Lq > Lk:
            pad = ((0, 0), (0, Lq - Lk), (0, 0), (0, 0))
            k = jnp.pad(k, pad)
            v = jnp.pad(v, pad)
        else:
            k = k[:, :Lq]
            v = v[:, :Lq]
        qt = jnp.transpose(q, (0, 2, 3, 1))
        kt = jnp.transpose(k, (0, 2, 3, 1))
        vt = jnp.transpose(v, (0, 2, 3, 1))
        qf = jnp.fft.rfft(qt)
        kf = jnp.fft.rfft(kt)
        c = qf.real * kf.real + 1j * -(qf.imag * kf.imag)
        corr = jnp.fft.irfft(c, n=Lq).astype(qt.dtype)
        agg = _time_delay_agg_inference(vt, corr)
        out = jnp.transpose(agg, (0, 3, 1, 2)).reshape(B, Lq, H * DK)
        return out @ Wo + bo

    def _L0_ffn_ref(x, weight_q, weight_scale, bias):
        import jax, jax.numpy as jnp
        import numpy as np
        B, S, IN, OUT = (4, 2048, 256, 256)
        EPS = 1e-06

        def _xla_quantized_matmul(x2d, weight_q, weight_scale):
            amax = jnp.max(jnp.abs(x2d), axis=-1, keepdims=True)
            x_scale = jnp.maximum(amax, EPS) / 127.0
            x_q = jnp.clip(jnp.round(x2d / x_scale), -128, 127).astype(jnp.int8)
            acc = jax.lax.dot_general(x_q, weight_q, (((1,), (1,)), ((), ())), preferred_element_type=jnp.int32)
            return acc.astype(jnp.float32) * x_scale * weight_scale[None, :]
        orig_shape = x.shape
        x2d = x.reshape(-1, orig_shape[-1])
        out = _xla_quantized_matmul(x2d, weight_q, weight_scale)
        out = out.reshape(*orig_shape[:-1], out.shape[-1])
        out = out + bias
        return out
    x = _layernorm(x + _L0_attn_ref(x, L0_attn_rotation_params, L0_attn_entangle_params), axis=-1)
    x = _layernorm(x + _L0_xattn_ref(x, ctx_1024, ctx_1024, L0_xattn_Wq, L0_xattn_bq, L0_xattn_Wk, L0_xattn_bk, L0_xattn_Wv, L0_xattn_bv, L0_xattn_Wo, L0_xattn_bo), axis=-1)
    x = _layernorm(x + _L0_ffn_ref(x, L0_ffn_weight_q, L0_ffn_weight_scale, L0_ffn_bias), axis=-1)
    return x

_drawn_inputs = setup_inputs


def setup_inputs(seed=0):
    import zlib

    import numpy as np

    out = dict(_drawn_inputs(seed))
    spreads = {'L0_xattn_bq': (0.0, 2.0),
     'L0_xattn_bk': (0.0, 0.1),
     'L0_xattn_bv': (0.0, 0.1),
     'L0_xattn_bo': (0.0, 0.1)}
    factors = {'L0_ffn_bias': 44.124}
    for name, (base, spread) in spreads.items():
        noise = np.random.default_rng([zlib.crc32(name.encode()), seed]).standard_normal(out[name].shape)
        drawn = base * np.exp(spread * noise) if base else spread * noise
        out[name] = jnp.asarray(drawn.astype(out[name].dtype))
    for name, factor in factors.items():
        out[name] = (out[name] * factor).astype(out[name].dtype)
    return out
```

```python
from contextlib import ExitStack
import math

import numpy as np

import concourse.bass as bass
from concourse import mybir

P = 128
F32 = mybir.dt.float32
BF16 = mybir.dt.bfloat16
I32 = mybir.dt.int32
ALU = mybir.AluOpType
ACT = mybir.ActivationFunctionType
AX = mybir.AxisListType

L, D, H, DH = 2048, 256, 16, 16
NT = L // P
LC = 1601
NCT = (LC + P - 1) // P
CT = D // P
ROWS = 6 * DH
KROWS = ROWS + 3
RING = 4
LOOPS = 3
UNITS = 16
AHEAD = 19
CHUNK = 512
NF = 9
EPS = 1e-5
TOPK = int(2 * math.log(L))
NEG = -3.0e38
ROUND = 1.5 * 2.0 ** 23
C1, S1, R2 = math.cos(math.pi / 8), math.sin(math.pi / 8), math.sqrt(0.5)
K_PARTS = [(0, 3, 0), (48, 2, 0), (80, 1, 0)]
Q_PARTS = [(0, 1, 0), (16, 1, 0), (32, 1, 0), (48, 1, 1), (64, 1, 1), (80, 1, 2)]
LOADS = len(K_PARTS) + len(Q_PARTS)


def tables():
    f1 = np.arange(NF)
    a, b = np.arange(P), np.arange(P)
    ang = 2 * np.pi * ((a[:, None, None] * (f1[None, :, None] + 16 * b[None, None, :])) % L) / L
    c, s = np.cos(ang), np.sin(ang)
    t1 = np.stack([c, s, -s], axis=2)
    t2 = np.stack([c.transpose(2, 1, 0), s.transpose(2, 1, 0)], axis=2)
    wt = np.where((f1 == 0) | (f1 == 8), 1.0, 2.0)
    ang16 = 2 * np.pi * ((f1[:, None] * np.arange(16)[None, :]) % 16) / 16
    w16 = np.stack([np.cos(ang16), -np.sin(ang16)], 1) * wt[:, None, None] / (L * D)
    e16 = np.stack([np.cos(ang16), np.sin(ang16)], 1) * wt[:, None, None] / L
    sgn = np.where(a < 64, 1.0, -1.0)
    sel = np.zeros((P, 68))
    for g in range(4):
        sel[32 * g + np.arange(17), 17 * g + np.arange(17)] = 1
    f = np.float32
    return {
        "tab_fwd": t1.astype(f), "tab_inv": t2.astype(f),
        "tab_w16": np.ascontiguousarray(w16.reshape(18, 16)).astype(f),
        "tab_e16": np.ascontiguousarray(e16.transpose(2, 0, 1).reshape(1, 16 * 18)).astype(f),
        "tab_sign": np.stack([sgn, -sgn], 1).astype(f),
        "tab_sel": sel.astype(f),
        "tab_ident": np.eye(P).astype(f),
    }


def decoder_layer(nc, A, out):
    ctx = ExitStack()
    base = (nc.sbuf_base + 31) // 32 * 32
    KB = 1024
    names = [0]

    def sb(off, shape, dt=F32):
        names[0] += 1
        return nc.alloc_sbuf_tensor_at(f"t{names[0]}", shape, dt, offset=base + off)

    O_X, O_Y, O_KV, O_KQ = 0, 16 * KB, 32 * KB, 64 * KB
    O_SP, O_P, O_OSB, O_V = 88 * KB, 120 * KB, 136 * KB, 140 * KB
    O_T1, O_T2, O_FR, O_S = 146 * KB, 160 * KB, 170 * KB, 186 * KB

    class Region:
        def __init__(self, at, end):
            self.at, self.end = at, end

        def __call__(self, shape, dt=F32):
            size = int(np.prod(shape[1:])) * {F32: 4, BF16: 2, I32: 4}[dt]
            t = sb(self.at, shape, dt)
            self.at += (size + 31) // 32 * 32
            assert base + self.at <= base + self.end, (self.at, self.end)
            return t

    xT = sb(O_Y, [P, CT, L])
    parts = [sb(O_SP + 8 * KB * n, [P, CT, L], BF16) for n in range(6)]
    full = [sb(O_FR + 8 * KB * n, [P, L]) for n in range(2)]
    ctxT = sb(O_T1, [P, CT, LC])
    wkT, wqT, wvT, wo = (sb(O_T2 + 2 * KB * n, [P, CT, D]) for n in range(4))
    bias_row = sb(O_T2 + 8 * KB, [1, 2 * D])
    ab = sb(O_OSB, [P, CT, 2 * D])
    x_sb = sb(O_X, [P, NT, D])
    y_sb = x_sb
    o_ring = [O_KQ, O_KQ + 8 * KB, O_KQ + 16 * KB, O_Y]
    k_ring = [sb(o, [P, L], BF16) for o in o_ring]
    q_ring = [sb(o + 4 * KB, [P, L], BF16) for o in o_ring]
    probs = [sb(O_P + 2 * KB * n, [P, CHUNK]) for n in range(8)]
    o_sb = [sb(O_OSB + 2 * KB * n, [P, CHUNK]) for n in range(2)]
    v_ring = [sb(O_Y + 8 * KB + 2 * KB * b, [P, NT, 32]) for b in range(RING)]
    kv = sb(O_KV, [P, NT, 2 * D])
    kvy = sb(O_SP, [P, 16, 2 * D])
    tab_fwd = sb(O_T1, [P, NF, 3, P])
    tab_inv = sb(O_T2, [P, NF, 2, P])
    mid = Region(O_FR, O_FR + 16 * KB)
    attn = [sb(O_V + KB * b, [P, NT, DH]) for b in range(RING)]
    bo_b, ws_b, fb_b = mid([P, D]), mid([P, D]), mid([P, D])
    wffn_words, wffn = mid([P, CT, 2 * D], I32), mid([P, CT, D], BF16)
    w16, e16, e16s = mid([18, 16]), mid([1, 16 * 18]), mid([1, 16 * 18])
    sign, rj, ri, hh, hf = mid([P, 2]), mid([P, NF, 4]), mid([P, NF, 2]), mid([P, NF, 4]), mid([P, NF, 3])
    u_sb, uT = mid([P, 18]), mid([18, P])
    mv, rstd, expo = mid([P, NT, 2]), mid([P, NT]), mid([P, NT])
    stats = mid([P, NT, 6])
    amax, xscale, xinv = mid([P, NT]), mid([P, NT]), mid([P, NT])
    top, wsum, wrec, nmax = mid([1, 16]), mid([1, 1]), mid([1, 1]), mid([1, 1])
    small = Region(O_S, O_S + 5 * KB + 700)
    ident, identb, sel = small([P, P]), small([P, P], BF16), small([P, 68])
    rotc, entc, bqc, bkc, bvc = (small([P, CT]) for _ in range(5))
    ones_row = small([1, P])
    mx, negm, mrest = small([P, NT, 2]), small([P, NT]), small([P, NT])
    msplit, mT, recip = small([P, 8, NT], BF16), small([3 * NT, P], BF16), small([P, 2, 4, 4])
    csum, gvec, bb, extra = small([P, CT]), small([P, CT]), small([1, 1]), small([1, 1])
    assert base + O_S + 5 * KB + 700 <= 212863
    x1 = sb(O_X, [P, NT, D])
    spec = sb(O_KV, [P, NF, 5, D])
    gtab = sb(O_KV + 46 * KB, [P, NF, 2, P])
    y1 = sb(O_P, [P, 16, D])
    scr1 = sb(O_Y, [P, 16, D])
    c_row = sb(O_OSB, [1, L])
    junk = sb(O_OSB + 8 * KB, [P, 2, D])
    c2_row, e_row, w_row = (sb(O_SP + 8 * KB * n, [1, L]) for n in range(3))
    gtmp = sb(O_OSB, [P, 2, 2, P])
    c_big = sb(O_OSB, [P, 8, D])
    z = sb(O_SP, [P, NF, 2, D])
    zs = sb(O_SP + 18 * KB, [P, 30, D])
    x2 = sb(O_Y, [P, NT, D])
    x2b = sb(O_KV, [P, NT, D])
    xq = sb(O_KV + 16 * KB, [P, 4, D])
    xqc = sb(O_KV + 20 * KB, [P, 4, D])
    xqb = sb(O_KV + 24 * KB, [P, NT, D], BF16)
    xqT = sb(O_KV + 32 * KB, [P, NT, D], BF16)
    y3 = sb(O_SP, [P, NT, D])
    x3 = sb(O_X, [P, NT, D])

    ps = ctx.enter_context(nc.psum_tensor("ps", [P, 8, CHUNK], F32))
    mx_ps = [ps[:, 0:2, :], ps[:, 2:4, :]]
    ex_ps = [ps[:, 4, :], ps[:, 5, :]]
    o_ps = [ps[:, 6 + n, :] for n in range(2)]
    out_t = [ps[:, 6 + n, 0:NT * 17].rearrange("p (s c d) -> p s c d", s=4, d=17) for n in range(2)]
    mt_ps = [ps[:, 6 + n, 384:448].bitcast(BF16) for n in range(2)]

    ks = nc.dram_tensor("k_parts", [3, D, L], BF16, kind="Internal").ap()
    qs = nc.dram_tensor("q_parts", [3, D, L], BF16, kind="Internal").ap()

    sems = {}

    def S(name):
        if name not in sems:
            sems[name] = ctx.enter_context(nc.semaphore(name))
        return sems[name]

    COMBOS = [(0, 0), (1, 0), (0, 1), (1, 1)]
    N_CONSTS = 6
    N_WEIGHTS = 4
    kq_loaded = [S(f"kq_loaded{b}") for b in range(RING)]
    m_rows = [S(f"m_rows{b}") for b in range(RING)]
    parts_out = [S(f"parts_out{n}") for n in range(4)]

    SLOT_R = {0: 0, 8: 1, 4: 2, 2: 4, 6: 5, 1: 8, 7: 9, 3: 10, 5: 11}
    SLOT_I = {4: 3, 2: 6, 6: 7, 1: 12, 7: 13, 3: 14, 5: 15}
    F_ORDER = [0, 8, 4, 2, 6, 1, 7, 3, 5]

    block = ctx.enter_context(nc.Block())

    def load(sp, b, h):
        for r, n, m in K_PARTS:
            sp.dma_start(k_ring[b][r:r + DH * n, :], ks[m:m + n, bass.ds(h * DH, DH), :]).then_inc(kq_loaded[b], 16)
        for r, n, m in Q_PARTS:
            sp.dma_start(q_ring[b][r:r + DH * n, :], qs[m:m + n, bass.ds(h * DH, DH), :]).then_inc(kq_loaded[b], 16)

    def rows(sp, b, h):
        sp.wait_ge(S("mT_copied"), h + 1)
        sp.dma_start(q_ring[b][ROWS:KROWS, :].rearrange("p (t i) -> p t i", i=P), mT[:, :]).then_inc(m_rows[b], 16)

    @block.sync
    def _(sp):
        for c in range(CT):
            sp.dma_start(xT[:, c, :], A["xT"][c * P:(c + 1) * P, :]).then_inc(S(f"xT_in{c}"), 16)
        x_v = A["x"].rearrange("(n p) c -> p n c", p=P)
        for n, (kq, c) in enumerate(COMBOS):
            dst = ks if kq else qs
            for m in range(3):
                if m < 2:
                    sp.wait_ge(S(f"part{m + 1}_ready"), n + 1)
                else:
                    sp.wait_ge(S("part3_dve" if kq else "part3_pool"), c + 1)
                sp.dma_start(dst[m, c * P:(c + 1) * P, :], parts[3 * kq + m][:, c, :]).then_inc(parts_out[n], 16)
            if n == 1:
                for i in range(2):
                    sp.wait_ge(parts_out[i], 48)
                for h in range(RING - 1):
                    load(sp, h, h)
                for i in range(4):
                    sp.dma_start(x_sb[:, 4 * i:4 * i + 4, :], x_v[:, 4 * i:4 * i + 4, :]).then_inc(S("x_in"), 16)
        for i in range(2, 4):
            sp.wait_ge(parts_out[i], 48)
        load(sp, RING - 1, RING - 1)
        late = [(bo_b, "bo_b"), (ws_b, "ws_b"), (fb_b, "fb_b"), (sign, "tab_sign"), (w16, "tab_w16"), (e16, "tab_e16")]
        for t, name in late:
            sp.dma_start(t[:, :], A[name]).then_inc(S("late_in"), 16)
        sp.dma_start(wffn_words[:, :, :], A["wffnT"].bitcast(I32).rearrange("(c p) n -> p c n", p=P))\
          .then_inc(S("late_in"), 16)
        rows(sp, 0, 0)
        sp.wait_ge(S("kv_ps"), NCT)
        sp.wait_ge(S("csum_ready"), 1)
        sp.dma_start(tab_fwd[:, :, :, :], A["tab_fwd"]).then_inc(S("tabs_in"), 16)
        sp.dma_start(tab_inv[:, :, :, :], A["tab_inv"]).then_inc(S("tabs_in"), 16)

        def step(it, hb, more_rows, more_loads):
            h = it * RING + hb
            if more_rows:
                rows(sp, (hb + 1) % RING, h + 1)
            if more_loads:
                sp.wait_ge(S("quads_done"), (h + 1) * UNITS + 2)
                load(sp, hb % RING, h + RING)

        with sp.Fori(0, LOOPS) as it:
            for hb in range(RING):
                step(it, hb, True, True)
        for hb in range(H - LOOPS * RING):
            h = LOOPS * RING + hb
            step(LOOPS, hb, h + 1 < H, h + RING < H)
        o_v = out.rearrange("(n p) c -> p n c", p=P)
        for n in range(4):
            sp.wait_ge(S("x3_ready"), 4 * n + 4)
            sp.dma_start(o_v[:, 4 * n:4 * n + 4, :], x3[:, 4 * n:4 * n + 4, :]).then_inc(S("stored"), 16)
        sp.wait_ge(S("stored"), 64)

    @block.tensor
    def _(pe):
        pe.sem_inc(S("quads_done"), 2)
        pe.wait_ge(S("weights_in"), 16 * N_WEIGHTS)
        pe.wait_ge(S("consts_in"), 16 * N_CONSTS)
        for e in range(CT):
            for half, (wl, wr) in enumerate(((wkT, wqT), (wvT, wo))):
                for c in range(CT):
                    pe.matmul(ps[:, e, half * D:(half + 1) * D], wl[:, c, e * P:(e + 1) * P], wr[:, c, :],
                              start=(c == 0), stop=(c == CT - 1))
        for half, (bl, wr) in enumerate(((bkc, wqT), (bvc, wo))):
            for c in range(CT):
                pe.matmul(ps[0:1, 2, half * D:(half + 1) * D], bl[:, c:c + 1], wr[:, c, :],
                          start=(c == 0), stop=(c == CT - 1))
        for e in range(CT):
            for c in range(CT):
                pe.matmul(ps[:, 3, e:e + 1], wkT[:, c, e * P:(e + 1) * P], bqc[:, c:c + 1],
                          start=(c == 0), stop=(c == CT - 1))
        for c in range(CT):
            last = pe.matmul(ps[0:1, 3, 4:5], bkc[:, c:c + 1], bqc[:, c:c + 1], start=(c == 0), stop=(c == CT - 1))
        last.then_inc(S("fold_ps"), 1)
        pe.wait_ge(S("fold_sb"), 5)
        pe.wait_ge(S("ones_set"), 1)
        pe.wait_ge(S("ctx_in"), 16)

        def context(t):
            n = min(P, LC - t * P)
            if t >= 3:
                pe.wait_ge(S("kv_sb"), t - 2)
            o = ps[0:n, 4 + t % 3, :]
            for c in range(CT):
                pe.matmul(o, ctxT[:, c, t * P:t * P + n], ab[:, c, :], start=(c == 0), stop=False)
            pe.matmul(o, ones_row[0:1, 0:n], bias_row[0:1, :], start=False, stop=True).then_inc(S("kv_ps"), 1)

        def maxima(b, half, tile, use):
            pe.wait_ge(S("mx_free"), use + 1)
            for n in range(2):
                k0 = half * 1024 + n * CHUNK
                last = pe.matmul(mx_ps[half][:, n, :], q_ring[b][0:ROWS, tile * P:(tile + 1) * P],
                                 k_ring[b][0:ROWS, k0:k0 + CHUNK], start=True, stop=True)
            last.then_inc(S("mx_ready"), 1)

        def turn_maxima(h, bank):
            pe.wait_ge(S("split_ready"), h + 1)
            pe.transpose(mt_ps[bank], msplit[:, :, :].rearrange("p m t -> p (m t)"), identb[:, :])\
              .then_inc(S("mT_ready"), 1)

        def exponents(b, c, j, e):
            pe.wait_ge(S("probs_ready"), e + 1)
            pe.matmul(ex_ps[c % 2], k_ring[b][0:KROWS, j * P:(j + 1) * P],
                      q_ring[b][0:KROWS, c * CHUNK:(c + 1) * CHUNK], start=True, stop=True).then_inc(S("scores_ready"), 1)

        def values(it, n):
            hb, j = n // UNITS, n % UNITS
            if j == 0:
                pe.wait_ge(S("mT_copied"), it * RING + hb + 1)
            pe.wait_ge(S("probs_ready"), (it * (RING * UNITS) + n) * 4 + 6)
            for c in range(4):
                last = pe.matmul(o_ps[hb % 2][32 * c:32 * c + 32, :], v_ring[hb % RING][:, j, :],
                                 probs[4 * (n % 2) + c][:, :], start=(j == 0), stop=(j == UNITS - 1))
            last.then_inc(S("quads_done"), 1)

        def turn_out(h, bank):
            pe.wait_ge(S("o_copied"), h + 1)
            for s in range(4):
                last = pe.matmul(out_t[bank][:, s, :, :], o_sb[bank][:, s * P:(s + 1) * P], sel[:, :],
                                 start=True, stop=True)
            last.then_inc(S("outt_ready"), 1)

        BEFORE = 6
        for t in range(BEFORE):
            context(t)
        for g in range(AHEAD):
            if g % UNITS == 0:
                pe.wait_ge(kq_loaded[g // UNITS], 16 * LOADS)
            for half in range(2):
                maxima(g // UNITS, half, g % UNITS, 2 * g + half)
            if g < NCT - BEFORE:
                context(BEFORE + g)
            if g == UNITS:
                pe.wait_ge(S("kv_sb"), NCT)
                turn_maxima(0, 0)
        pe.wait_ge(S("csum_ready"), 1)
        pe.wait_ge(S("mT_copied"), 1)
        for c in range(CT):
            last = pe.matmul(ps[0:1, 7, 0:1], csum[:, c:c + 1], gvec[:, c:c + 1], start=(c == 0), stop=(c == CT - 1))
        last.then_inc(S("fold_ps"), 1)
        pe.wait_ge(S("fold_sb"), 6)
        pe.wait_ge(S("v_set"), RING)
        pe.wait_ge(S("k_ones"), 1)

        def heads(it, count, end):
            for n in range(count * UNITS):
                hb, j = n // UNITS, n % UNITS
                b, h = hb % RING, it * RING + hb
                g = n + AHEAD
                mb, tile, use = g // UNITS % RING, g % UNITS, (it * (RING * UNITS) + g) * 2
                e = it * (RING * UNITS * 4) + 4 * n
                if j == 0:
                    pe.wait_ge(m_rows[b], (it + hb // RING) * 16 + 16)
                    pe.wait_ge(S("v_ready"), h + 1)
                exponents(b, 0, j, e)
                exponents(b, 1, j, e + 1)
                if n:
                    values(it, n - 1)
                exponents(b, 2, j, e + 2)
                exponents(b, 3, j, e + 3)
                if j == 1 and hb:
                    turn_out(h - 1, (hb - 1) % 2)
                if j == 13 and (hb + 1) * UNITS < end:
                    pe.wait_ge(S("attn_ready"), h)
                    turn_maxima(h + 1, (hb + 1) % 2)
                if g < end:
                    if tile == 0:
                        pe.wait_ge(kq_loaded[mb], (it + g // UNITS // RING) * (16 * LOADS) + 16 * LOADS)
                    maxima(mb, 0, tile, use)
                    maxima(mb, 1, tile, use + 1)
            values(it, count * UNITS - 1)
            turn_out(it * RING + count - 1, (count - 1) % 2)

        with pe.Fori(0, LOOPS) as it:
            heads(it, RING, 1 << 30)
        heads(LOOPS, H - LOOPS * RING, (H - LOOPS * RING) * UNITS)

        def forward(src, f, re, im):
            yr = src[:, SLOT_R[f], :]
            odd = f not in (0, 8)
            pe.matmul(re, tab_fwd[:, f, 0, :], yr, start=True, stop=not odd)
            if odd:
                pe.matmul(re, tab_fwd[:, f, 2, :], src[:, SLOT_I[f], :], start=False, stop=True)
            last = pe.matmul(im, tab_fwd[:, f, 1, :], yr, start=True, stop=not odd)
            if odd:
                last = pe.matmul(im, tab_fwd[:, f, 0, :], src[:, SLOT_I[f], :], start=False, stop=True)
            return last

        pe.wait_ge(S("tabs_in"), 32)
        pe.wait_ge(S("kvy_ready"), 1)
        pe.wait_ge(S("mx_free"), 2 * H * UNITS + 2)
        for n, f in enumerate(F_ORDER):
            if n >= 2:
                pe.wait_ge(S("kvf_sb"), 3 * (n - 1))
            b = 2 * (n % 2)
            forward(kvy, f, ps[:, b, :], ps[:, b + 1, :]).then_inc(S("kvf_ps"), 1)
        pe.wait_ge(S("probs_ready"), H * 64 + 2)
        pe.wait_ge(S("attn_ready"), H)
        for n, f in enumerate(F_ORDER):
            pe.wait_ge(S("y1_ready" if f % 2 else "y1_even"), 1)
            if f in (2, 6):
                pe.wait_ge(S("y1_two"), 1)
            if n >= 4:
                pe.wait_ge(S("prod_done"), 2 * (n - 3))
            b = 4 + n % 4
            forward(y1, f, ps[:, b, 0:D], ps[:, b, D:2 * D]).then_inc(S("x1f_ps"), 1)

        pe.wait_ge(S("rj_ready"), 4)
        pe.wait_ge(S("kvf_sb"), 3 * NF)
        for f in range(NF):
            o = ps[:, 0, 2 * f:2 * f + 2]
            pe.matmul(o, tab_inv[:, f, 0, :], rj[:, f, 0:2], start=True, stop=False)
            last = pe.matmul(o, tab_inv[:, f, 1, :], rj[:, f, 2:4], start=False, stop=True)
        last.then_inc(S("u_ps"), 1)
        pe.wait_ge(S("u_sb"), 1)
        pe.transpose(ps[0:18, 1, 0:P], u_sb[:, :], ident[:, :]).then_inc(S("u_ps"), 1)
        pe.wait_ge(S("u_sb"), 2)
        for t in range(16):
            last = pe.matmul(ps[0:1, 2 + t // 4, t % 4 * P:t % 4 * P + P], w16[:, t:t + 1], uT[:, :],
                             start=True, stop=True)
        last.then_inc(S("corr_ps"), 1)
        pe.wait_ge(S("w_ready"), 1)
        pe.wait_ge(S("e16_ready"), 1)
        for t in range(16):
            last = pe.matmul(ps[:, 0, 0:18], w_row[0:1, t * P:(t + 1) * P], e16s[0:1, 18 * t:18 * t + 18],
                             start=(t == 0), stop=(t == 15))
        last.then_inc(S("h_ps"), 1)
        pe.wait_ge(S("h_sb"), 3)
        for f in range(NF):
            o = ps[:, 1, 2 * f:2 * f + 2]
            pe.matmul(o, tab_fwd[:, f, 0, :], hh[:, f, 0:2], start=True, stop=False)
            last = pe.matmul(o, tab_fwd[:, f, 1, :], hh[:, f, 2:4], start=False, stop=True)
        last.then_inc(S("h_ps"), 1)
        pe.wait_ge(S("corr_sb"), 1)
        for n, f in enumerate(F_ORDER):
            pe.wait_ge(S("g_ready"), 2 * (n + 1))
            if n >= 6:
                pe.wait_ge(S("z_sb"), n - 5)
            w = D if f in (0, 8) else 2 * D
            o = ps[:, 2 + n % 6, 0:w]
            if f in (0, 8):
                pe.matmul(o, gtab[:, f, 0, :], spec[:, f, 2, :], start=True, stop=False)
                last = pe.matmul(o, gtab[:, f, 1, :], spec[:, f, 3, :], start=False, stop=True)
            else:
                pe.matmul(o, gtab[:, f, 0, :], spec[:, f, 2:4, :].rearrange("p a c -> p (a c)"), start=True, stop=False)
                last = pe.matmul(o, gtab[:, f, 1, :], spec[:, f, 3:5, :].rearrange("p a c -> p (a c)"),
                                 start=False, stop=True)
            last.then_inc(S("z_ps"), 1)
        pe.wait_ge(S("wffn_ready"), 1)
        pe.wait_ge(S("z_sb"), NF)

        def product(t):
            pe.wait_ge(S("xqT_sb"), t + 1)
            if t >= 4:
                pe.wait_ge(S("y3_made"), t - 3)
            for c in range(CT):
                last = pe.matmul(ps[:, 4 + t % 4, 0:D], xqT[:, t, c * P:(c + 1) * P], wffn[:, c, :],
                                 start=(c == 0), stop=(c == CT - 1))
            last.then_inc(S("ffn_ps"), 1)

        for t in range(NT):
            pe.wait_ge(S("xqb_ready"), t + 1)
            if t >= 4:
                pe.wait_ge(S("xqT_sb"), t - 3)
            for c in range(CT):
                last = pe.transpose(ps[:, t % 4, 64 * c:64 * (c + 1)].bitcast(BF16), xqb[:, t, c * P:(c + 1) * P],
                                    identb[:, :])
            last.then_inc(S("xqT_ps"), 1)
            if t:
                product(t - 1)
        product(NT - 1)

    @block.scalar
    def _(act):
        act.sem_inc(S("probs_ready"), 2)
        for t, name in ((rotc, "rotc"), (entc, "entc")):
            act.dma_start(t[:, :], A[name]).then_inc(S("rot_in"), 16)
        for t, name in ((wkT, "wkT"), (wqT, "wqT"), (wvT, "wvT"), (wo, "wo")):
            act.dma_start(t[:, :, :], A[name].rearrange("(c p) n -> p c n", p=P)).then_inc(S("weights_in"), 16)
        consts = [(ident, "tab_ident"), (sel, "tab_sel"),
                  (bqc, "bq"), (bkc, "bk"), (bvc, "bv")]
        for t, name in consts:
            act.dma_start(t[:, :], A[name]).then_inc(S("consts_in"), 16)
        act.dma_start(ctxT[:, :, :], A["ctxT"].rearrange("(c p) t -> p c t", p=P)).then_inc(S("ctx_in"), 16)
        act.wait_ge(S("consts_in"), 16 * (N_CONSTS - 1))
        act.activation(identb[:, :], ident[:, :], ACT.Copy).then_inc(S("consts_in"), 16)
        for first in (0, 2):
            for m, made in ((0, "full_ready"), (1, "rest_ready")):
                for n in (first, first + 1):
                    kq, c = COMBOS[n]
                    act.wait_ge(S(made), n + 1)
                    act.activation(parts[3 * kq + m][:, c, :], full[n % 2][:, :], ACT.Copy)\
                       .then_inc(S(f"part{m + 1}_ready"), 1)
            if first == 0:
                act.wait_ge(S("fold_ps"), 1)
                for e in range(CT):
                    act.activation(ab[:, e, :], ps[:, e, :], ACT.Copy).then_inc(S("fold_sb"), 1)
                act.activation(bias_row[0:1, :], ps[0:1, 2, :], ACT.Copy).then_inc(S("fold_sb"), 1)
                act.activation(gvec[:, :], ps[:, 3, 0:2], ACT.Copy).then_inc(S("fold_sb"), 1)
                act.activation(bb[0:1, :], ps[0:1, 3, 4:5], ACT.Copy).then_inc(S("fold_sb"), 1)
        for t in range(NCT):
            n = min(P, LC - t * P)
            act.wait_ge(S("kv_ps"), t + 1)
            if t == NCT - 1:
                act.wait_ge(S("kv_zero"), 1)
            act.activation(kv[0:n, t, :], ps[0:n, 4 + t % 3, :], ACT.Copy).then_inc(S("kv_sb"), 1)

        def copy_turned(h, bank, sent):
            act.wait_ge(S("mT_ready"), h + 1)
            if sent:
                act.wait_ge(*sent)
            act.activation(mT[:, :], mt_ps[bank][0:3 * NT, :], ACT.Copy).then_inc(S("mT_copied"), 1)

        copy_turned(0, 0, None)
        act.wait_ge(S("fold_ps"), 2)
        act.activation(extra[0:1, :], ps[0:1, 7, 0:1], ACT.Copy).then_inc(S("fold_sb"), 1)

        def exps(it, n, r):
            e = it * (RING * UNITS * 4) + 4 * n + r
            act.wait_ge(S("scores_ready"), e + 1)
            if r == 0:
                act.wait_ge(S("quads_done"), it * (RING * UNITS) + n + 1)
            act.activation(probs[4 * (n % 2) + r][:, :], ex_ps[r % 2], ACT.Exp).then_inc(S("probs_ready"), 1)

        def copy_out(h, bank):
            act.wait_ge(S("quads_done"), (h + 1) * UNITS + 2)
            act.activation(o_sb[bank][:, :], o_ps[bank], ACT.Copy).then_inc(S("o_copied"), 1)

        def heads(it, count, end):
            for n in range(count * UNITS):
                hb, j = n // UNITS, n % UNITS
                h = it * RING + hb
                exps(it, n, 0)
                exps(it, n, 1)
                if j == 14 and (hb + 1) * UNITS < end:
                    copy_turned(h + 1, (hb + 1) % 2, (m_rows[hb % RING], (it + hb // RING) * 16 + 16))
                exps(it, n, 2)
                exps(it, n, 3)
                if j == 0 and hb:
                    copy_out(h - 1, (hb - 1) % 2)
            copy_out(it * RING + count - 1, (count - 1) % 2)

        with act.Fori(0, LOOPS) as it:
            heads(it, RING, 1 << 30)
        heads(LOOPS, H - LOOPS * RING, (H - LOOPS * RING) * UNITS)

        for n, f in enumerate(F_ORDER):
            act.wait_ge(S("kvf_ps"), n + 1)
            b = 2 * (n % 2)
            for m in range(2):
                act.activation(spec[:, f, m:m + 3:2, :], ps[:, b + m, :].rearrange("p (a c) -> p a c", a=2), ACT.Copy)\
                   .then_inc(S("kvf_sb"), 1)
            act.activation(spec[:, f, 4, :], ps[:, b, D:2 * D], ACT.Copy, scale=-1.0).then_inc(S("kvf_sb"), 1)
        act.wait_ge(S("u_ps"), 1)
        act.activation(u_sb[:, :], ps[:, 0, 0:18], ACT.Copy).then_inc(S("u_sb"), 1)
        act.wait_ge(S("u_ps"), 2)
        act.activation(uT[:, :], ps[0:18, 1, 0:P], ACT.Copy).then_inc(S("u_sb"), 1)
        act.wait_ge(S("corr_ps"), 1)
        act.activation(c_row[0:1, :], ps[0:1, 2:6, :], ACT.Copy).then_inc(S("corr_sb"), 1)
        act.wait_ge(S("nmax_ready"), 1)
        act.activation(e_row[0:1, :], c_row[0:1, :], ACT.Exp, bias=nmax[0:1, :]).then_inc(S("e_ready"), 1)
        act.wait_ge(S("hf_sb"), 2)
        for n, f in enumerate(F_ORDER):
            if n >= 2:
                act.wait_ge(S("g_ready"), 2 * (n - 1))
            act.activation(gtmp[:, n % 2, :, :], tab_inv[:, f, :, :], ACT.Copy, scale=hf[:, f, 0:1])\
               .then_inc(S("g_tmp"), 1)
        for n, f in enumerate(F_ORDER):
            act.wait_ge(S("z_ps"), n + 1)
            w = 1 if f in (0, 8) else 2
            act.activation(z[:, f, 0:w, :], ps[:, 2 + n % 6, 0:w * D].rearrange("p (a c) -> p a c", a=w), ACT.Copy)\
               .then_inc(S("z_sb"), 1)
        def copy_xqT(t):
            act.wait_ge(S("xqT_ps"), t + 1)
            act.activation(xqT[:, t, :], ps[:, t % 4, 0:P].bitcast(BF16), ACT.Copy).then_inc(S("xqT_sb"), 1)

        for t in range(NT):
            act.wait_ge(S("xinv_ready"), t // 4 + 1)
            if t >= 4:
                act.wait_ge(S("xqc_ready"), t - 3)
            act.activation(xq[:, t % 4, :], x2[:, t, :], ACT.Copy, bias=ROUND, scale=xinv[:, t:t + 1])\
               .then_inc(S("xq_ready"), 1)
            if t >= 2:
                copy_xqT(t - 2)
        copy_xqT(NT - 2)
        copy_xqT(NT - 1)

    @block.gpsimd
    def _(pool):
        chain = [0]

        def link(ins):
            chain[0] += 1
            ins.then_inc(S("pool_chain"), 1)
            pool.wait_ge(S("pool_chain"), chain[0])

        def tt(o, a, b, op):
            return pool.tensor_tensor(o, a, b, op)

        def scaled(o, a, by):
            return pool.tensor_scalar(o, a, by, None, ALU.mult)

        pool.sem_inc(S("attn_used"), RING)
        pool.memset(ones_row[:, :], 1.0).then_inc(S("ones_set"), 1)
        pool.memset(kv[:, NCT - 1:NT, :], 0.0).then_inc(S("kv_zero"), 1)
        for n in (0, 2):
            c = COMBOS[n][1]
            pool.wait_ge(S("part2_ready"), n + 1)
            tt(parts[2][:, c, :], full[n % 2][:, :], parts[1][:, c, :], ALU.subtract).then_inc(S("part3_pool"), 1)
        pool.wait_ge(S("full_ready"), 4)
        for b in range(RING):
            pool.memset(v_ring[b][:, :, 16:17], 1.0)
            pool.memset(v_ring[b][:, :, 17:32], 0.0).then_inc(S("v_set"), 1)
        pool.wait_ge(S("x_in"), 64)

        def take_values(h):
            if h >= RING:
                pool.wait_ge(S("quads_done"), (h - RING + 1) * UNITS + 2)
            pool.tensor_copy(v_ring[h % RING][:, :, 0:DH], x_sb[:, :, h * DH:(h + 1) * DH]).then_inc(S("v_ready"), 1)

        def residual(h):
            pool.wait_ge(S("attn_ready"), h + 1)
            tt(y_sb[:, :, h * DH:(h + 1) * DH], attn[h % RING][:, :, :], x_sb[:, :, h * DH:(h + 1) * DH], ALU.add)\
                .then_inc(S("attn_used"), 1)

        def even_side(x, y, s):
            link(tt(s[:, 0:4, :], y[:, 0:4, :], y[:, 4:8, :], ALU.add))
            link(tt(s[:, 4:8, :], y[:, 0:4, :], y[:, 4:8, :], ALU.subtract))
            link(tt(s[:, 8:10, :], s[:, 0:2, :], s[:, 2:4, :], ALU.add))
            link(tt(y[:, 2:4, :], s[:, 0:2, :], s[:, 2:4, :], ALU.subtract))
            link(tt(y[:, 0, :], s[:, 8, :], s[:, 9, :], ALU.add))
            link(tt(y[:, 1, :], s[:, 8, :], s[:, 9, :], ALU.subtract))
            link(tt(s[:, 8, :], s[:, 5, :], s[:, 7, :], ALU.subtract))
            link(tt(s[:, 9, :], s[:, 5, :], s[:, 7, :], ALU.add))

        def kv_dft():
            x, y, s = kv, kvy, kv
            pool.wait_ge(S("kv_sb"), NCT)
            for n in range(4):
                pool.wait_ge(parts_out[n], 48)
            link(tt(y[:, 0:8, :], x[:, 0:8, :], x[:, 8:16, :], ALU.add))
            yield
            link(tt(y[:, 8:16, :], x[:, 0:8, :], x[:, 8:16, :], ALU.subtract))
            yield
            even_side(x, y, s)
            link(scaled(s[:, 8:10, :], s[:, 8:10, :], R2))
            link(tt(y[:, 4, :], s[:, 4, :], s[:, 8, :], ALU.add))
            link(tt(y[:, 5, :], s[:, 4, :], s[:, 8, :], ALU.subtract))
            link(tt(y[:, 6, :], s[:, 9, :], s[:, 6, :], ALU.add))
            link(tt(y[:, 7, :], s[:, 9, :], s[:, 6, :], ALU.subtract))
            yield
            for t in range(3):
                link(tt(s[:, t, :], y[:, 9 + t, :], y[:, 15 - t, :], ALU.subtract))
                link(tt(s[:, 3 + t, :], y[:, 9 + t, :], y[:, 15 - t, :], ALU.add))
            link(pool.tensor_copy(s[:, 14, :], y[:, 8, :]))
            link(pool.tensor_copy(s[:, 15, :], y[:, 12, :]))
            yield
            for side, b0, p in ((0, 14, 0), (1, 15, 3)):
                link(scaled(s[:, 6, :], s[:, p + 1, :], R2))
                link(tt(s[:, 7, :], s[:, b0, :], s[:, 6, :], ALU.add))
                if side == 0:
                    link(tt(s[:, 8, :], s[:, b0, :], s[:, 6, :], ALU.subtract))
                else:
                    link(tt(s[:, 8, :], s[:, 6, :], s[:, b0, :], ALU.subtract))
                ca, cb = (C1, S1) if side == 0 else (S1, C1)
                link(scaled(s[:, 9, :], s[:, p, :], ca))
                link(scaled(s[:, 10, :], s[:, p + 2, :], cb))
                link(tt(s[:, 9, :], s[:, 9, :], s[:, 10, :], ALU.add))
                link(scaled(s[:, 10, :], s[:, p, :], cb))
                link(scaled(s[:, 11, :], s[:, p + 2, :], ca))
                link(tt(s[:, 10, :], s[:, 10, :], s[:, 11, :], ALU.subtract))
                o = 8 + 4 * side
                link(tt(y[:, o, :], s[:, 7, :], s[:, 9, :], ALU.add))
                link(tt(y[:, o + 2, :], s[:, 8, :], s[:, 10, :], ALU.add))
                if side == 0:
                    link(tt(y[:, o + 1, :], s[:, 7, :], s[:, 9, :], ALU.subtract))
                    link(tt(y[:, o + 3, :], s[:, 8, :], s[:, 10, :], ALU.subtract))
                else:
                    link(tt(y[:, o + 1, :], s[:, 9, :], s[:, 7, :], ALU.subtract))
                    link(tt(y[:, o + 3, :], s[:, 10, :], s[:, 8, :], ALU.subtract))
                yield
            pool.memset(expo[:, :], -0.5).then_inc(S("kvy_ready"), 1)

        for h in range(RING):
            take_values(h)
        work = kv_dft()
        for h in range(H):
            next(work, None)
            residual(h)
            if h + RING < H:
                take_values(h + RING)
        for _ in work:
            pass

        def inverse_roots(lo, n, which, name):
            pool.wait_ge(S(name), which)
            link(pool.tensor_scalar(rstd[:, lo:lo + n], mv[:, lo:lo + n, 1], EPS, None, ALU.add))
            tt(rstd[:, lo:lo + n], rstd[:, lo:lo + n], expo[:, lo:lo + n], ALU.pow).then_inc(S(name + "_root"), 1)

        inverse_roots(0, NT, 1, "var1")
        pool.wait_ge(S("y1_sum"), 1)
        s, y = scr1, y1
        even_side(x1, y, s)
        pool.sem_inc(S("y1_even"), 1)
        pool.wait_ge(S("late_in"), 16 * 7)
        pool.wait_ge(S("y1_diff"), 1)
        tt(x1[:, :, :], x1[:, :, :], bo_b[:, :].unsqueeze(1).broadcast_to([P, NT, D]), ALU.add).then_inc(S("x1b_ready"), 1)
        pool.wait_ge(S("z_sb"), NF)
        Z = lambda f: z[:, f, 1, :]
        t_ = lambda n: zs[:, 16 + n, :]
        F1, F2, A1, A2, B1, B2, T1, T2, T3 = (t_(n) for n in (7, 8, 9, 10, 11, 12, 13, 6, 5))
        O = {1: t_(0), 2: t_(1), 3: t_(2), 4: t_(3), 5: t_(4), 6: t_(6), 7: t_(5)}
        link(tt(F1, Z(2), Z(6), ALU.add))
        link(tt(F2, Z(2), Z(6), ALU.subtract))
        link(tt(A1, Z(1), Z(7), ALU.add))
        link(tt(A2, Z(1), Z(7), ALU.subtract))
        link(tt(B1, Z(3), Z(5), ALU.add))
        link(tt(B2, Z(3), Z(5), ALU.subtract))
        link(scaled(F1, F1, R2))
        link(tt(O[4], A2, B2, ALU.subtract))
        link(tt(A2, A2, B2, ALU.add))
        link(scaled(A2, A2, R2))
        link(tt(O[2], A2, F2, ALU.add))
        link(tt(O[6], A2, F2, ALU.subtract))
        link(scaled(A2, A1, S1))
        link(scaled(B2, B1, C1))
        link(tt(A2, A2, B2, ALU.add))
        link(scaled(A1, A1, C1))
        link(scaled(B1, B1, S1))
        link(tt(A1, A1, B1, ALU.subtract))
        link(tt(F2, F1, Z(4), ALU.add))
        link(tt(F1, F1, Z(4), ALU.subtract))
        link(tt(O[1], A2, F2, ALU.add))
        link(tt(O[7], A2, F2, ALU.subtract))
        link(tt(O[3], A1, F1, ALU.add))
        link(tt(O[5], A1, F1, ALU.subtract))
        pool.sem_inc(S("osum_ready"), 1)

        for n in range(4):
            inverse_roots(4 * n, 4, n + 1, "var2")
        for n in range(NT):
            pool.wait_ge(S("x2_ready"), n + 1)
            if n == 0:
                pool.wait_ge(S("z_ps"), NF)
            tt(x2b[:, n, :], x2[:, n, :], fb_b[:, :], ALU.add).then_inc(S("x2b_ready"), 1)
        for n in range(4):
            inverse_roots(4 * n, 4, n + 1, "var3")

    @block.vector
    def _(dve):
        chain = [0]

        def link(ins):
            chain[0] += 1
            ins.then_inc(S("dve_chain"), 1)
            dve.wait_ge(S("dve_chain"), chain[0])

        dve.sem_inc(S("mx_free"), 2)
        dve.memset(msplit[:, 3:8, :], 0.0)
        for b in range(RING - 1):
            dve.memset(k_ring[b][ROWS:KROWS, :], 1.0)
        dve.wait_ge(S("rot_in"), 32)
        for first in (0, 2):
            for n in (first, first + 1):
                kq, c = COMBOS[n]
                dve.wait_ge(S(f"xT_in{c}"), 16)
                if n == 2:
                    dve.wait_ge(S("part3_pool"), 1)
                if n == 3:
                    dve.wait_ge(S("part3_dve"), 1)
                col = (entc if kq else rotc)[:, c:c + 1]
                if kq:
                    dve.tensor_scalar(full[n % 2][:, :], xT[:, c, :], col, None, ALU.mult).then_inc(S("full_ready"), 1)
                else:
                    dve.tensor_scalar(full[n % 2][:, :], xT[:, c, :], col, float(DH) ** -0.5, ALU.mult, ALU.mult)\
                       .then_inc(S("full_ready"), 1)
            for n in (first, first + 1):
                kq, c = COMBOS[n]
                dve.wait_ge(S("part1_ready"), n + 1)
                dve.wait_ge(S("full_ready"), n + 1)
                dve.tensor_tensor(full[n % 2][:, :], full[n % 2][:, :], parts[3 * kq][:, c, :], ALU.subtract)\
                   .then_inc(S("rest_ready"), 1)
            n = first + 1
            c = COMBOS[n][1]
            dve.wait_ge(S("part2_ready"), n + 1)
            dve.wait_ge(S("rest_ready"), n + 1)
            dve.tensor_tensor(parts[5][:, c, :], full[1][:, :], parts[4][:, c, :], ALU.subtract)\
               .then_inc(S("part3_dve"), 1)
        dve.memset(k_ring[RING - 1][ROWS:KROWS, :], 1.0).then_inc(S("k_ones"), 1)
        dve.wait_ge(S("ctx_in"), 16)
        dve.tensor_reduce(csum[:, :], ctxT[:, :, :], AX.X, ALU.add).then_inc(S("csum_ready"), 1)

        def reduce_max(half, tile, use):
            dve.wait_ge(S("mx_ready"), use + 1)
            dve.tensor_reduce(mx[:, tile, half:half + 1], mx_ps[half], AX.XY, ALU.max).then_inc(S("mx_free"), 1)

        def split(h):
            def then(ins, n):
                ins.then_inc(S("split_chain"), 1)
                dve.wait_ge(S("split_chain"), h * 4 + n)
            dve.wait_ge(S("mx_free"), (h + 1) * (2 * UNITS) + 2)
            then(dve.tensor_reduce(negm[:, :], mx[:, :, :], AX.X, ALU.max, negate=True), 1)
            dve.wait_ge(S("mT_ready"), h) if not (isinstance(h, int) and h == 0) else None
            then(dve.tensor_copy(msplit[:, 0, :], negm[:, :]), 2)
            then(dve.tensor_tensor(mrest[:, :], negm[:, :], msplit[:, 0, :], ALU.subtract), 3)
            then(dve.tensor_copy(msplit[:, 1, :], mrest[:, :]), 4)
            dve.tensor_tensor(msplit[:, 2, :], mrest[:, :], msplit[:, 1, :], ALU.subtract).then_inc(S("split_ready"), 1)

        def normalise(b, h, bank):
            dve.wait_ge(S("outt_ready"), h + 1)
            dve.reciprocal(recip[:, bank, :, :], out_t[bank][:, :, :, 16]).then_inc(S("recip_ready"), 1)
            dve.wait_ge(S("recip_ready"), h + 1)
            dve.wait_ge(S("attn_used"), h + 1)
            dve.tensor_tensor(attn[b][:, :, :].rearrange("p (c s) d -> p s c d", s=4), out_t[bank][:, :, :, 0:DH],
                              recip[:, bank, :, :].unsqueeze(3).broadcast_to([P, 4, 4, DH]), ALU.mult)\
               .then_inc(S("attn_ready"), 1)

        for g in range(AHEAD):
            for half in range(2):
                reduce_max(half, g % UNITS, 2 * g + half)
            if g == UNITS - 1:
                split(0)

        def heads(it, count, end):
            for n in range(count * UNITS):
                g = n + AHEAD
                tile, h = g % UNITS, it * RING + n // UNITS
                if g < end:
                    for half in range(2):
                        reduce_max(half, tile, (it * (RING * UNITS) + g) * 2 + half)
                    if tile == UNITS - 1:
                        split(it * RING + g // UNITS)
                if n % UNITS == 2 and n > 2:
                    normalise((n // UNITS - 1) % RING, h - 1, (n // UNITS - 1) % 2)
            normalise((count - 1) % RING, it * RING + count - 1, (count - 1) % 2)

        with dve.Fori(0, LOOPS) as it:
            heads(it, RING, 1 << 30)
        heads(LOOPS, H - LOOPS * RING, (H - LOOPS * RING) * UNITS)

        def moments(src, lo, n, name):
            for t in range(lo, lo + n):
                last = dve.bn_stats(stats[:, t, :], src[:, t, :])
            link(last)
            for t in range(lo, lo + n):
                last = dve.bn_aggr(mv[:, t, :], stats[:, t, :])
            last.then_inc(S(name), 1)

        def norm(dst, src, t):
            return dve.tensor_scalar(dst[:, t, :], src[:, t, :], mv[:, t, 0:1], rstd[:, t:t + 1],
                                     ALU.subtract, ALU.mult)

        dve.wait_ge(S("attn_used"), H + RING)
        moments(y_sb, 0, NT, "var1")
        dve.wait_ge(S("var1_root"), 1)
        for t in range(NT):
            last = norm(x1, y_sb, t)
        link(last)
        y, s = y1, scr1
        dve.tensor_tensor(y[:, 0:8, :], x1[:, 0:8, :], x1[:, 8:16, :], ALU.add).then_inc(S("y1_sum"), 1)
        dve.tensor_tensor(y[:, 8:16, :], x1[:, 0:8, :], x1[:, 8:16, :], ALU.subtract).then_inc(S("y1_diff"), 1)
        dve.wait_ge(S("y1_diff"), 1)
        for t in range(3):
            dve.tensor_tensor(s[:, 10 + t, :], y[:, 9 + t, :], y[:, 15 - t, :], ALU.subtract)
            last = dve.tensor_tensor(s[:, 13 + t, :], y[:, 9 + t, :], y[:, 15 - t, :], ALU.add)
        link(last)

        def stt(o, a, by, b, op):
            return dve.scalar_tensor_tensor(o, a, by, b, ALU.mult, op)

        g0 = junk[:, 0, :]
        g1 = junk[:, 1, :]
        v0, v1, v2, v3 = (c_big[:, n, :] for n in range(4))
        for side in range(2):
            b0, p = y[:, 8 + 4 * side, :], 10 + 3 * side
            ca, cb = (C1, S1) if side == 0 else (S1, C1)
            stt(v0, s[:, p + 1, :], R2, b0, ALU.add)
            if side == 0:
                stt(v1, s[:, p + 1, :], -R2, b0, ALU.add)
            else:
                stt(v1, s[:, p + 1, :], R2, b0, ALU.subtract)
            dve.tensor_scalar(g0, s[:, p + 2, :], cb, None, ALU.mult)
            link(dve.tensor_scalar(g1, s[:, p + 2, :], ca, None, ALU.mult))
            stt(v2, s[:, p, :], ca, g0, ALU.add)
            link(stt(v3, s[:, p, :], cb, g1, ALU.subtract))
            if side == 0:
                b4 = y[:, 12, :]
            o = 8 + 4 * side
            dve.tensor_tensor(y[:, o, :], v0, v2, ALU.add)
            dve.tensor_tensor(y[:, o + 2, :], v1, v3, ALU.add)
            if side == 0:
                dve.tensor_tensor(y[:, o + 1, :], v0, v2, ALU.subtract)
                last = dve.tensor_tensor(y[:, o + 3, :], v1, v3, ALU.subtract)
            else:
                dve.tensor_tensor(y[:, o + 1, :], v2, v0, ALU.subtract)
                last = dve.tensor_tensor(y[:, o + 3, :], v3, v1, ALU.subtract)
            link(last)
        dve.wait_ge(S("y1_even"), 1)
        stt(y[:, 4, :], s[:, 8, :], R2, s[:, 4, :], ALU.add)
        stt(y[:, 5, :], s[:, 8, :], -R2, s[:, 4, :], ALU.add)
        stt(y[:, 6, :], s[:, 9, :], R2, s[:, 6, :], ALU.add)
        stt(y[:, 7, :], s[:, 9, :], R2, s[:, 6, :], ALU.subtract).then_inc(S("y1_two"), 1)
        dve.sem_inc(S("y1_ready"), 1)
        for n, f in enumerate(F_ORDER):
            dve.wait_ge(S("x1f_ps"), n + 1)
            dve.wait_ge(S("kvf_sb"), 3 * (n + 1))
            b = 4 + n % 4
            for m in range(2):
                if n:
                    dve.wait_ge(S("prod_done"), 2 * n - 1 + m)
                dve.tensor_tensor_reduce(out=junk[:, m, :], in0=ps[:, b, m * D:(m + 1) * D], in1=spec[:, f, m, :],
                                         scale=1.0, scalar=0.0, op0=ALU.mult, op1=ALU.add,
                                         accum_out=ri[:, f, m:m + 1]).then_inc(S("prod_done"), 1)
        dve.wait_ge(S("prod_done"), 2 * NF)
        dve.wait_ge(S("fold_sb"), 6)
        link(dve.scalar_tensor_tensor(extra[:, :], bb[:, :], float(LC), extra[:, :], ALU.mult, ALU.add))
        link(dve.scalar_tensor_tensor(ri[0:1, 0, 0:1], extra[:, :], float(L), ri[0:1, 0, 0:1], ALU.mult, ALU.add))
        dve.wait_ge(S("late_in"), 16 * 7)
        dve.tensor_copy(rj[:, :, 0], ri[:, :, 0]).then_inc(S("rj_ready"), 1)
        dve.tensor_scalar(rj[:, :, 1], ri[:, :, 1], sign[:, 1:2], None, ALU.mult).then_inc(S("rj_ready"), 1)
        dve.tensor_scalar(rj[:, :, 2], ri[:, :, 1], sign[:, 0:1], None, ALU.mult).then_inc(S("rj_ready"), 1)
        dve.tensor_copy(rj[:, :, 3], ri[:, :, 0]).then_inc(S("rj_ready"), 1)
        dve.tensor_copy(wffn[:, :, :], wffn_words[:, :, 0:2 * D:2]).then_inc(S("wffn_ready"), 1)
        dve.wait_ge(S("corr_sb"), 1)
        link(dve.max(top[:, 0:8], c_row[:, :]))
        dve.tensor_scalar(nmax[:, :], top[:, 0:1], -1.0, None, ALU.mult).then_inc(S("nmax_ready"), 1)
        link(dve.match_replace(c2_row[:, :], top[:, 0:8], c_row[:, :], NEG))
        link(dve.max(top[:, 8:16], c2_row[:, :]))
        link(dve.memset(top[:, TOPK:16], NEG))
        link(dve.match_replace(w_row[:, :], top[:, 8:16], c2_row[:, :], NEG))
        dve.wait_ge(S("e_ready"), 1)
        dve.scalar_tensor_tensor(w_row[:, :], w_row[:, :], NEG, e_row[:, :], ALU.is_equal, ALU.mult,
                                 accum_out=wsum[:, :]).then_inc(S("w_ready"), 1)
        dve.wait_ge(S("w_ready"), 1)
        link(dve.reciprocal(wrec[:, :], wsum[:, :]))
        dve.tensor_scalar(e16s[:, :], e16[:, :], wrec[:, :], None, ALU.mult).then_inc(S("e16_ready"), 1)
        hp = ps[:, 0, 0:18].rearrange("p (f m) -> p f m", m=2)
        dve.wait_ge(S("h_ps"), 1)
        dve.tensor_copy(hh[:, :, 0:2], hp).then_inc(S("h_sb"), 1)
        dve.tensor_scalar(hh[:, :, 2], hp[:, :, 1], -1.0, None, ALU.mult).then_inc(S("h_sb"), 1)
        dve.tensor_copy(hh[:, :, 3], hp[:, :, 0]).then_inc(S("h_sb"), 1)
        hp2 = ps[:, 1, 0:18].rearrange("p (f m) -> p f m", m=2)
        dve.wait_ge(S("h_ps"), 2)
        dve.tensor_copy(hf[:, :, 0:2], hp2).then_inc(S("hf_sb"), 1)
        dve.tensor_scalar(hf[:, :, 2], hp2[:, :, 1], -1.0, None, ALU.mult).then_inc(S("hf_sb"), 1)
        dve.wait_ge(S("hf_sb"), 2)
        for n, f in enumerate(F_ORDER):
            dve.wait_ge(S("g_tmp"), n + 1)
            stt(gtab[:, f, 0, :], tab_inv[:, f, 1, :], hf[:, f, 2:3], gtmp[:, n % 2, 0, :], ALU.add).then_inc(S("g_ready"), 1)
            stt(gtab[:, f, 1, :], tab_inv[:, f, 0, :], hf[:, f, 1:2], gtmp[:, n % 2, 1, :], ALU.add).then_inc(S("g_ready"), 1)
        R = lambda f: z[:, f, 0, :]
        tt = lambda o, a, b, op: dve.tensor_tensor(o, a, b, op)
        E = [zs[:, n, :] for n in range(9)]
        A1, A2, B1, B2, P1, P2, Q1 = (zs[:, 9 + n, :] for n in range(7))
        Q2 = g0
        dve.wait_ge(S("z_sb"), NF)
        tt(A1, R(0), R(8), ALU.add)
        tt(A2, R(0), R(8), ALU.subtract)
        tt(B1, R(2), R(6), ALU.add)
        tt(B2, R(2), R(6), ALU.subtract)
        tt(P1, R(1), R(7), ALU.add)
        tt(P2, R(1), R(7), ALU.subtract)
        tt(Q1, R(3), R(5), ALU.add)
        link(tt(Q2, R(3), R(5), ALU.subtract))
        tt(g1, A1, R(4), ALU.add)
        tt(E[2], A1, R(4), ALU.subtract)
        stt(E[1], B2, R2, A2, ALU.add)
        stt(E[3], B2, -R2, A2, ALU.add)
        tt(v0, P1, Q1, ALU.subtract)
        link(tt(v1, P1, Q1, ALU.add))
        tt(E[0], g1, B1, ALU.add)
        tt(E[4], g1, B1, ALU.subtract)
        dve.tensor_scalar(v2, Q2, S1, None, ALU.mult)
        link(dve.tensor_scalar(v3, Q2, C1, None, ALU.mult))
        stt(A1, P2, C1, v2, ALU.add)
        stt(A2, P2, S1, v3, ALU.subtract)
        stt(E[6], v0, -R2, E[2], ALU.add)
        link(tt(E[8], E[0], v1, ALU.subtract))
        stt(E[2], v0, R2, E[2], ALU.add)
        tt(E[0], E[0], v1, ALU.add)
        tt(E[7], E[1], A1, ALU.subtract)
        link(tt(E[5], E[3], A2, ALU.subtract))
        tt(E[1], E[1], A1, ALU.add)
        link(tt(E[3], E[3], A2, ALU.add))
        dve.wait_ge(S("x1b_ready"), 1)
        dve.wait_ge(S("osum_ready"), 1)
        osl = {1: 16, 2: 17, 3: 18, 4: 19, 5: 20, 6: 22, 7: 21}
        tt(x2[:, 0, :], E[0], x1[:, 0, :], ALU.add)
        tt(x2[:, 8, :], E[8], x1[:, 8, :], ALU.add)
        for t in range(1, 8):
            tt(x2[:, t, :], E[t], zs[:, osl[t], :], ALU.add)
            last = tt(x2[:, 16 - t, :], E[t], zs[:, osl[t], :], ALU.subtract)
        link(last)
        tt(x2[:, 1:8, :], x2[:, 1:8, :], x1[:, 1:8, :], ALU.add)
        link(tt(x2[:, 9:16, :], x2[:, 9:16, :], x1[:, 9:16, :], ALU.add))
        moments(x2, 0, 4, "var2")
        for n in range(4):
            if n < 3:
                moments(x2, 4 * n + 4, 4, "var2")
            dve.wait_ge(S("var2_root"), n + 1)
            for t in range(4 * n, 4 * n + 4):
                norm(x2, x2, t).then_inc(S("x2_ready"), 1)
            for t in range(4 * n, 4 * n + 4):
                dve.wait_ge(S("x2_ready"), t + 1)
                last = dve.tensor_reduce(amax[:, t:t + 1], x2[:, t, :], AX.X, ALU.max, apply_absolute_value=True)
            link(last)
            g = slice(4 * n, 4 * n + 4)
            link(dve.tensor_scalar(xscale[:, g], amax[:, g], 1e-6, 1.0 / 127.0, ALU.max, ALU.mult))
            dve.reciprocal(xinv[:, g], xscale[:, g]).then_inc(S("xinv_ready"), 1)
        dve.wait_ge(S("xinv_ready"), 4)

        def clip(t):
            dve.wait_ge(S("xq_ready"), t + 1)
            dve.tensor_scalar(xqc[:, t % 4, :], xq[:, t % 4, :], ROUND - 128.0, ROUND + 127.0, ALU.max, ALU.min)\
               .then_inc(S("xqc_ready"), 1)
            dve.wait_ge(S("xqc_ready"), t + 1)
            dve.tensor_scalar(xqb[:, t, :], xqc[:, t % 4, :], -ROUND, None, ALU.add).then_inc(S("xqb_ready"), 1)

        def scale(t):
            dve.wait_ge(S("ffn_ps"), t + 1)
            dve.scalar_tensor_tensor(y3[:, t, :], ps[:, 4 + t % 4, 0:D], xscale[:, t:t + 1], ws_b[:, :],
                                     ALU.mult, ALU.mult).then_inc(S("y3_made"), 1)
            dve.wait_ge(S("y3_made"), t + 1)
            dve.wait_ge(S("x2b_ready"), t + 1)
            return dve.tensor_tensor(y3[:, t, :], y3[:, t, :], x2b[:, t, :], ALU.add)

        for t in range(NT):
            clip(t)
            if t >= 4:
                link(scale(t - 4))
        for t in range(NT - 4, NT):
            link(scale(t))
        for n in range(4):
            moments(y3, 4 * n, 4, "var3")
        for n in range(4):
            dve.wait_ge(S("var3_root"), n + 1)
            for t in range(4 * n, 4 * n + 4):
                norm(x3, y3, t).then_inc(S("x3_ready"), 1)


def kernel(**inputs):
    import concourse.bacc as bacc
    from concourse.bass_utils import run_bass_kernel_spmd

    a = {k: np.asarray(v) for k, v in inputs.items()}

    def cols(v):
        return np.ascontiguousarray(v.reshape(CT, P).T)

    def rows_of(v):
        return np.ascontiguousarray(np.broadcast_to(v[None, :], (P, v.shape[0])))

    arrays = {
        "x": a["x"][0], "xT": a["x"][0].T, "ctxT": a["ctx_1024"][0].T,
        "rotc": cols(a["L0_attn_rotation_params"].reshape(-1)), "entc": cols(a["L0_attn_entangle_params"].reshape(-1)),
        "wkT": a["L0_xattn_Wk"].T, "wqT": a["L0_xattn_Wq"].T, "wvT": a["L0_xattn_Wv"].T, "wo": a["L0_xattn_Wo"],
        "bq": cols(a["L0_xattn_bq"]), "bk": cols(a["L0_xattn_bk"]), "bv": cols(a["L0_xattn_bv"]),
        "bo_b": rows_of(a["L0_xattn_bo"]), "ws_b": rows_of(a["L0_ffn_weight_scale"]), "fb_b": rows_of(a["L0_ffn_bias"]),
        "wffnT": a["L0_ffn_weight_q"].T.astype(np.int64),
        **tables(),
    }
    arrays = {k: np.ascontiguousarray(v) for k, v in arrays.items()}
    nc = bacc.Bacc("TRN2", target_bir_lowering=False, num_devices=1)
    handles = {k: nc.dram_tensor(k, v.shape, mybir.dt.from_np(v.dtype), kind="ExternalInput").ap()
               for k, v in arrays.items()}
    result = nc.dram_tensor("layer_out", [L, D], F32, kind="ExternalOutput").ap()
    decoder_layer(nc, handles, result)
    r = run_bass_kernel_spmd(nc, [arrays], core_ids=[0])
    return r.results[0]["layer_out"].reshape(1, L, D)
```

```python
from contextlib import ExitStack
import math

import numpy as np

import concourse.bass as bass
from concourse import mybir

P = 128
F32 = mybir.dt.float32
BF16 = mybir.dt.bfloat16
I32 = mybir.dt.int32
ALU = mybir.AluOpType
ACT = mybir.ActivationFunctionType
AX = mybir.AxisListType

L, D, H, DH = 2048, 256, 16, 16
NT = L // P
LC = 1601
NCT = (LC + P - 1) // P
CT = D // P
ROWS = 6 * DH
KROWS = ROWS + 3
RING = 4
LOOPS = 3
UNITS = 16
AHEAD = 19
CHUNK = 512
NF = 9
EPS = 1e-5
TOPK = int(2 * math.log(L))
NEG = -3.0e38
ROUND = 1.5 * 2.0 ** 23
C1, S1, R2 = math.cos(math.pi / 8), math.sin(math.pi / 8), math.sqrt(0.5)
K_PARTS = [(0, 3, 0), (48, 2, 0), (80, 1, 0)]
Q_PARTS = [(0, 1, 0), (16, 1, 0), (32, 1, 0), (48, 1, 1), (64, 1, 1), (80, 1, 2)]
LOADS = len(K_PARTS) + len(Q_PARTS)


def tables():
    f1 = np.arange(NF)
    a, b = np.arange(P), np.arange(P)
    ang = 2 * np.pi * ((a[:, None, None] * (f1[None, :, None] + 16 * b[None, None, :])) % L) / L
    c, s = np.cos(ang), np.sin(ang)
    t1 = np.stack([c, s, -s], axis=2)
    t2 = np.stack([c.transpose(2, 1, 0), s.transpose(2, 1, 0)], axis=2)
    wt = np.where((f1 == 0) | (f1 == 8), 1.0, 2.0)
    ang16 = 2 * np.pi * ((f1[:, None] * np.arange(16)[None, :]) % 16) / 16
    w16 = np.stack([np.cos(ang16), -np.sin(ang16)], 1) * wt[:, None, None] / (L * D)
    e16 = np.stack([np.cos(ang16), np.sin(ang16)], 1) * wt[:, None, None] / L
    sgn = np.where(a < 64, 1.0, -1.0)
    sel = np.zeros((P, 68))
    for g in range(4):
        sel[32 * g + np.arange(17), 17 * g + np.arange(17)] = 1
    f = np.float32
    return {
        "tab_fwd": t1.astype(f), "tab_inv": t2.astype(f),
        "tab_w16": np.ascontiguousarray(w16.reshape(18, 16)).astype(f),
        "tab_e16": np.ascontiguousarray(e16.transpose(2, 0, 1).reshape(1, 16 * 18)).astype(f),
        "tab_sign": np.stack([sgn, -sgn], 1).astype(f),
        "tab_select": np.concatenate([np.eye(P), sel], 1).astype(f),
    }


def decoder_layer(nc, A, out):
    ctx = ExitStack()
    base = (nc.sbuf_base + 31) // 32 * 32
    KB = 1024
    names = [0]

    def sb(off, shape, dt=F32):
        names[0] += 1
        return nc.alloc_sbuf_tensor_at(f"t{names[0]}", shape, dt, offset=base + off)

    O_X, O_Y, O_KV, O_KQ = 0, 16 * KB, 32 * KB, 64 * KB
    O_SP, O_P, O_OSB, O_V = 88 * KB, 120 * KB, 136 * KB, 140 * KB
    O_T1, O_T2, O_FR, O_S = 146 * KB, 160 * KB, 170 * KB, 186 * KB

    class Region:
        def __init__(self, at, end):
            self.at, self.end = at, end

        def __call__(self, shape, dt=F32):
            size = int(np.prod(shape[1:])) * {F32: 4, BF16: 2, I32: 4}[dt]
            t = sb(self.at, shape, dt)
            self.at += (size + 31) // 32 * 32
            assert base + self.at <= base + self.end, (self.at, self.end)
            return t

    xT = sb(O_Y, [P, CT, L])
    parts = [sb(O_SP + 8 * KB * n, [P, CT, L], BF16) for n in range(6)]
    full = [sb(O_FR + 8 * KB * n, [P, L]) for n in range(2)]
    ctxT = sb(O_T1, [P, CT, LC])
    weights = sb(O_T2, [P, 4 * CT, D])
    wkT, wqT, wvT, wo = (weights[:, CT * n:CT * n + CT, :] for n in range(4))
    sum_junk = sb(O_V + 2 * KB, [P, LC], BF16)
    bias_b = sb(O_V, [P, 2 * D])
    bias_row = sb(O_T2 + 8 * KB, [1, 2 * D])
    ab = sb(O_OSB, [P, CT, 2 * D])
    x_sb = sb(O_X, [P, NT, D])
    y_sb = x_sb
    o_ring = [O_KQ, O_KQ + 8 * KB, O_KQ + 16 * KB, O_Y]
    k_ring = [sb(o, [P, L], BF16) for o in o_ring]
    q_ring = [sb(o + 4 * KB, [P, L], BF16) for o in o_ring]
    probs = [sb(O_P + 2 * KB * n, [P, CHUNK]) for n in range(8)]
    o_sb = [sb(O_OSB + 2 * KB * n, [P, CHUNK]) for n in range(2)]
    v_ring = [sb(O_Y + 8 * KB + 2 * KB * b, [P, NT, 32]) for b in range(RING)]
    kv = sb(O_KV, [P, NT, 2 * D])
    kvy = sb(O_SP, [P, 16, 2 * D])
    tab_fwd = sb(O_T1, [P, NF, 3, P])
    tab_inv = sb(O_T2, [P, NF, 2, P])
    mid = Region(O_FR, O_FR + 16 * KB)
    attn = [sb(O_V + KB * b, [P, NT, DH]) for b in range(RING)]
    bo_b, ws_b, fb_b = mid([P, D]), mid([P, D]), mid([P, D])
    wffn_words, wffn = mid([P, CT, 2 * D], I32), mid([P, CT, D], BF16)
    w16, e16, e16s = mid([18, 16]), mid([1, 16 * 18]), mid([1, 16 * 18])
    sign, rj, ri, hh, hf = mid([P, 2]), mid([P, NF, 4]), mid([P, NF, 2]), mid([P, NF, 4]), mid([P, NF, 3])
    u_sb, uT = mid([P, 18]), mid([18, P])
    mv, rstd, expo = mid([P, NT, 2]), mid([P, NT]), mid([P, NT])
    stats = mid([P, NT, 6])
    amax, xscale, xinv = mid([P, NT]), mid([P, NT]), mid([P, NT])
    top, wsum, wrec, nmax = mid([1, 16]), mid([1, 1]), mid([1, 1]), mid([1, 1])
    small = Region(O_S, O_S + 5 * KB + 700)
    select, identb = small([P, P + 68]), small([P, P], BF16)
    ident, sel = select[:, 0:P], select[:, P:P + 68]
    cols = small([P, 5 * CT])
    rotc, entc, bqc, bkc, bvc = (cols[:, CT * n:CT * n + CT] for n in range(5))
    ones_row = small([1, P])
    mx, negm, mrest = small([P, NT, 2]), small([P, NT]), small([P, NT])
    msplit, mT, recip = small([P, 8, NT], BF16), small([3 * NT, P], BF16), small([P, 2, 4, 4])
    csum, gvec, bb, extra = small([P, CT]), small([P, CT]), small([1, 1]), small([1, 1])
    assert base + O_S + 5 * KB + 700 <= 212863
    x1 = sb(O_X, [P, NT, D])
    spec = sb(O_KV, [P, NF, 5, D])
    gtab = sb(O_KV + 46 * KB, [P, NF, 2, P])
    y1 = sb(O_P, [P, 16, D])
    scr1 = sb(O_Y, [P, 16, D])
    c_row = sb(O_OSB, [1, L])
    junk = sb(O_OSB + 8 * KB, [P, 2, D])
    c2_row, e_row, w_row = (sb(O_SP + 8 * KB * n, [1, L]) for n in range(3))
    gtmp = sb(O_OSB, [P, 2, 2, P])
    c_big = sb(O_OSB, [P, 8, D])
    z = sb(O_SP, [P, NF, 2, D])
    zs = sb(O_SP + 18 * KB, [P, 30, D])
    x2 = sb(O_Y, [P, NT, D])
    x2b = sb(O_KV, [P, NT, D])
    xq = sb(O_KV + 16 * KB, [P, 4, D])
    xqc = sb(O_KV + 20 * KB, [P, 4, D])
    xqb = sb(O_KV + 24 * KB, [P, NT, D], BF16)
    xqT = sb(O_KV + 32 * KB, [P, NT, D], BF16)
    y3 = sb(O_SP, [P, NT, D])
    x3 = sb(O_X, [P, NT, D])

    ps = ctx.enter_context(nc.psum_tensor("ps", [P, 8, CHUNK], F32))
    mx_ps = [ps[:, 0:2, :], ps[:, 2:4, :]]
    ex_ps = [ps[:, 4, :], ps[:, 5, :]]
    o_ps = [ps[:, 6 + n, :] for n in range(2)]
    out_t = [ps[:, 6 + n, 0:NT * 17].rearrange("p (s c d) -> p s c d", s=4, d=17) for n in range(2)]
    mt_ps = [ps[:, 6 + n, 384:448].bitcast(BF16) for n in range(2)]

    ks = nc.dram_tensor("k_parts", [3, D, L], BF16, kind="Internal").ap()
    qs = nc.dram_tensor("q_parts", [3, D, L], BF16, kind="Internal").ap()

    sems = {}

    def S(name):
        if name not in sems:
            sems[name] = ctx.enter_context(nc.semaphore(name))
        return sems[name]

    HALF = L // 2
    PIECES = [(0, 0, slice(0, HALF)), (1, 0, slice(0, HALF)), (0, 0, slice(HALF, L)), (1, 0, slice(HALF, L)),
              (0, 1, slice(0, L)), (1, 1, slice(0, L))]
    CTX_BANKS = (4, 5, 7)
    kq_loaded = [S(f"kq_loaded{b}") for b in range(RING)]
    m_rows = [S(f"m_rows{b}") for b in range(RING)]
    parts_out = [S(f"parts_out{c}") for c in range(CT)]

    SLOT_R = {0: 0, 8: 1, 4: 2, 2: 4, 6: 5, 1: 8, 7: 9, 3: 10, 5: 11}
    SLOT_I = {4: 3, 2: 6, 6: 7, 1: 12, 7: 13, 3: 14, 5: 15}
    F_ORDER = [0, 8, 4, 2, 6, 1, 7, 3, 5]

    block = ctx.enter_context(nc.Block())

    def load(sp, b, h):
        for r, n, m in K_PARTS:
            sp.dma_start(k_ring[b][r:r + DH * n, :], ks[m:m + n, bass.ds(h * DH, DH), :]).then_inc(kq_loaded[b], 16)
        for r, n, m in Q_PARTS:
            sp.dma_start(q_ring[b][r:r + DH * n, :], qs[m:m + n, bass.ds(h * DH, DH), :]).then_inc(kq_loaded[b], 16)

    def rows(sp, b, h):
        sp.wait_ge(S("mT_copied"), h + 1)
        sp.dma_start(q_ring[b][ROWS:KROWS, :].rearrange("p (t i) -> p t i", i=P), mT[:, :]).then_inc(m_rows[b], 16)

    @block.sync
    def _(sp):
        for n in range(2):
            sp.dma_start(xT[:, 0, HALF * n:HALF * n + HALF], A["xT"][0:P, HALF * n:HALF * n + HALF])\
              .then_inc(S(f"xT_in{n}"), 16)
        sp.dma_start(weights[:, :, :], A["weights"].rearrange("(g p) n -> p g n", p=P)).then_inc(S("weights_in"), 16)
        sp.dma_start(ctxT[:, :, :], A["ctxT"].rearrange("(c p) t -> p c t", p=P)).then_inc(S("ctx_in"), 16)
        sp.dma_start(xT[:, 1, :], A["xT"][P:2 * P, :]).then_inc(S("xT_in2"), 16)
        x_v = A["x"].rearrange("(n p) c -> p n c", p=P)
        for m in range(3):
            if m < 2:
                sp.wait_ge(S(f"part{m + 1}_ready"), 4)
            else:
                sp.wait_ge(S("part3_k"), 2)
            for r, n, first in K_PARTS:
                if first <= m < first + n:
                    sp.dma_start(k_ring[0][r + DH * m:r + DH * m + DH, :], parts[3 + m][0:DH, 0, :])\
                      .then_inc(S("first_loaded"), 16)
            if m == 2:
                sp.wait_ge(S("part3_q"), 2)
            for r, _, part in Q_PARTS:
                if part == m:
                    sp.dma_start(q_ring[0][r:r + DH, :], parts[m][0:DH, 0, :]).then_inc(S("first_loaded"), 16)

        def send_parts(c):
            for n in range(6):
                dst = ks if n >= 3 else qs
                sp.dma_start(dst[n % 3, c * P:(c + 1) * P, :], parts[n][:, c, :]).then_inc(parts_out[c], 16)

        send_parts(0)
        for i in range(4):
            sp.dma_start(x_sb[:, 4 * i:4 * i + 4, :], x_v[:, 4 * i:4 * i + 4, :]).then_inc(S("x_in"), 16)
        sp.wait_ge(parts_out[0], 96)
        load(sp, 1, 1)
        load(sp, 2, 2)
        sp.wait_ge(S("full_ready"), 6)
        load(sp, 3, 3)
        sp.wait_ge(S("part3_late"), 2)
        send_parts(1)
        rows(sp, 0, 0)
        sp.wait_ge(parts_out[1], 96)
        late = [(bo_b, "bo_b"), (ws_b, "ws_b"), (fb_b, "fb_b"), (sign, "tab_sign"), (w16, "tab_w16"), (e16, "tab_e16")]
        for t, name in late:
            sp.dma_start(t[:, :], A[name]).then_inc(S("late_in"), 16)
        sp.dma_start(wffn_words[:, :, :], A["wffnT"].bitcast(I32).rearrange("(c p) n -> p c n", p=P))\
          .then_inc(S("late_in"), 16)
        sp.wait_ge(S("kv_ps"), NCT)
        sp.wait_ge(S("csum_ready"), CT)
        sp.dma_start(tab_fwd[:, :, :, :], A["tab_fwd"]).then_inc(S("tabs_in"), 16)
        sp.dma_start(tab_inv[:, :, :, :], A["tab_inv"]).then_inc(S("tabs_in"), 16)

        def step(it, hb, more_rows, more_loads):
            h = it * RING + hb
            if more_rows:
                rows(sp, (hb + 1) % RING, h + 1)
            if more_loads:
                sp.wait_ge(S("quads_done"), (h + 1) * UNITS + 2)
                load(sp, hb % RING, h + RING)

        with sp.Fori(0, LOOPS) as it:
            for hb in range(RING):
                step(it, hb, True, True)
        for hb in range(H - LOOPS * RING):
            h = LOOPS * RING + hb
            step(LOOPS, hb, h + 1 < H, h + RING < H)
        o_v = out.rearrange("(n p) c -> p n c", p=P)
        for n in range(4):
            sp.wait_ge(S("x3_ready"), 4 * n + 4)
            sp.dma_start(o_v[:, 4 * n:4 * n + 4, :], x3[:, 4 * n:4 * n + 4, :]).then_inc(S("stored"), 16)
        sp.wait_ge(S("stored"), 64)

    @block.tensor
    def _(pe):
        pe.sem_inc(S("quads_done"), 2)
        pe.wait_ge(S("weights_in"), 16)
        pe.wait_ge(S("cols_in"), 16)
        for e in range(CT):
            for half, (wl, wr) in enumerate(((wkT, wqT), (wvT, wo))):
                for c in range(CT):
                    pe.matmul(ps[:, e, half * D:(half + 1) * D], wl[:, c, e * P:(e + 1) * P], wr[:, c, :],
                              start=(c == 0), stop=(c == CT - 1))
        for half, (bl, wr) in enumerate(((bkc, wqT), (bvc, wo))):
            for c in range(CT):
                pe.matmul(ps[0:1, 2, half * D:(half + 1) * D], bl[:, c:c + 1], wr[:, c, :],
                          start=(c == 0), stop=(c == CT - 1))
        for e in range(CT):
            for c in range(CT):
                pe.matmul(ps[:, 3, e:e + 1], wkT[:, c, e * P:(e + 1) * P], bqc[:, c:c + 1],
                          start=(c == 0), stop=(c == CT - 1))
        for c in range(CT):
            last = pe.matmul(ps[0:1, 3, 4:5], bkc[:, c:c + 1], bqc[:, c:c + 1], start=(c == 0), stop=(c == CT - 1))
        last.then_inc(S("fold_ps"), 1)
        pe.wait_ge(S("ones_set"), 1)
        pe.wait_ge(S("fold_sb"), 3)
        pe.matmul(ps[:, 6, :], ones_row[0:1, :], bias_row[0:1, :], start=True, stop=True).then_inc(S("fold_ps"), 1)

        def context(n):
            t, half, c = n // 4, n // 2 % 2, n % 2
            if n == 0:
                pe.wait_ge(S("ctx_in"), 16)
            if n % 4 == 0 and t >= 3:
                pe.wait_ge(S("kv_sb"), t - 2)
            m = min(P, LC - t * P)
            last = pe.matmul(ps[0:m, CTX_BANKS[t % 3], half * D:(half + 1) * D], ctxT[:, c, t * P:t * P + m],
                             ab[:, c, half * D:(half + 1) * D], start=(c == 0), stop=(c == CT - 1))
            if n % 4 == 3:
                last.then_inc(S("kv_ps"), 1)

        def maxima(b, half, tile, use):
            pe.wait_ge(S("mx_free"), use + 1)
            for n in range(2):
                k0 = half * 1024 + n * CHUNK
                last = pe.matmul(mx_ps[half][:, n, :], q_ring[b][0:ROWS, tile * P:(tile + 1) * P],
                                 k_ring[b][0:ROWS, k0:k0 + CHUNK], start=True, stop=True)
            last.then_inc(S("mx_ready"), 1)

        def turn_maxima(h, bank):
            pe.wait_ge(S("split_ready"), h + 1)
            pe.transpose(mt_ps[bank], msplit[:, :, :].rearrange("p m t -> p (m t)"), identb[:, :])\
              .then_inc(S("mT_ready"), 1)

        def exponents(b, c, j, e):
            pe.wait_ge(S("probs_ready"), e + 1)
            pe.matmul(ex_ps[c % 2], k_ring[b][0:KROWS, j * P:(j + 1) * P],
                      q_ring[b][0:KROWS, c * CHUNK:(c + 1) * CHUNK], start=True, stop=True).then_inc(S("scores_ready"), 1)

        def values(it, n):
            hb, j = n // UNITS, n % UNITS
            if j == 0:
                pe.wait_ge(S("mT_copied"), it * RING + hb + 1)
            pe.wait_ge(S("probs_ready"), (it * (RING * UNITS) + n) * 4 + 6)
            for c in range(4):
                last = pe.matmul(o_ps[hb % 2][32 * c:32 * c + 32, :], v_ring[hb % RING][:, j, :],
                                 probs[4 * (n % 2) + c][:, :], start=(j == 0), stop=(j == UNITS - 1))
            last.then_inc(S("quads_done"), 1)

        def turn_out(h, bank):
            pe.wait_ge(S("o_copied"), h + 1)
            for s in range(4):
                last = pe.matmul(out_t[bank][:, s, :, :], o_sb[bank][:, s * P:(s + 1) * P], sel[:, :],
                                 start=True, stop=True)
            last.then_inc(S("outt_ready"), 1)

        done = 0
        for use in range(2 * AHEAD):
            g, half = use // 2, use % 2
            if use == 0:
                pe.wait_ge(S("first_loaded"), 16 * 12)
                pe.wait_ge(S("fold_sb"), 5)
            if g == UNITS and half == 0:
                pe.wait_ge(kq_loaded[1], 16 * LOADS)
            maxima(g // UNITS, half, g % UNITS, use)
            while done < 4 * NCT and done * (2 * UNITS) < (use + 1) * 4 * NCT:
                context(done)
                done += 1
            if use == 2 * UNITS + 1:
                pe.wait_ge(S("consts_in"), 32)
                pe.wait_ge(S("fold_sb"), 6)
                turn_maxima(0, 0)
        pe.wait_ge(S("kv_sb"), NCT)
        pe.wait_ge(S("v_set"), RING)
        pe.wait_ge(S("k_ones"), RING)

        def scores(it, n, c):
            hb, j = n // UNITS, n % UNITS
            if j == 0 and c == 0:
                pe.wait_ge(m_rows[hb % RING], (it + hb // RING) * 16 + 16)
            exponents(hb % RING, c, j, it * (RING * UNITS * 4) + 4 * n + c)

        def heads(it, count, last):
            for n in range(count * UNITS):
                hb, j = n // UNITS, n % UNITS
                h = it * RING + hb
                g = n + AHEAD
                more = not last or n + 1 < count * UNITS
                if more:
                    scores(it, n + 1, 0)
                    scores(it, n + 1, 1)
                if j == 0:
                    pe.wait_ge(S("v_ready"), h + 1)
                if j == 14 and (not last or hb + 1 < count):
                    pe.wait_ge(S("attn_ready"), h)
                    turn_maxima(h + 1, (hb + 1) % 2)
                values(it, n)
                if more:
                    scores(it, n + 1, 2)
                    scores(it, n + 1, 3)
                if not last or g < count * UNITS:
                    mb, tile, use = g // UNITS % RING, g % UNITS, (it * (RING * UNITS) + g) * 2
                    if tile == 0:
                        nth = it + g // UNITS // RING + (1 if mb else 0)
                        pe.wait_ge(kq_loaded[mb], nth * (16 * LOADS))
                    maxima(mb, 0, tile, use)
                    maxima(mb, 1, tile, use + 1)
                if j == UNITS - 1:
                    turn_out(h, hb % 2)

        for c in range(4):
            scores(0, 0, c)
        with pe.Fori(0, LOOPS) as it:
            heads(it, RING, False)
        heads(LOOPS, H - LOOPS * RING, True)

        def forward(src, f, re, im):
            yr = src[:, SLOT_R[f], :]
            odd = f not in (0, 8)
            pe.matmul(re, tab_fwd[:, f, 0, :], yr, start=True, stop=not odd)
            if odd:
                pe.matmul(re, tab_fwd[:, f, 2, :], src[:, SLOT_I[f], :], start=False, stop=True)
            last = pe.matmul(im, tab_fwd[:, f, 1, :], yr, start=True, stop=not odd)
            if odd:
                last = pe.matmul(im, tab_fwd[:, f, 0, :], src[:, SLOT_I[f], :], start=False, stop=True)
            return last

        pe.wait_ge(S("tabs_in"), 32)
        pe.wait_ge(S("kvy_ready"), 1)
        pe.wait_ge(S("mx_free"), 2 * H * UNITS + 2)
        pe.wait_ge(S("csum_ready"), CT)
        for c in range(CT):
            last = pe.matmul(ps[0:1, 3, 0:1], csum[:, c:c + 1], gvec[:, c:c + 1], start=(c == 0), stop=(c == CT - 1))
        last.then_inc(S("fold_ps"), 1)
        for n, f in enumerate(F_ORDER):
            if n == 1:
                pe.wait_ge(S("fold_sb"), 7)
            if n >= 2:
                pe.wait_ge(S("kvf_sb"), 3 * (n - 1))
            b = 2 * (n % 2)
            forward(kvy, f, ps[:, b, :], ps[:, b + 1, :]).then_inc(S("kvf_ps"), 1)
        pe.wait_ge(S("probs_ready"), H * 64 + 2)
        pe.wait_ge(S("attn_ready"), H)
        for n, f in enumerate(F_ORDER):
            pe.wait_ge(S("y1_ready" if f % 2 else "y1_even"), 1)
            if f in (2, 6):
                pe.wait_ge(S("y1_two"), 1)
            if n >= 4:
                pe.wait_ge(S("prod_done"), 2 * (n - 3))
            b = 4 + n % 4
            forward(y1, f, ps[:, b, 0:D], ps[:, b, D:2 * D]).then_inc(S("x1f_ps"), 1)

        pe.wait_ge(S("rj_ready"), 4)
        pe.wait_ge(S("kvf_sb"), 3 * NF)
        for f in range(NF):
            o = ps[:, 0, 2 * f:2 * f + 2]
            pe.matmul(o, tab_inv[:, f, 0, :], rj[:, f, 0:2], start=True, stop=False)
            last = pe.matmul(o, tab_inv[:, f, 1, :], rj[:, f, 2:4], start=False, stop=True)
        last.then_inc(S("u_ps"), 1)
        pe.wait_ge(S("u_sb"), 1)
        pe.transpose(ps[0:18, 1, 0:P], u_sb[:, :], ident[:, :]).then_inc(S("u_ps"), 1)
        pe.wait_ge(S("u_sb"), 2)
        for t in range(16):
            last = pe.matmul(ps[0:1, 2 + t // 4, t % 4 * P:t % 4 * P + P], w16[:, t:t + 1], uT[:, :],
                             start=True, stop=True)
        last.then_inc(S("corr_ps"), 1)
        pe.wait_ge(S("w_ready"), 1)
        pe.wait_ge(S("e16_ready"), 1)
        for t in range(16):
            last = pe.matmul(ps[:, 0, 0:18], w_row[0:1, t * P:(t + 1) * P], e16s[0:1, 18 * t:18 * t + 18],
                             start=(t == 0), stop=(t == 15))
        last.then_inc(S("h_ps"), 1)
        pe.wait_ge(S("h_sb"), 3)
        for f in range(NF):
            o = ps[:, 1, 2 * f:2 * f + 2]
            pe.matmul(o, tab_fwd[:, f, 0, :], hh[:, f, 0:2], start=True, stop=False)
            last = pe.matmul(o, tab_fwd[:, f, 1, :], hh[:, f, 2:4], start=False, stop=True)
        last.then_inc(S("h_ps"), 1)
        pe.wait_ge(S("corr_sb"), 1)
        for n, f in enumerate(F_ORDER):
            pe.wait_ge(S("g_ready"), 2 * (n + 1))
            if n >= 6:
                pe.wait_ge(S("z_sb"), n - 5)
            w = D if f in (0, 8) else 2 * D
            o = ps[:, 2 + n % 6, 0:w]
            if f in (0, 8):
                pe.matmul(o, gtab[:, f, 0, :], spec[:, f, 2, :], start=True, stop=False)
                last = pe.matmul(o, gtab[:, f, 1, :], spec[:, f, 3, :], start=False, stop=True)
            else:
                pe.matmul(o, gtab[:, f, 0, :], spec[:, f, 2:4, :].rearrange("p a c -> p (a c)"), start=True, stop=False)
                last = pe.matmul(o, gtab[:, f, 1, :], spec[:, f, 3:5, :].rearrange("p a c -> p (a c)"),
                                 start=False, stop=True)
            last.then_inc(S("z_ps"), 1)
        pe.wait_ge(S("wffn_ready"), 1)
        pe.wait_ge(S("z_sb"), NF)

        def product(t):
            pe.wait_ge(S("xqT_sb"), t + 1)
            if t >= 4:
                pe.wait_ge(S("y3_made"), t - 3)
            for c in range(CT):
                last = pe.matmul(ps[:, 4 + t % 4, 0:D], xqT[:, t, c * P:(c + 1) * P], wffn[:, c, :],
                                 start=(c == 0), stop=(c == CT - 1))
            last.then_inc(S("ffn_ps"), 1)

        for t in range(NT):
            pe.wait_ge(S("xqb_ready"), t + 1)
            if t >= 4:
                pe.wait_ge(S("xqT_sb"), t - 3)
            for c in range(CT):
                last = pe.transpose(ps[:, t % 4, 64 * c:64 * (c + 1)].bitcast(BF16), xqb[:, t, c * P:(c + 1) * P],
                                    identb[:, :])
            last.then_inc(S("xqT_ps"), 1)
            if t:
                product(t - 1)
        product(NT - 1)

    @block.scalar
    def _(act):
        act.sem_inc(S("probs_ready"), 2)
        act.dma_start(cols[:, :], A["cols"]).then_inc(S("cols_in"), 16)
        act.dma_start(select[:, :], A["tab_select"]).then_inc(S("consts_in"), 16)

        def part(m, n):
            kq, c, r = PIECES[n]
            if m == 0:
                act.wait_ge(S("full_ready"), n + 1)
            elif n < 4:
                act.wait_ge(S("rest_ready"), n + 1)
            else:
                act.wait_ge(S("rest_late"), n - 3)
            act.activation(parts[3 * kq + m][:, c, r], full[kq][:, r], ACT.Copy).then_inc(S(f"part{m + 1}_ready"), 1)

        for m in range(2):
            for n in range(4):
                part(m, n)
        act.wait_ge(S("fold_ps"), 1)
        act.activation(bias_row[0:1, :], ps[0:1, 2, :], ACT.Copy).then_inc(S("fold_sb"), 1)
        for e in range(CT):
            act.activation(ab[:, e, :], ps[:, e, :], ACT.Copy).then_inc(S("fold_sb"), 1)
        act.activation(gvec[:, :], ps[:, 3, 0:2], ACT.Copy).then_inc(S("fold_sb"), 1)
        act.activation(bb[0:1, :], ps[0:1, 3, 4:5], ACT.Copy).then_inc(S("fold_sb"), 1)
        act.wait_ge(S("fold_ps"), 2)
        act.activation(bias_b[:, :], ps[:, 6, :], ACT.Copy).then_inc(S("fold_sb"), 1)
        act.wait_ge(S("consts_in"), 16)
        act.activation(identb[:, :], ident[:, :], ACT.Copy).then_inc(S("consts_in"), 16)
        for t in range(NCT):
            if t in (3, 5):
                part((t - 3) // 2, 4)
                part((t - 3) // 2, 5)
            if t == 9:
                act.wait_ge(S("ctx_in"), 16)
                for c in range(CT):
                    if c:
                        act.wait_ge(S("csum_ready"), c)
                    act.activation(sum_junk[:, :], ctxT[:, c, :], ACT.Copy, accum_out=csum[:, c:c + 1])\
                       .then_inc(S("csum_ready"), 1)
            n = min(P, LC - t * P)
            act.wait_ge(S("kv_ps"), t + 1)
            if t == NCT - 1:
                act.wait_ge(S("kv_zero"), 1)
            act.activation(kv[0:n, t, :], ps[0:n, CTX_BANKS[t % 3], :], ACT.Copy).then_inc(S("kv_sb"), 1)

        def copy_turned(h, bank, sent):
            act.wait_ge(S("mT_ready"), h + 1)
            if sent:
                act.wait_ge(*sent)
            act.activation(mT[:, :], mt_ps[bank][0:3 * NT, :], ACT.Copy).then_inc(S("mT_copied"), 1)

        copy_turned(0, 0, None)
        act.wait_ge(parts_out[1], 96)

        def exps(it, n, r):
            e = it * (RING * UNITS * 4) + 4 * n + r
            if r == 0:
                act.wait_ge(S("quads_done"), it * (RING * UNITS) + n + 1)
            act.wait_ge(S("scores_ready"), e + 1)
            act.activation(probs[4 * (n % 2) + r][:, :], ex_ps[r % 2], ACT.Exp).then_inc(S("probs_ready"), 1)

        def copy_out(h, bank):
            act.wait_ge(S("quads_done"), (h + 1) * UNITS + 2)
            act.activation(o_sb[bank][:, :], o_ps[bank], ACT.Copy).then_inc(S("o_copied"), 1)

        def heads(it, count, last):
            for n in range(count * UNITS):
                hb, j = n // UNITS, n % UNITS
                h = it * RING + hb
                more = not last or n + 1 < count * UNITS
                if more:
                    exps(it, n + 1, 0)
                if j == 14 and (not last or hb + 1 < count):
                    copy_turned(h + 1, (hb + 1) % 2, (m_rows[hb % RING], (it + hb // RING) * 16 + 16))
                if more:
                    exps(it, n + 1, 1)
                if j == UNITS - 1:
                    copy_out(h, hb % 2)
                if more:
                    exps(it, n + 1, 2)
                    exps(it, n + 1, 3)

        for r in range(4):
            exps(0, 0, r)
        with act.Fori(0, LOOPS) as it:
            heads(it, RING, False)
        heads(LOOPS, H - LOOPS * RING, True)

        act.wait_ge(S("fold_ps"), 3)
        act.activation(extra[0:1, :], ps[0:1, 3, 0:1], ACT.Copy).then_inc(S("fold_sb"), 1)
        for n, f in enumerate(F_ORDER):
            act.wait_ge(S("kvf_ps"), n + 1)
            b = 2 * (n % 2)
            for m in range(2):
                act.activation(spec[:, f, m:m + 3:2, :], ps[:, b + m, :].rearrange("p (a c) -> p a c", a=2), ACT.Copy)\
                   .then_inc(S("kvf_sb"), 1)
            act.activation(spec[:, f, 4, :], ps[:, b, D:2 * D], ACT.Copy, scale=-1.0).then_inc(S("kvf_sb"), 1)
        act.wait_ge(S("u_ps"), 1)
        act.activation(u_sb[:, :], ps[:, 0, 0:18], ACT.Copy).then_inc(S("u_sb"), 1)
        act.wait_ge(S("u_ps"), 2)
        act.activation(uT[:, :], ps[0:18, 1, 0:P], ACT.Copy).then_inc(S("u_sb"), 1)
        act.wait_ge(S("corr_ps"), 1)
        act.activation(c_row[0:1, :], ps[0:1, 2:6, :], ACT.Copy).then_inc(S("corr_sb"), 1)
        act.wait_ge(S("nmax_ready"), 1)
        act.activation(e_row[0:1, :], c_row[0:1, :], ACT.Exp, bias=nmax[0:1, :]).then_inc(S("e_ready"), 1)
        act.wait_ge(S("hf_sb"), 2)
        for n, f in enumerate(F_ORDER):
            if n >= 2:
                act.wait_ge(S("g_ready"), 2 * (n - 1))
            act.activation(gtmp[:, n % 2, :, :], tab_inv[:, f, :, :], ACT.Copy, scale=hf[:, f, 0:1])\
               .then_inc(S("g_tmp"), 1)
        for n, f in enumerate(F_ORDER):
            act.wait_ge(S("z_ps"), n + 1)
            w = 1 if f in (0, 8) else 2
            act.activation(z[:, f, 0:w, :], ps[:, 2 + n % 6, 0:w * D].rearrange("p (a c) -> p a c", a=w), ACT.Copy)\
               .then_inc(S("z_sb"), 1)
        def copy_xqT(t):
            act.wait_ge(S("xqT_ps"), t + 1)
            act.activation(xqT[:, t, :], ps[:, t % 4, 0:P].bitcast(BF16), ACT.Copy).then_inc(S("xqT_sb"), 1)

        for t in range(NT):
            act.wait_ge(S("xinv_ready"), t // 4 + 1)
            if t >= 4:
                act.wait_ge(S("xqc_ready"), t - 3)
            act.activation(xq[:, t % 4, :], x2[:, t, :], ACT.Copy, bias=ROUND, scale=xinv[:, t:t + 1])\
               .then_inc(S("xq_ready"), 1)
            if t >= 2:
                copy_xqT(t - 2)
        copy_xqT(NT - 2)
        copy_xqT(NT - 1)

    @block.gpsimd
    def _(pool):
        chain = [0]

        def link(ins):
            chain[0] += 1
            ins.then_inc(S("pool_chain"), 1)
            pool.wait_ge(S("pool_chain"), chain[0])

        def tt(o, a, b, op):
            return pool.tensor_tensor(o, a, b, op)

        def scaled(o, a, by):
            return pool.tensor_scalar(o, a, by, None, ALU.mult)

        pool.memset(ones_row[:, :], 1.0).then_inc(S("ones_set"), 1)
        pool.memset(kv[:, NCT - 1:NT, :], 0.0).then_inc(S("kv_zero"), 1)
        for n in (0, 2):
            r = PIECES[n][2]
            pool.wait_ge(S("part2_ready"), n + 1)
            tt(parts[2][:, 0, r], full[0][:, r], parts[1][:, 0, r], ALU.subtract).then_inc(S("part3_q"), 1)
        pool.wait_ge(S("part3_q"), 2)
        link(pool.memset(k_ring[2][ROWS:KROWS, :], 1.0))
        pool.sem_inc(S("k_ones"), 1)
        pool.wait_ge(S("full_ready"), 6)
        for b in range(RING):
            pool.memset(v_ring[b][:, :, 16:17], 1.0)
            pool.memset(v_ring[b][:, :, 17:32], 0.0).then_inc(S("v_set"), 1)
        for n in (4, 5):
            kq, c, r = PIECES[n]
            pool.wait_ge(S("part1_ready"), n + 1)
            tt(full[kq][:, r], full[kq][:, r], parts[3 * kq][:, c, r], ALU.subtract).then_inc(S("rest_late"), 1)
        for n in (4, 5):
            kq, c, r = PIECES[n]
            pool.wait_ge(S("rest_late"), n - 3)
            pool.wait_ge(S("part2_ready"), n + 1)
            tt(parts[3 * kq + 2][:, c, r], full[kq][:, r], parts[3 * kq + 1][:, c, r], ALU.subtract)\
                .then_inc(S("part3_late"), 1)
        pool.wait_ge(S("x_in"), 64)

        def take_values(h):
            if h >= RING:
                pool.wait_ge(S("quads_done"), (h - RING + 1) * UNITS + 2)
            pool.tensor_copy(v_ring[h % RING][:, :, 0:DH], x_sb[:, :, h * DH:(h + 1) * DH]).then_inc(S("v_ready"), 1)

        def residual(h):
            pool.wait_ge(S("attn_ready"), h + 1)
            tt(y_sb[:, :, h * DH:(h + 1) * DH], attn[h % RING][:, :, :], x_sb[:, :, h * DH:(h + 1) * DH], ALU.add)\
                .then_inc(S("attn_used"), 1)

        def even_side(x, y, s):
            link(tt(s[:, 0:4, :], y[:, 0:4, :], y[:, 4:8, :], ALU.add))
            link(tt(s[:, 4:8, :], y[:, 0:4, :], y[:, 4:8, :], ALU.subtract))
            link(tt(s[:, 8:10, :], s[:, 0:2, :], s[:, 2:4, :], ALU.add))
            link(tt(y[:, 2:4, :], s[:, 0:2, :], s[:, 2:4, :], ALU.subtract))
            link(tt(y[:, 0, :], s[:, 8, :], s[:, 9, :], ALU.add))
            link(tt(y[:, 1, :], s[:, 8, :], s[:, 9, :], ALU.subtract))
            link(tt(s[:, 8, :], s[:, 5, :], s[:, 7, :], ALU.subtract))
            link(tt(s[:, 9, :], s[:, 5, :], s[:, 7, :], ALU.add))

        def kv_dft():
            x, y, s = kv, kvy, kv
            for c in range(CT):
                pool.wait_ge(parts_out[c], 96)
            link(tt(y[:, 0:8, :], x[:, 0:8, :], x[:, 8:16, :], ALU.add))
            yield
            link(tt(y[:, 8:16, :], x[:, 0:8, :], x[:, 8:16, :], ALU.subtract))
            yield
            even_side(x, y, s)
            link(scaled(s[:, 8:10, :], s[:, 8:10, :], R2))
            link(tt(y[:, 4, :], s[:, 4, :], s[:, 8, :], ALU.add))
            link(tt(y[:, 5, :], s[:, 4, :], s[:, 8, :], ALU.subtract))
            link(tt(y[:, 6, :], s[:, 9, :], s[:, 6, :], ALU.add))
            link(tt(y[:, 7, :], s[:, 9, :], s[:, 6, :], ALU.subtract))
            yield
            for t in range(3):
                link(tt(s[:, t, :], y[:, 9 + t, :], y[:, 15 - t, :], ALU.subtract))
                link(tt(s[:, 3 + t, :], y[:, 9 + t, :], y[:, 15 - t, :], ALU.add))
            link(pool.tensor_copy(s[:, 14, :], y[:, 8, :]))
            link(pool.tensor_copy(s[:, 15, :], y[:, 12, :]))
            yield
            for side, b0, p in ((0, 14, 0), (1, 15, 3)):
                link(scaled(s[:, 6, :], s[:, p + 1, :], R2))
                link(tt(s[:, 7, :], s[:, b0, :], s[:, 6, :], ALU.add))
                if side == 0:
                    link(tt(s[:, 8, :], s[:, b0, :], s[:, 6, :], ALU.subtract))
                else:
                    link(tt(s[:, 8, :], s[:, 6, :], s[:, b0, :], ALU.subtract))
                ca, cb = (C1, S1) if side == 0 else (S1, C1)
                link(scaled(s[:, 9, :], s[:, p, :], ca))
                link(scaled(s[:, 10, :], s[:, p + 2, :], cb))
                link(tt(s[:, 9, :], s[:, 9, :], s[:, 10, :], ALU.add))
                link(scaled(s[:, 10, :], s[:, p, :], cb))
                link(scaled(s[:, 11, :], s[:, p + 2, :], ca))
                link(tt(s[:, 10, :], s[:, 10, :], s[:, 11, :], ALU.subtract))
                o = 8 + 4 * side
                link(tt(y[:, o, :], s[:, 7, :], s[:, 9, :], ALU.add))
                link(tt(y[:, o + 2, :], s[:, 8, :], s[:, 10, :], ALU.add))
                if side == 0:
                    link(tt(y[:, o + 1, :], s[:, 7, :], s[:, 9, :], ALU.subtract))
                    link(tt(y[:, o + 3, :], s[:, 8, :], s[:, 10, :], ALU.subtract))
                else:
                    link(tt(y[:, o + 1, :], s[:, 9, :], s[:, 7, :], ALU.subtract))
                    link(tt(y[:, o + 3, :], s[:, 10, :], s[:, 8, :], ALU.subtract))
                yield
            pool.memset(expo[:, :], -0.5).then_inc(S("kvy_ready"), 1)

        for h in range(RING):
            take_values(h)
        pool.wait_ge(S("v_ready"), RING)
        link(pool.memset(k_ring[3][ROWS:KROWS, :], 1.0))
        pool.sem_inc(S("k_ones"), 1)
        pool.wait_ge(S("kv_sb"), NCT)
        for t in range(NCT):
            n = min(P, LC - t * P)
            ins = tt(kv[0:n, t, :], kv[0:n, t, :], bias_b[0:n, :], ALU.add)
        link(ins)
        pool.sem_inc(S("attn_used"), RING)
        work = kv_dft()
        for h in range(H):
            next(work, None)
            residual(h)
            if h + RING < H:
                take_values(h + RING)
        for _ in work:
            pass

        def inverse_roots(lo, n, which, name):
            pool.wait_ge(S(name), which)
            link(pool.tensor_scalar(rstd[:, lo:lo + n], mv[:, lo:lo + n, 1], EPS, None, ALU.add))
            tt(rstd[:, lo:lo + n], rstd[:, lo:lo + n], expo[:, lo:lo + n], ALU.pow).then_inc(S(name + "_root"), 1)

        inverse_roots(0, NT, 1, "var1")
        pool.wait_ge(S("y1_sum"), 1)
        s, y = scr1, y1
        even_side(x1, y, s)
        pool.sem_inc(S("y1_even"), 1)
        pool.wait_ge(S("late_in"), 16 * 7)
        pool.wait_ge(S("y1_diff"), 1)
        tt(x1[:, :, :], x1[:, :, :], bo_b[:, :].unsqueeze(1).broadcast_to([P, NT, D]), ALU.add).then_inc(S("x1b_ready"), 1)
        pool.wait_ge(S("z_sb"), NF)
        Z = lambda f: z[:, f, 1, :]
        t_ = lambda n: zs[:, 16 + n, :]
        F1, F2, A1, A2, B1, B2, T1, T2, T3 = (t_(n) for n in (7, 8, 9, 10, 11, 12, 13, 6, 5))
        O = {1: t_(0), 2: t_(1), 3: t_(2), 4: t_(3), 5: t_(4), 6: t_(6), 7: t_(5)}
        link(tt(F1, Z(2), Z(6), ALU.add))
        link(tt(F2, Z(2), Z(6), ALU.subtract))
        link(tt(A1, Z(1), Z(7), ALU.add))
        link(tt(A2, Z(1), Z(7), ALU.subtract))
        link(tt(B1, Z(3), Z(5), ALU.add))
        link(tt(B2, Z(3), Z(5), ALU.subtract))
        link(scaled(F1, F1, R2))
        link(tt(O[4], A2, B2, ALU.subtract))
        link(tt(A2, A2, B2, ALU.add))
        link(scaled(A2, A2, R2))
        link(tt(O[2], A2, F2, ALU.add))
        link(tt(O[6], A2, F2, ALU.subtract))
        link(scaled(A2, A1, S1))
        link(scaled(B2, B1, C1))
        link(tt(A2, A2, B2, ALU.add))
        link(scaled(A1, A1, C1))
        link(scaled(B1, B1, S1))
        link(tt(A1, A1, B1, ALU.subtract))
        link(tt(F2, F1, Z(4), ALU.add))
        link(tt(F1, F1, Z(4), ALU.subtract))
        link(tt(O[1], A2, F2, ALU.add))
        link(tt(O[7], A2, F2, ALU.subtract))
        link(tt(O[3], A1, F1, ALU.add))
        link(tt(O[5], A1, F1, ALU.subtract))
        pool.sem_inc(S("osum_ready"), 1)

        for n in range(4):
            inverse_roots(4 * n, 4, n + 1, "var2")
        for n in range(NT):
            pool.wait_ge(S("x2_ready"), n + 1)
            if n == 0:
                pool.wait_ge(S("z_ps"), NF)
            tt(x2b[:, n, :], x2[:, n, :], fb_b[:, :], ALU.add).then_inc(S("x2b_ready"), 1)
        for n in range(4):
            inverse_roots(4 * n, 4, n + 1, "var3")

    @block.vector
    def _(dve):
        chain = [0]

        def link(ins):
            chain[0] += 1
            ins.then_inc(S("dve_chain"), 1)
            dve.wait_ge(S("dve_chain"), chain[0])

        dve.sem_inc(S("mx_free"), 2)
        dve.memset(msplit[:, 3:8, :], 0.0)
        for b in range(2):
            dve.memset(k_ring[b][ROWS:KROWS, :], 1.0).then_inc(S("k_ones"), 1)
        dve.wait_ge(S("cols_in"), 16)

        def full_piece(n):
            kq, c, r = PIECES[n]
            if kq:
                ins = dve.tensor_scalar(full[1][:, r], xT[:, c, r], entc[:, c:c + 1], None, ALU.mult)
            else:
                dve.wait_ge(S(f"xT_in{n // 2}"), 16)
                ins = dve.tensor_scalar(full[0][:, r], xT[:, c, r], rotc[:, c:c + 1], float(DH) ** -0.5, ALU.mult, ALU.mult)
            ins.then_inc(S("full_ready"), 1)

        for n in range(4):
            full_piece(n)
        for n in range(4):
            kq, _, r = PIECES[n]
            dve.wait_ge(S("part1_ready"), n + 1)
            dve.wait_ge(S("full_ready"), n + 1)
            dve.tensor_tensor(full[kq][:, r], full[kq][:, r], parts[3 * kq][:, 0, r], ALU.subtract)\
               .then_inc(S("rest_ready"), 1)
        for n in (1, 3):
            r = PIECES[n][2]
            dve.wait_ge(S("part2_ready"), n + 1)
            dve.wait_ge(S("rest_ready"), n + 1)
            dve.tensor_tensor(parts[5][:, 0, r], full[1][:, r], parts[4][:, 0, r], ALU.subtract).then_inc(S("part3_k"), 1)

        def reduce_max(half, tile, use):
            dve.wait_ge(S("mx_ready"), use + 1)
            dve.tensor_reduce(mx[:, tile, half:half + 1], mx_ps[half], AX.XY, ALU.max).then_inc(S("mx_free"), 1)

        def split(h, first=False):
            def then(ins, n):
                ins.then_inc(S("split_chain"), 1)
                dve.wait_ge(S("split_chain"), h * 4 + n)
            dve.wait_ge(S("mx_free"), (h + 1) * (2 * UNITS) + 2)
            then(dve.tensor_reduce(negm[:, :], mx[:, :, :], AX.X, ALU.max, negate=True), 1)
            if not first:
                dve.wait_ge(S("mT_ready"), h)
            then(dve.tensor_copy(msplit[:, 0, :], negm[:, :]), 2)
            then(dve.tensor_tensor(mrest[:, :], negm[:, :], msplit[:, 0, :], ALU.subtract), 3)
            then(dve.tensor_copy(msplit[:, 1, :], mrest[:, :]), 4)
            dve.tensor_tensor(msplit[:, 2, :], mrest[:, :], msplit[:, 1, :], ALU.subtract).then_inc(S("split_ready"), 1)

        def normalise(b, h, bank):
            dve.wait_ge(S("outt_ready"), h + 1)
            dve.reciprocal(recip[:, bank, :, :], out_t[bank][:, :, :, 16]).then_inc(S("recip_ready"), 1)
            dve.wait_ge(S("recip_ready"), h + 1)
            dve.wait_ge(S("attn_used"), h + 1)
            dve.tensor_tensor(attn[b][:, :, :].rearrange("p (c s) d -> p s c d", s=4), out_t[bank][:, :, :, 0:DH],
                              recip[:, bank, :, :].unsqueeze(3).broadcast_to([P, 4, 4, DH]), ALU.mult)\
               .then_inc(S("attn_ready"), 1)

        for g in range(AHEAD):
            if g == 3:
                dve.wait_ge(S("part3_k"), 2)
                dve.wait_ge(S("part3_q"), 2)
                full_piece(4)
                full_piece(5)
            for half in range(2):
                reduce_max(half, g % UNITS, 2 * g + half)
            if g == UNITS - 1:
                split(0, True)

        def heads(it, count, last):
            for n in range(count * UNITS):
                g = n + AHEAD
                if not last or g < count * UNITS:
                    for half in range(2):
                        reduce_max(half, g % UNITS, (it * (RING * UNITS) + g) * 2 + half)
                    if g % UNITS == UNITS - 1:
                        split(it * RING + g // UNITS)
                if n % UNITS == UNITS - 1:
                    hb = n // UNITS
                    normalise(hb % RING, it * RING + hb, hb % 2)

        with dve.Fori(0, LOOPS) as it:
            heads(it, RING, False)
        heads(LOOPS, H - LOOPS * RING, True)

        def moments(src, lo, n, name):
            for t in range(lo, lo + n):
                last = dve.bn_stats(stats[:, t, :], src[:, t, :])
            link(last)
            for t in range(lo, lo + n):
                last = dve.bn_aggr(mv[:, t, :], stats[:, t, :])
            last.then_inc(S(name), 1)

        def norm(dst, src, t):
            return dve.tensor_scalar(dst[:, t, :], src[:, t, :], mv[:, t, 0:1], rstd[:, t:t + 1],
                                     ALU.subtract, ALU.mult)

        dve.wait_ge(S("attn_used"), H + RING)
        moments(y_sb, 0, NT, "var1")
        dve.wait_ge(S("var1_root"), 1)
        for t in range(NT):
            last = norm(x1, y_sb, t)
        link(last)
        y, s = y1, scr1
        dve.tensor_tensor(y[:, 0:8, :], x1[:, 0:8, :], x1[:, 8:16, :], ALU.add).then_inc(S("y1_sum"), 1)
        dve.tensor_tensor(y[:, 8:16, :], x1[:, 0:8, :], x1[:, 8:16, :], ALU.subtract).then_inc(S("y1_diff"), 1)
        dve.wait_ge(S("y1_diff"), 1)
        for t in range(3):
            dve.tensor_tensor(s[:, 10 + t, :], y[:, 9 + t, :], y[:, 15 - t, :], ALU.subtract)
            last = dve.tensor_tensor(s[:, 13 + t, :], y[:, 9 + t, :], y[:, 15 - t, :], ALU.add)
        link(last)

        def stt(o, a, by, b, op):
            return dve.scalar_tensor_tensor(o, a, by, b, ALU.mult, op)

        g0 = junk[:, 0, :]
        g1 = junk[:, 1, :]
        v0, v1, v2, v3 = (c_big[:, n, :] for n in range(4))
        for side in range(2):
            b0, p = y[:, 8 + 4 * side, :], 10 + 3 * side
            ca, cb = (C1, S1) if side == 0 else (S1, C1)
            stt(v0, s[:, p + 1, :], R2, b0, ALU.add)
            if side == 0:
                stt(v1, s[:, p + 1, :], -R2, b0, ALU.add)
            else:
                stt(v1, s[:, p + 1, :], R2, b0, ALU.subtract)
            dve.tensor_scalar(g0, s[:, p + 2, :], cb, None, ALU.mult)
            link(dve.tensor_scalar(g1, s[:, p + 2, :], ca, None, ALU.mult))
            stt(v2, s[:, p, :], ca, g0, ALU.add)
            link(stt(v3, s[:, p, :], cb, g1, ALU.subtract))
            if side == 0:
                b4 = y[:, 12, :]
            o = 8 + 4 * side
            dve.tensor_tensor(y[:, o, :], v0, v2, ALU.add)
            dve.tensor_tensor(y[:, o + 2, :], v1, v3, ALU.add)
            if side == 0:
                dve.tensor_tensor(y[:, o + 1, :], v0, v2, ALU.subtract)
                last = dve.tensor_tensor(y[:, o + 3, :], v1, v3, ALU.subtract)
            else:
                dve.tensor_tensor(y[:, o + 1, :], v2, v0, ALU.subtract)
                last = dve.tensor_tensor(y[:, o + 3, :], v3, v1, ALU.subtract)
            link(last)
        dve.wait_ge(S("y1_even"), 1)
        stt(y[:, 4, :], s[:, 8, :], R2, s[:, 4, :], ALU.add)
        stt(y[:, 5, :], s[:, 8, :], -R2, s[:, 4, :], ALU.add)
        stt(y[:, 6, :], s[:, 9, :], R2, s[:, 6, :], ALU.add)
        stt(y[:, 7, :], s[:, 9, :], R2, s[:, 6, :], ALU.subtract).then_inc(S("y1_two"), 1)
        dve.sem_inc(S("y1_ready"), 1)
        for n, f in enumerate(F_ORDER):
            dve.wait_ge(S("x1f_ps"), n + 1)
            dve.wait_ge(S("kvf_sb"), 3 * (n + 1))
            b = 4 + n % 4
            for m in range(2):
                if n:
                    dve.wait_ge(S("prod_done"), 2 * n - 1 + m)
                dve.tensor_tensor_reduce(out=junk[:, m, :], in0=ps[:, b, m * D:(m + 1) * D], in1=spec[:, f, m, :],
                                         scale=1.0, scalar=0.0, op0=ALU.mult, op1=ALU.add,
                                         accum_out=ri[:, f, m:m + 1]).then_inc(S("prod_done"), 1)
        dve.wait_ge(S("prod_done"), 2 * NF)
        dve.wait_ge(S("fold_sb"), 7)
        link(dve.scalar_tensor_tensor(extra[:, :], bb[:, :], float(LC), extra[:, :], ALU.mult, ALU.add))
        link(dve.scalar_tensor_tensor(ri[0:1, 0, 0:1], extra[:, :], float(L), ri[0:1, 0, 0:1], ALU.mult, ALU.add))
        dve.wait_ge(S("late_in"), 16 * 7)
        dve.tensor_copy(rj[:, :, 0], ri[:, :, 0]).then_inc(S("rj_ready"), 1)
        dve.tensor_scalar(rj[:, :, 1], ri[:, :, 1], sign[:, 1:2], None, ALU.mult).then_inc(S("rj_ready"), 1)
        dve.tensor_scalar(rj[:, :, 2], ri[:, :, 1], sign[:, 0:1], None, ALU.mult).then_inc(S("rj_ready"), 1)
        dve.tensor_copy(rj[:, :, 3], ri[:, :, 0]).then_inc(S("rj_ready"), 1)
        dve.tensor_copy(wffn[:, :, :], wffn_words[:, :, 0:2 * D:2]).then_inc(S("wffn_ready"), 1)
        dve.wait_ge(S("corr_sb"), 1)
        link(dve.max(top[:, 0:8], c_row[:, :]))
        dve.tensor_scalar(nmax[:, :], top[:, 0:1], -1.0, None, ALU.mult).then_inc(S("nmax_ready"), 1)
        link(dve.match_replace(c2_row[:, :], top[:, 0:8], c_row[:, :], NEG))
        link(dve.max(top[:, 8:16], c2_row[:, :]))
        link(dve.memset(top[:, TOPK:16], NEG))
        link(dve.match_replace(w_row[:, :], top[:, 8:16], c2_row[:, :], NEG))
        dve.wait_ge(S("e_ready"), 1)
        dve.scalar_tensor_tensor(w_row[:, :], w_row[:, :], NEG, e_row[:, :], ALU.is_equal, ALU.mult,
                                 accum_out=wsum[:, :]).then_inc(S("w_ready"), 1)
        dve.wait_ge(S("w_ready"), 1)
        link(dve.reciprocal(wrec[:, :], wsum[:, :]))
        dve.tensor_scalar(e16s[:, :], e16[:, :], wrec[:, :], None, ALU.mult).then_inc(S("e16_ready"), 1)
        hp = ps[:, 0, 0:18].rearrange("p (f m) -> p f m", m=2)
        dve.wait_ge(S("h_ps"), 1)
        dve.tensor_copy(hh[:, :, 0:2], hp).then_inc(S("h_sb"), 1)
        dve.tensor_scalar(hh[:, :, 2], hp[:, :, 1], -1.0, None, ALU.mult).then_inc(S("h_sb"), 1)
        dve.tensor_copy(hh[:, :, 3], hp[:, :, 0]).then_inc(S("h_sb"), 1)
        hp2 = ps[:, 1, 0:18].rearrange("p (f m) -> p f m", m=2)
        dve.wait_ge(S("h_ps"), 2)
        dve.tensor_copy(hf[:, :, 0:2], hp2).then_inc(S("hf_sb"), 1)
        dve.tensor_scalar(hf[:, :, 2], hp2[:, :, 1], -1.0, None, ALU.mult).then_inc(S("hf_sb"), 1)
        dve.wait_ge(S("hf_sb"), 2)
        for n, f in enumerate(F_ORDER):
            dve.wait_ge(S("g_tmp"), n + 1)
            stt(gtab[:, f, 0, :], tab_inv[:, f, 1, :], hf[:, f, 2:3], gtmp[:, n % 2, 0, :], ALU.add).then_inc(S("g_ready"), 1)
            stt(gtab[:, f, 1, :], tab_inv[:, f, 0, :], hf[:, f, 1:2], gtmp[:, n % 2, 1, :], ALU.add).then_inc(S("g_ready"), 1)
        R = lambda f: z[:, f, 0, :]
        tt = lambda o, a, b, op: dve.tensor_tensor(o, a, b, op)
        E = [zs[:, n, :] for n in range(9)]
        A1, A2, B1, B2, P1, P2, Q1 = (zs[:, 9 + n, :] for n in range(7))
        Q2 = g0
        dve.wait_ge(S("z_sb"), NF)
        tt(A1, R(0), R(8), ALU.add)
        tt(A2, R(0), R(8), ALU.subtract)
        tt(B1, R(2), R(6), ALU.add)
        tt(B2, R(2), R(6), ALU.subtract)
        tt(P1, R(1), R(7), ALU.add)
        tt(P2, R(1), R(7), ALU.subtract)
        tt(Q1, R(3), R(5), ALU.add)
        link(tt(Q2, R(3), R(5), ALU.subtract))
        tt(g1, A1, R(4), ALU.add)
        tt(E[2], A1, R(4), ALU.subtract)
        stt(E[1], B2, R2, A2, ALU.add)
        stt(E[3], B2, -R2, A2, ALU.add)
        tt(v0, P1, Q1, ALU.subtract)
        link(tt(v1, P1, Q1, ALU.add))
        tt(E[0], g1, B1, ALU.add)
        tt(E[4], g1, B1, ALU.subtract)
        dve.tensor_scalar(v2, Q2, S1, None, ALU.mult)
        link(dve.tensor_scalar(v3, Q2, C1, None, ALU.mult))
        stt(A1, P2, C1, v2, ALU.add)
        stt(A2, P2, S1, v3, ALU.subtract)
        stt(E[6], v0, -R2, E[2], ALU.add)
        link(tt(E[8], E[0], v1, ALU.subtract))
        stt(E[2], v0, R2, E[2], ALU.add)
        tt(E[0], E[0], v1, ALU.add)
        tt(E[7], E[1], A1, ALU.subtract)
        link(tt(E[5], E[3], A2, ALU.subtract))
        tt(E[1], E[1], A1, ALU.add)
        link(tt(E[3], E[3], A2, ALU.add))
        dve.wait_ge(S("x1b_ready"), 1)
        dve.wait_ge(S("osum_ready"), 1)
        osl = {1: 16, 2: 17, 3: 18, 4: 19, 5: 20, 6: 22, 7: 21}
        tt(x2[:, 0, :], E[0], x1[:, 0, :], ALU.add)
        tt(x2[:, 8, :], E[8], x1[:, 8, :], ALU.add)
        for t in range(1, 8):
            tt(x2[:, t, :], E[t], zs[:, osl[t], :], ALU.add)
            last = tt(x2[:, 16 - t, :], E[t], zs[:, osl[t], :], ALU.subtract)
        link(last)
        tt(x2[:, 1:8, :], x2[:, 1:8, :], x1[:, 1:8, :], ALU.add)
        link(tt(x2[:, 9:16, :], x2[:, 9:16, :], x1[:, 9:16, :], ALU.add))
        moments(x2, 0, 4, "var2")
        for n in range(4):
            if n < 3:
                moments(x2, 4 * n + 4, 4, "var2")
            dve.wait_ge(S("var2_root"), n + 1)
            for t in range(4 * n, 4 * n + 4):
                norm(x2, x2, t).then_inc(S("x2_ready"), 1)
            for t in range(4 * n, 4 * n + 4):
                dve.wait_ge(S("x2_ready"), t + 1)
                last = dve.tensor_reduce(amax[:, t:t + 1], x2[:, t, :], AX.X, ALU.max, apply_absolute_value=True)
            link(last)
            g = slice(4 * n, 4 * n + 4)
            link(dve.tensor_scalar(xscale[:, g], amax[:, g], 1e-6, 1.0 / 127.0, ALU.max, ALU.mult))
            dve.reciprocal(xinv[:, g], xscale[:, g]).then_inc(S("xinv_ready"), 1)
        dve.wait_ge(S("xinv_ready"), 4)

        def clip(t):
            dve.wait_ge(S("xq_ready"), t + 1)
            dve.tensor_scalar(xqc[:, t % 4, :], xq[:, t % 4, :], ROUND - 128.0, ROUND + 127.0, ALU.max, ALU.min)\
               .then_inc(S("xqc_ready"), 1)
            dve.wait_ge(S("xqc_ready"), t + 1)
            dve.tensor_scalar(xqb[:, t, :], xqc[:, t % 4, :], -ROUND, None, ALU.add).then_inc(S("xqb_ready"), 1)

        def scale(t):
            dve.wait_ge(S("ffn_ps"), t + 1)
            dve.scalar_tensor_tensor(y3[:, t, :], ps[:, 4 + t % 4, 0:D], xscale[:, t:t + 1], ws_b[:, :],
                                     ALU.mult, ALU.mult).then_inc(S("y3_made"), 1)
            dve.wait_ge(S("y3_made"), t + 1)
            dve.wait_ge(S("x2b_ready"), t + 1)
            return dve.tensor_tensor(y3[:, t, :], y3[:, t, :], x2b[:, t, :], ALU.add)

        for t in range(NT):
            clip(t)
            if t >= 4:
                link(scale(t - 4))
        for t in range(NT - 4, NT):
            link(scale(t))
        for n in range(4):
            moments(y3, 4 * n, 4, "var3")
        for n in range(4):
            dve.wait_ge(S("var3_root"), n + 1)
            for t in range(4 * n, 4 * n + 4):
                norm(x3, y3, t).then_inc(S("x3_ready"), 1)


def kernel(**inputs):
    import concourse.bacc as bacc
    from concourse.bass_utils import run_bass_kernel_spmd

    a = {k: np.asarray(v) for k, v in inputs.items()}

    def cols(v):
        return np.ascontiguousarray(v.reshape(CT, P).T)

    def rows_of(v):
        return np.ascontiguousarray(np.broadcast_to(v[None, :], (P, v.shape[0])))

    arrays = {
        "x": a["x"][0], "xT": a["x"][0].T, "ctxT": a["ctx_1024"][0].T,
        "cols": np.concatenate([cols(a[n].reshape(-1)) for n in (
            "L0_attn_rotation_params", "L0_attn_entangle_params", "L0_xattn_bq", "L0_xattn_bk", "L0_xattn_bv")], 1),
        "weights": np.concatenate([a["L0_xattn_Wk"].T, a["L0_xattn_Wq"].T, a["L0_xattn_Wv"].T, a["L0_xattn_Wo"]], 0),
        "bo_b": rows_of(a["L0_xattn_bo"]), "ws_b": rows_of(a["L0_ffn_weight_scale"]), "fb_b": rows_of(a["L0_ffn_bias"]),
        "wffnT": a["L0_ffn_weight_q"].T.astype(np.int64),
        **tables(),
    }
    arrays = {k: np.ascontiguousarray(v) for k, v in arrays.items()}
    nc = bacc.Bacc("TRN2", target_bir_lowering=False, num_devices=1)
    handles = {k: nc.dram_tensor(k, v.shape, mybir.dt.from_np(v.dtype), kind="ExternalInput").ap()
               for k, v in arrays.items()}
    result = nc.dram_tensor("layer_out", [L, D], F32, kind="ExternalOutput").ap()
    decoder_layer(nc, handles, result)
    r = run_bass_kernel_spmd(nc, [arrays], core_ids=[0])
    return r.results[0]["layer_out"].reshape(1, L, D)
```

```python
from contextlib import ExitStack
import math

import numpy as np

import concourse.bass as bass
from concourse import mybir

P = 128
F32 = mybir.dt.float32
BF16 = mybir.dt.bfloat16
I8 = mybir.dt.int8
ALU = mybir.AluOpType
ACT = mybir.ActivationFunctionType
AX = mybir.AxisListType

L, D, H, DH = 2048, 256, 16, 16
NT = L // P
LC = 1601
NCT = (LC + P - 1) // P
CT = D // P
ROWS = 6 * DH
KROWS = ROWS + 3
RING = 4
LOOPS = 3
UNITS = 16
AHEAD = 20
CHUNK = 512
NF = 9
EPS = 1e-5
TOPK = int(2 * math.log(L))
NEG = -3.0e38
ROUND = 1.5 * 2.0 ** 23
C1, S1, R2 = math.cos(math.pi / 8), math.sin(math.pi / 8), math.sqrt(0.5)
K_PARTS = [(0, 3, 0), (48, 2, 0), (80, 1, 0)]
Q_PARTS = [(0, 1, 0), (16, 1, 0), (32, 1, 0), (48, 1, 1), (64, 1, 1), (80, 1, 2)]
LOADS = len(K_PARTS) + len(Q_PARTS)
LATE_LOADS = 7


def tables():
    f1 = np.arange(NF)
    a, b = np.arange(P), np.arange(P)
    ang = 2 * np.pi * ((a[:, None, None] * (f1[None, :, None] + 16 * b[None, None, :])) % L) / L
    c, s = np.cos(ang), np.sin(ang)
    t1 = np.stack([c, s, -s], axis=2)
    t2 = np.stack([c.transpose(2, 1, 0), s.transpose(2, 1, 0)], axis=2)
    wt = np.where((f1 == 0) | (f1 == 8), 1.0, 2.0)
    ang16 = 2 * np.pi * ((f1[:, None] * np.arange(16)[None, :]) % 16) / 16
    w16 = np.stack([np.cos(ang16), -np.sin(ang16)], 1) * wt[:, None, None] / (L * D)
    e16 = np.stack([np.cos(ang16), np.sin(ang16)], 1) * wt[:, None, None] / L
    sgn = np.where(a < 64, 1.0, -1.0)
    sel = np.zeros((P, 68))
    for g in range(4):
        sel[32 * g + np.arange(17), 17 * g + np.arange(17)] = 1
    f = np.float32
    return {
        "tab_fwd": t1.astype(f), "tab_inv": t2.astype(f),
        "tab_w16": np.ascontiguousarray(w16.reshape(18, 16)).astype(f),
        "tab_e16": np.ascontiguousarray(e16.transpose(2, 0, 1).reshape(16, 18)).astype(f),
        "tab_sign": np.stack([sgn, -sgn], 1).astype(f),
        "tab_select": np.concatenate([np.eye(P), sel], 1).astype(f),
    }


def decoder_layer(nc, A, out):
    ctx = ExitStack()
    base = (nc.sbuf_base + 31) // 32 * 32
    KB = 1024
    names = [0]

    def sb(off, shape, dt=F32):
        names[0] += 1
        return nc.alloc_sbuf_tensor_at(f"t{names[0]}", shape, dt, offset=base + off)

    O_X, O_Y, O_KV, O_KQ = 0, 16 * KB, 32 * KB, 64 * KB
    O_SP, O_P, O_OSB, O_V = 88 * KB, 120 * KB, 136 * KB, 140 * KB
    O_T1, O_T2, O_FR, O_S = 146 * KB, 160 * KB, 170 * KB, 186 * KB

    class Region:
        def __init__(self, at, end):
            self.at, self.end = at, end

        def __call__(self, shape, dt=F32):
            size = int(np.prod(shape[1:])) * {F32: 4, BF16: 2, I8: 1}[dt]
            t = sb(self.at, shape, dt)
            self.at += (size + 31) // 32 * 32
            assert self.at <= self.end, (self.at, self.end)
            return t

    xT = sb(O_Y, [P, CT, L])
    parts = [sb(O_SP + 8 * KB * n, [P, CT, L], BF16) for n in range(6)]
    full = [sb(O_FR + 8 * KB * n, [P, L]) for n in range(2)]
    ctxT = sb(O_T1, [P, CT, LC])
    weights = sb(O_T2, [P, 4 * CT, D])
    wkT, wqT, wvT, wo = (weights[:, CT * n:CT * n + CT, :] for n in range(4))
    sum_junk = sb(O_V + 2 * KB, [P, LC], BF16)
    bias_b = sb(O_V, [P, 2 * D])
    bias_row = sb(O_T2 + 8 * KB, [1, 2 * D])
    ab = sb(O_OSB, [P, CT, 2 * D])
    x_sb = sb(O_X, [P, NT, D])
    y_sb = x_sb
    o_ring = [O_KQ, O_KQ + 8 * KB, O_KQ + 16 * KB, O_Y]
    k_ring = [sb(o, [P, L], BF16) for o in o_ring]
    q_ring = [sb(o + 4 * KB, [P, L], BF16) for o in o_ring]
    probs = [sb(O_P + 2 * KB * n, [P, CHUNK]) for n in range(8)]
    o_sb = [sb(O_OSB + 2 * KB * n, [P, CHUNK]) for n in range(2)]
    v_ring = [sb(O_Y + 8 * KB + 2 * KB * b, [P, NT, 32]) for b in range(RING)]
    kv = sb(O_KV, [P, NT, 2 * D])
    kvy = sb(O_SP, [P, 16, 2 * D])
    tab_fwd = sb(O_T1, [P, NF, 3, P])
    tab_inv = sb(O_T2, [P, NF, 2, P])
    mid = Region(O_FR, O_FR + 16 * KB)
    attn = [sb(O_V + KB * b, [P, NT, DH]) for b in range(RING)]
    bo_b, ws_b, fb_b = mid([P, D]), mid([P, D]), mid([P, D])
    wffn_int8, wffn = mid([P, CT, D], I8), mid([P, CT, D], BF16)
    w16, e16 = mid([18, 16]), mid([16, 18])
    c_tiles, w_tiles = mid([16, P]), mid([16, P])
    sign, rj, ri, hh, hf = mid([P, 2]), mid([P, NF, 4]), mid([P, NF, 2]), mid([P, NF, 4]), mid([P, NF, 3])
    u_sb, uT, by_cos, by_sin = mid([P, 18]), mid([18, P]), mid([P, NF, 2]), mid([P, NF, 2])
    nbias = mid([P, NT])
    mv, rstd, expo = mid([P, NT, 2]), mid([P, NT]), mid([P, NT])
    stats = mid([P, NT, 2, 6])
    amax, xscale, xinv = mid([P, NT]), mid([P, NT]), mid([P, NT])
    top, wsum, wrec, nmax = mid([1, 16]), mid([1, 1]), mid([1, 1]), mid([1, 1])
    wrec_b = mid([P, 1])
    small = Region(O_S, O_S + 5 * KB + 700)
    select, identb = small([P, P + 68]), small([P, P], BF16)
    ident, sel = select[:, 0:P], select[:, P:P + 68]
    cols = small([P, 5 * CT])
    rotc, entc, bqc, bkc, bvc = (cols[:, CT * n:CT * n + CT] for n in range(5))
    ones_row = small([1, P])
    mx, negm, mrest = small([P, 2, NT, 2]), small([P, NT]), small([P, NT])
    msplit, mT, recip = small([P, 8, NT], BF16), small([3 * NT, P], BF16), small([P, 2, 4, 4])
    csum, gvec, bb, extra = small([P, CT]), small([P, CT]), small([1, 1]), small([1, 1])
    assert base + O_S + 5 * KB + 700 <= 212863
    x1 = sb(O_X, [P, NT, D])
    spec = sb(O_KV, [P, NF, 5, D])
    gtab = sb(O_KV + 46 * KB, [P, NF, 2, P])
    y1 = sb(O_P, [P, 16, D])
    scr1 = sb(O_Y, [P, 16, D])
    c_row = sb(O_OSB, [1, L])
    junk = sb(O_OSB + 8 * KB, [P, 2, D])
    c2_row, e_row, w_row = (sb(o, [1, L]) for o in (O_Y, O_X, O_X + 8 * KB))
    gtmp = sb(O_OSB, [P, 2, 2, P])
    c_big = sb(O_OSB, [P, 8, D])
    z = sb(O_SP, [P, NF, 2, D])
    zs_a, zs_b = sb(O_SP + 18 * KB, [P, 14, D]), sb(O_X, [P, 16, D])
    x2 = sb(O_Y, [P, NT, D])
    x2b = sb(O_KV, [P, NT, D])
    TILE_OF = [0, 8] + [t for n in range(1, 8) for t in (n, 16 - n)]
    GROUPS = 4
    xq = sb(O_KV + 16 * KB, [P, 4, D])
    xqc = sb(O_KV + 20 * KB, [P, 4, D])
    xqb = sb(O_KV + 24 * KB, [P, NT, D], BF16)
    xqT = sb(O_KV + 32 * KB, [P, NT, D], BF16)
    y3 = sb(O_SP, [P, NT, D])
    x3 = sb(O_X, [P, NT, D])

    ps = ctx.enter_context(nc.psum_tensor("ps", [P, 8, CHUNK], F32))
    mx_ps = [ps[:, 0:2, :], ps[:, 2:4, :]]

    def ex_bank(c, wide):
        return ps[:, c - 2 if wide and c >= 2 else 4 + c % 2, :]

    o_ps = [ps[:, 6 + n, :] for n in range(2)]
    out_t = [ps[:, 6 + n, 0:NT * 17].rearrange("p (s c d) -> p s c d", s=4, d=17) for n in range(2)]
    mt_ps = [ps[:, 6 + n, 384:448].bitcast(BF16) for n in range(2)]

    ks = nc.dram_tensor("k_parts", [3, D, L], BF16, kind="Internal").ap()
    qs = nc.dram_tensor("q_parts", [3, D, L], BF16, kind="Internal").ap()

    sems = {}

    def S(name):
        if name not in sems:
            sems[name] = ctx.enter_context(nc.semaphore(name))
        return sems[name]

    HALF = L // 2
    PIECES = [(0, 0, slice(0, HALF)), (1, 0, slice(0, HALF)), (0, 0, slice(HALF, L)), (1, 0, slice(HALF, L)),
              (0, 1, slice(0, L)), (1, 1, slice(0, L))]
    CTX_BANKS = (4, 5, 7)
    kq_loaded = [S(f"kq_loaded{b}") for b in range(RING)]
    m_rows = [S(f"m_rows{b}") for b in range(RING)]
    parts_out = [S(f"parts_out{c}") for c in range(CT)]

    SLOT_R = {0: 0, 8: 1, 4: 2, 2: 4, 6: 5, 1: 8, 7: 9, 3: 10, 5: 11}
    SLOT_I = {4: 3, 2: 6, 6: 7, 1: 12, 7: 13, 3: 14, 5: 15}
    X_ORDER = [0, 8, 4, 1, 7, 3, 5, 2, 6]
    F_ORDER = [0, 8, 4, 2, 6, 1, 7, 3, 5]

    slot = [zs_a[:, n, :] for n in range(14)] + [zs_b[:, n, :] for n in range(16)]
    F1, F2, G1, G3, SA1, SA2, SB1, SB2 = slot[22:30]
    O = {4: c_big[:, 4, :], 1: y1[:, 4, :], 2: y1[:, 5, :], 3: y1[:, 6, :], 5: y1[:, 7, :], 6: y1[:, 8, :], 7: y1[:, 9, :]}
    SD = c_big[:, 5, :]

    block = ctx.enter_context(nc.Block())

    def load(sp, b, h):
        for r, n, m in K_PARTS:
            sp.dma_start(k_ring[b][r:r + DH * n, :], ks[m:m + n, bass.ds(h * DH, DH), :]).then_inc(kq_loaded[b], 16)
        for r, n, m in Q_PARTS:
            sp.dma_start(q_ring[b][r:r + DH * n, :], qs[m:m + n, bass.ds(h * DH, DH), :]).then_inc(kq_loaded[b], 16)

    def rows(sp, b, h):
        sp.wait_ge(S("mT_copied"), h + 1)
        sp.dma_start(q_ring[b][ROWS:KROWS, :].rearrange("p (t i) -> p t i", i=P), mT[:, :]).then_inc(m_rows[b], 16)

    @block.sync
    def _(sp):
        for n in range(2):
            sp.dma_start(xT[:, 0, HALF * n:HALF * n + HALF], A["xT"][0:P, HALF * n:HALF * n + HALF])\
              .then_inc(S(f"xT_in{n}"), 16)
        sp.dma_start(weights[:, :, :], A["weights"].rearrange("(g p) n -> p g n", p=P)).then_inc(S("weights_in"), 16)
        sp.dma_start(ctxT[:, :, :], A["ctxT"].rearrange("(c p) t -> p c t", p=P)).then_inc(S("ctx_in"), 16)
        sp.dma_start(xT[:, 1, :], A["xT"][P:2 * P, :]).then_inc(S("xT_in2"), 16)
        x_v = A["x"].rearrange("(n p) c -> p n c", p=P)
        for m in range(3):
            if m < 2:
                sp.wait_ge(S(f"part{m + 1}_ready"), 4)
            else:
                sp.wait_ge(S("part3_k"), 2)
            for r, n, first in K_PARTS:
                if first <= m < first + n:
                    sp.dma_start(k_ring[0][r + DH * m:r + DH * m + DH, :], parts[3 + m][0:DH, 0, :])\
                      .then_inc(S("first_loaded"), 16)
            if m == 2:
                sp.wait_ge(S("part3_q"), 2)
            for r, _, part in Q_PARTS:
                if part == m:
                    sp.dma_start(q_ring[0][r:r + DH, :], parts[m][0:DH, 0, :]).then_inc(S("first_loaded"), 16)

        def send_parts(c):
            for n in range(6):
                dst = ks if n >= 3 else qs
                sp.dma_start(dst[n % 3, c * P:(c + 1) * P, :], parts[n][:, c, :]).then_inc(parts_out[c], 16)

        send_parts(0)
        for i in range(4):
            sp.dma_start(x_sb[:, 4 * i:4 * i + 4, :], x_v[:, 4 * i:4 * i + 4, :]).then_inc(S("x_in"), 16)
        sp.wait_ge(parts_out[0], 96)
        load(sp, 1, 1)
        load(sp, 2, 2)
        sp.wait_ge(S("full_ready"), 6)
        load(sp, 3, 3)
        sp.wait_ge(S("part3_late"), 2)
        send_parts(1)
        rows(sp, 0, 0)
        sp.wait_ge(parts_out[1], 96)
        late = [(bo_b, "bo_b"), (ws_b, "ws_b"), (fb_b, "fb_b"), (sign, "tab_sign"), (w16, "tab_w16"), (e16, "tab_e16")]
        for t, name in late:
            sp.dma_start(t[:, :], A[name]).then_inc(S("late_in"), 16)
        sp.dma_start(wffn_int8[:, :, :], A["wffnT_bytes"].bitcast(I8).rearrange("(c p) n -> p c n", p=P))\
          .then_inc(S("late_in"), 16)
        assert len(late) + 1 == LATE_LOADS
        sp.wait_ge(S("kv_ps"), NCT)
        sp.wait_ge(S("csum_ready"), CT)
        sp.dma_start(tab_fwd[:, :, :, :], A["tab_fwd"]).then_inc(S("tabs_in"), 16)
        sp.dma_start(tab_inv[:, :, :, :], A["tab_inv"]).then_inc(S("tabs_in"), 16)

        def step(it, hb, more_rows, more_loads):
            h = it * RING + hb
            if more_rows:
                rows(sp, (hb + 1) % RING, h + 1)
            if more_loads:
                sp.wait_ge(S("quads_done"), (h + 1) * UNITS + 2)
                load(sp, hb % RING, h + RING)

        with sp.Fori(0, LOOPS) as it:
            for hb in range(RING):
                step(it, hb, True, True)
        for hb in range(H - LOOPS * RING):
            h = LOOPS * RING + hb
            step(LOOPS, hb, h + 1 < H, h + RING < H)
        sp.wait_ge(S("corr_tiles"), 1)
        sp.dma_start(c_row[0:1, :].rearrange("p (t i) -> p t i", i=P), c_tiles[:, :]).then_inc(S("corr_sb"), 16)
        sp.wait_ge(S("w_ready"), 1)
        sp.dma_start(w_tiles[:, :], w_row[0:1, :].rearrange("p (t i) -> p t i", i=P)).then_inc(S("w_turned"), 16)
        o_v = out.rearrange("(n p) c -> p n c", p=P)
        stores = 0
        for k in range(GROUPS):
            sp.wait_ge(S("x3_ready"), min(4 * k + 4, NT - 2))
            if k == GROUPS - 1:
                sp.wait_ge(S("x3_last"), 2)
            tiles = sorted(TILE_OF[4 * k:4 * k + 4])
            while tiles:
                n = 2 if len(tiles) > 1 and tiles[1] == tiles[0] + 1 else 1
                r = slice(tiles[0], tiles[0] + n)
                sp.dma_start(o_v[:, r, :], x3[:, r, :]).then_inc(S("stored"), 16)
                stores, tiles = stores + 1, tiles[n:]
        sp.wait_ge(S("stored"), 16 * stores)

    @block.tensor
    def _(pe):
        pe.sem_inc(S("quads_done"), 2)
        pe.wait_ge(S("weights_in"), 16)
        pe.wait_ge(S("cols_in"), 16)
        for e in range(CT):
            for half, (wl, wr) in enumerate(((wkT, wqT), (wvT, wo))):
                for c in range(CT):
                    pe.matmul(ps[:, 4 + e, half * D:(half + 1) * D], wl[:, c, e * P:(e + 1) * P], wr[:, c, :],
                              start=(c == 0), stop=(c == CT - 1))
        for half, (bl, wr) in enumerate(((bkc, wqT), (bvc, wo))):
            for c in range(CT):
                pe.matmul(ps[0:1, 7, half * D:(half + 1) * D], bl[:, c:c + 1], wr[:, c, :],
                          start=(c == 0), stop=(c == CT - 1))
        for e in range(CT):
            for c in range(CT):
                pe.matmul(ps[:, 6, e:e + 1], wkT[:, c, e * P:(e + 1) * P], bqc[:, c:c + 1],
                          start=(c == 0), stop=(c == CT - 1))
        for c in range(CT):
            last = pe.matmul(ps[0:1, 6, 4:5], bkc[:, c:c + 1], bqc[:, c:c + 1], start=(c == 0), stop=(c == CT - 1))
        last.then_inc(S("fold_ps"), 1)

        def context(n):
            t, half, c = n // 4, n // 2 % 2, n % 2
            if n == 0:
                pe.wait_ge(S("ctx_in"), 16)
                pe.wait_ge(S("ones_set"), 1)
                pe.wait_ge(S("fold_sb"), 5)
                pe.matmul(ps[:, 6, :], ones_row[0:1, :], bias_row[0:1, :], start=True, stop=True)\
                  .then_inc(S("fold_ps"), 1)
            if n % 4 == 0 and t >= 3:
                pe.wait_ge(S("kv_sb"), t - 2)
            m = min(P, LC - t * P)
            last = pe.matmul(ps[0:m, CTX_BANKS[t % 3], half * D:(half + 1) * D], ctxT[:, c, t * P:t * P + m],
                             ab[:, c, half * D:(half + 1) * D], start=(c == 0), stop=(c == CT - 1))
            if n % 4 == 3:
                last.then_inc(S("kv_ps"), 1)

        def maxima(b, half, tile, use):
            pe.wait_ge(S("mx_free"), use + 1)
            for n in range(2):
                k0 = half * 1024 + n * CHUNK
                last = pe.matmul(mx_ps[half][:, n, :], q_ring[b][0:ROWS, tile * P:(tile + 1) * P],
                                 k_ring[b][0:ROWS, k0:k0 + CHUNK], start=True, stop=True)
            last.then_inc(S("mx_ready"), 1)

        def turn_maxima(h, bank):
            pe.wait_ge(S("split_ready"), h + 1)
            pe.transpose(mt_ps[bank], msplit[:, :, :].rearrange("p m t -> p (m t)"), identb[:, :])\
              .then_inc(S("mT_ready"), 1)

        def exponents(b, c, j, e, wide):
            if not wide or (j == 0 and c < 2):
                pe.wait_ge(S("probs_ready"), e + 1)
            elif j == 0:
                pe.wait_ge(S("mx_free"), 2 * H * UNITS + 2)
            else:
                pe.wait_ge(S("probs_ready"), e - 1)
            pe.matmul(ex_bank(c, wide), k_ring[b][0:KROWS, j * P:(j + 1) * P],
                      q_ring[b][0:KROWS, c * CHUNK:(c + 1) * CHUNK], start=True, stop=True).then_inc(S("scores_ready"), 1)

        def values(it, n):
            hb, j = n // UNITS, n % UNITS
            if j == 0:
                pe.wait_ge(S("mT_copied"), it * RING + hb + 1)
            pe.wait_ge(S("probs_ready"), (it * (RING * UNITS) + n) * 4 + 6)
            for c in range(4):
                last = pe.matmul(o_ps[hb % 2][32 * c:32 * c + 32, :], v_ring[hb % RING][:, j, :],
                                 probs[4 * (n % 2) + c][:, :], start=(j == 0), stop=(j == UNITS - 1))
            last.then_inc(S("quads_done"), 1)

        def turn_out(h, bank):
            pe.wait_ge(S("o_copied"), h + 1)
            for s in range(4):
                last = pe.matmul(out_t[bank][:, s, :, :], o_sb[bank][:, s * P:(s + 1) * P], sel[:, :],
                                 start=True, stop=True)
            last.then_inc(S("outt_ready"), 1)

        done, FIRST = 0, 4
        for use in range(2 * AHEAD):
            g, half = use // 2, use % 2
            if use == 0:
                pe.wait_ge(S("first_loaded"), 16 * 12)
            if g == UNITS and half == 0:
                pe.wait_ge(kq_loaded[1], 16 * LOADS)
            maxima(g // UNITS, half, g % UNITS, use)
            while use >= FIRST and done < 4 * NCT and done * (2 * UNITS + 2 - FIRST) < (use + 1 - FIRST) * 4 * NCT:
                context(done)
                done += 1
            if use == 2 * UNITS + 1:
                pe.wait_ge(S("consts_in"), 32)
                pe.wait_ge(S("fold_sb"), 6)
                turn_maxima(0, 0)
        pe.wait_ge(S("kv_sb"), NCT)
        pe.wait_ge(S("v_set"), RING)
        pe.wait_ge(S("k_ones"), RING)

        def scores(it, n, c, wide=False):
            hb, j = n // UNITS, n % UNITS
            if j == 0 and c == 0:
                pe.wait_ge(m_rows[hb % RING], (it + hb // RING) * 16 + 16)
            exponents(hb % RING, c, j, it * (RING * UNITS * 4) + 4 * n + c, wide)

        def heads(it, count, last):
            for n in range(count * UNITS):
                hb, j = n // UNITS, n % UNITS
                h = it * RING + hb
                g = n + AHEAD
                more = not last or n + 1 < count * UNITS
                wide = last and n + 1 >= (count - 1) * UNITS
                if more:
                    for c in range(4 if wide else 2):
                        scores(it, n + 1, c, wide)
                if j == 0:
                    pe.wait_ge(S("v_ready"), h + 1)
                values(it, n)
                if more and not wide:
                    scores(it, n + 1, 2)
                    scores(it, n + 1, 3)
                if j == 13 and (not last or hb + 1 < count):
                    pe.wait_ge(S("attn_ready"), h + 1)
                    turn_maxima(h + 1, (hb + 1) % 2)
                if not last or g < count * UNITS:
                    mb, tile, use = g // UNITS % RING, g % UNITS, (it * (RING * UNITS) + g) * 2
                    if tile == 0:
                        nth = it + g // UNITS // RING + (1 if mb else 0)
                        pe.wait_ge(kq_loaded[mb], nth * (16 * LOADS))
                    maxima(mb, 0, tile, use)
                    maxima(mb, 1, tile, use + 1)
                if j == UNITS - 1:
                    turn_out(h, hb % 2)

        for c in range(4):
            scores(0, 0, c)
        with pe.Fori(0, LOOPS) as it:
            heads(it, RING, False)
        heads(LOOPS, H - LOOPS * RING, True)

        def forward(src, cols, f, re, im):
            yr = src[:, SLOT_R[f], cols]
            odd = f not in (0, 8)
            pe.matmul(re, tab_fwd[:, f, 0, :], yr, start=True, stop=not odd)
            if odd:
                pe.matmul(re, tab_fwd[:, f, 2, :], src[:, SLOT_I[f], cols], start=False, stop=True)
            last = pe.matmul(im, tab_fwd[:, f, 1, :], yr, start=True, stop=not odd)
            if odd:
                last = pe.matmul(im, tab_fwd[:, f, 0, :], src[:, SLOT_I[f], cols], start=False, stop=True)
            return last

        pe.wait_ge(S("tabs_in"), 32)
        pe.wait_ge(S("kvy_ready"), 1)
        pe.wait_ge(S("mx_free"), 2 * H * UNITS + 2)
        pe.wait_ge(S("csum_ready"), CT)
        for c in range(CT):
            last = pe.matmul(ps[0:1, 3, 0:1], csum[:, c:c + 1], gvec[:, c:c + 1], start=(c == 0), stop=(c == CT - 1))
        last.then_inc(S("fold_ps"), 1)
        for n, f in enumerate(X_ORDER):
            if n == 3:
                pe.wait_ge(S("fold_sb"), 7)
            if n >= 4:
                pe.wait_ge(S("kf_sb"), n - 3)
            forward(kvy, slice(0, D), f, ps[:, n % 4, 0:D], ps[:, n % 4, D:2 * D]).then_inc(S("kf_ps"), 1)
        pe.wait_ge(S("probs_ready"), H * 64 + 2)
        pe.wait_ge(S("attn_ready"), H + 1)
        for n, f in enumerate(X_ORDER):
            if f == 0:
                pe.wait_ge(S("y1_first"), 1)
            elif f == 4:
                pe.wait_ge(S("y1_four"), 1)
            elif f == 1:
                pe.wait_ge(S("y1_odd"), 1)
            elif f == 2:
                pe.wait_ge(S("y1_two"), 1)
            if n == 4:
                pe.wait_ge(S("kf_sb"), NF)
            elif n == 8:
                pe.wait_ge(S("prod_done"), 2)
            b = (4 + n) % 8
            forward(y1, slice(0, D), f, ps[:, b, 0:D], ps[:, b, D:2 * D]).then_inc(S("x1f_ps"), 1)

        pe.wait_ge(S("rj_ready"), 4)
        o = ps[:, 0, 0:18].rearrange("p (f m) -> p f m", m=2)
        pe.matmul(o, tab_inv[:, 0, 0, :], rj[:, :, 0:2], start=True, stop=False)
        pe.matmul(o, tab_inv[:, 0, 1, :], rj[:, :, 2:4], start=False, stop=True).then_inc(S("u_ps"), 1)
        pe.wait_ge(S("u_sb"), 1)
        pe.transpose(ps[0:18, 1, 0:P], u_sb[:, :], ident[:, :]).then_inc(S("u_ps"), 1)
        pe.wait_ge(S("u_sb"), 2)
        pe.matmul(ps[0:16, 2, 0:P], w16[:, :], uT[:, :], start=True, stop=True).then_inc(S("corr_ps"), 1)
        for n, f in enumerate(F_ORDER):
            b = 3 + n % 4
            if n >= 4:
                pe.wait_ge(S("vf_sb"), 2 * (n - 3))
            forward(kvy, slice(D, 2 * D), f, ps[:, b, 0:D], ps[:, b, D:2 * D]).then_inc(S("vf_ps"), 1)
        pe.wait_ge(S("wrec_ready"), 1)
        pe.matmul(ps[:, 7, 0:1], ones_row[0:1, :], wrec[0:1, :], start=True, stop=True).then_inc(S("wrec_ps"), 1)
        pe.wait_ge(S("w_turned"), 16)
        pe.matmul(ps[:, 0, 0:18], w_tiles[:, :], e16[:, :], start=True, stop=True).then_inc(S("h_ps"), 1)
        pe.wait_ge(S("h_sb"), 4)
        o = ps[:, 1, 0:18].rearrange("p (f m) -> p f m", m=2)
        pe.matmul(o, tab_fwd[:, 0, 0, :], hh[:, :, 0:2], start=True, stop=False)
        pe.matmul(o, tab_fwd[:, 0, 1, :], hh[:, :, 2:4], start=False, stop=True).then_inc(S("h_ps"), 1)
        pe.wait_ge(S("vf_sb"), 2 * NF)
        for n, f in enumerate(F_ORDER):
            pe.wait_ge(S("g_ready"), 2 * (n + 1))
            if n >= 6:
                pe.wait_ge(S("z_sb"), n - 5)
            w = D if f in (0, 8) else 2 * D
            o = ps[:, 2 + n % 6, 0:w]
            if f in (0, 8):
                pe.matmul(o, gtab[:, f, 0, :], spec[:, f, 2, :], start=True, stop=False)
                last = pe.matmul(o, gtab[:, f, 1, :], spec[:, f, 3, :], start=False, stop=True)
            else:
                pe.matmul(o, gtab[:, f, 0, :], spec[:, f, 2:4, :].rearrange("p a c -> p (a c)"), start=True, stop=False)
                last = pe.matmul(o, gtab[:, f, 1, :], spec[:, f, 3:5, :].rearrange("p a c -> p (a c)"),
                                 start=False, stop=True)
            last.then_inc(S("z_ps"), 1)
        pe.wait_ge(S("wffn_ready"), 1)
        pe.wait_ge(S("z_sb"), NF)
        for k in range(GROUPS):
            pe.wait_ge(S("xqb_ready"), k + 1)
            for n in range(4):
                for c in range(CT):
                    o = 128 * n + 64 * c
                    last = pe.transpose(ps[:, k % 2, o:o + 64].bitcast(BF16), xqb[:, 4 * k + n, c * P:(c + 1) * P],
                                        identb[:, :])
            last.then_inc(S("xqT_ps"), 1)
            pe.wait_ge(S("xqT_sb"), k + 1)
            if k >= 2:
                pe.wait_ge(S("y3_made"), 4 * (k - 1))
            for n in range(4):
                for c in range(CT):
                    last = pe.matmul(ps[:, 4 + 2 * (k % 2) + n // 2, n % 2 * D:(n % 2 + 1) * D],
                                     xqT[:, 4 * k + n, c * P:(c + 1) * P], wffn[:, c, :],
                                     start=(c == 0), stop=(c == CT - 1))
            last.then_inc(S("ffn_ps"), 1)

    @block.scalar
    def _(act):
        act.sem_inc(S("probs_ready"), 2)
        act.dma_start(cols[:, :], A["cols"]).then_inc(S("cols_in"), 16)
        act.dma_start(select[:, :], A["tab_select"]).then_inc(S("consts_in"), 16)

        def part(m, n):
            kq, c, r = PIECES[n]
            if m == 0:
                act.wait_ge(S("full_ready"), n + 1)
            elif n < 4:
                act.wait_ge(S("rest_ready"), n + 1)
            else:
                act.wait_ge(S("rest_late"), n - 3)
            act.activation(parts[3 * kq + m][:, c, r], full[kq][:, r], ACT.Copy).then_inc(S(f"part{m + 1}_ready"), 1)

        for m in range(2):
            for n in range(4):
                part(m, n)
        act.wait_ge(S("fold_ps"), 1)
        act.activation(bias_row[0:1, :], ps[0:1, 7, :], ACT.Copy).then_inc(S("fold_sb"), 1)
        for e in range(CT):
            act.activation(ab[:, e, :], ps[:, 4 + e, :], ACT.Copy).then_inc(S("fold_sb"), 1)
        act.activation(gvec[:, :], ps[:, 6, 0:2], ACT.Copy).then_inc(S("fold_sb"), 1)
        act.activation(bb[0:1, :], ps[0:1, 6, 4:5], ACT.Copy).then_inc(S("fold_sb"), 1)
        act.wait_ge(S("fold_ps"), 2)
        act.activation(bias_b[:, :], ps[:, 6, :], ACT.Copy).then_inc(S("fold_sb"), 1)
        act.wait_ge(S("consts_in"), 16)
        act.activation(identb[:, :], ident[:, :], ACT.Copy).then_inc(S("consts_in"), 16)

        def copy_turned(h, bank, sent):
            act.wait_ge(S("mT_ready"), h + 1)
            if sent:
                act.wait_ge(*sent)
            act.activation(mT[:, :], mt_ps[bank][0:3 * NT, :], ACT.Copy).then_inc(S("mT_copied"), 1)

        for t in range(NCT):
            if t in (3, 5):
                part((t - 3) // 2, 4)
                part((t - 3) // 2, 5)
            if t == 9:
                act.wait_ge(S("ctx_in"), 16)
                for c in range(CT):
                    if c:
                        act.wait_ge(S("csum_ready"), c)
                    act.activation(sum_junk[:, :], ctxT[:, c, :], ACT.Copy, accum_out=csum[:, c:c + 1])\
                       .then_inc(S("csum_ready"), 1)
            if t == NCT - 1:
                copy_turned(0, 0, None)
            act.wait_ge(S("kv_ps"), t + 1)
            if t == NCT - 1:
                act.wait_ge(S("kv_zero"), 1)
            n = min(P, LC - t * P)
            act.activation(kv[0:n, t, :], ps[0:n, CTX_BANKS[t % 3], :], ACT.Copy).then_inc(S("kv_sb"), 1)

        act.wait_ge(parts_out[1], 96)

        def exps(it, n, r, wide=False):
            e = it * (RING * UNITS * 4) + 4 * n + r
            if r == 0:
                act.wait_ge(S("quads_done"), it * (RING * UNITS) + n + 1)
            act.wait_ge(S("scores_ready"), e + 1)
            act.activation(probs[4 * (n % 2) + r][:, :], ex_bank(r, wide), ACT.Exp).then_inc(S("probs_ready"), 1)

        def copy_out(h, bank):
            act.wait_ge(S("quads_done"), (h + 1) * UNITS + 2)
            act.activation(o_sb[bank][:, :], o_ps[bank], ACT.Copy).then_inc(S("o_copied"), 1)

        def heads(it, count, last):
            for n in range(count * UNITS):
                hb, j = n // UNITS, n % UNITS
                h = it * RING + hb
                more = not last or n + 1 < count * UNITS
                wide = last and n + 1 >= (count - 1) * UNITS
                if more:
                    exps(it, n + 1, 0, wide)
                    exps(it, n + 1, 1, wide)
                if j == UNITS - 1:
                    copy_out(h, hb % 2)
                if more:
                    exps(it, n + 1, 2, wide)
                    exps(it, n + 1, 3, wide)
                if j == 13 and (not last or hb + 1 < count):
                    copy_turned(h + 1, (hb + 1) % 2, (m_rows[hb % RING], (it + hb // RING) * 16 + 16))

        for r in range(4):
            exps(0, 0, r)
        with act.Fori(0, LOOPS) as it:
            heads(it, RING, False)
        heads(LOOPS, H - LOOPS * RING, True)

        act.wait_ge(S("fold_ps"), 3)
        act.activation(extra[0:1, :], ps[0:1, 3, 0:1], ACT.Copy).then_inc(S("fold_sb"), 1)
        for n, f in enumerate(X_ORDER):
            act.wait_ge(S("kf_ps"), n + 1)
            act.activation(spec[:, f, 0:2, :], ps[:, n % 4, :].rearrange("p (a c) -> p a c", a=2), ACT.Copy)\
               .then_inc(S("kf_sb"), 1)
            if 1 <= n <= 4:
                g = n - 1
                act.wait_ge(S("nbias_ready"), g + 1)
                for t in (8 + 2 * g, 9 + 2 * g):
                    act.activation(x1[:, t, :], y_sb[:, t, :], ACT.Identity, bias=nbias[:, t:t + 1],
                                   scale=rstd[:, t:t + 1]).then_inc(S("x1_act"), 1)
        act.wait_ge(S("u_ps"), 2)
        act.activation(uT[:, :], ps[0:18, 1, 0:P], ACT.Copy).then_inc(S("u_sb"), 1)
        act.wait_ge(S("corr_ps"), 1)
        act.activation(c_tiles[:, :], ps[0:16, 2, 0:P], ACT.Copy).then_inc(S("corr_tiles"), 1)
        for n, f in enumerate(F_ORDER):
            act.wait_ge(S("vf_ps"), n + 1)
            b = 3 + n % 4
            act.activation(spec[:, f, 2:4, :], ps[:, b, :].rearrange("p (a c) -> p a c", a=2), ACT.Copy)\
               .then_inc(S("vf_sb"), 1)
            act.activation(spec[:, f, 4, :], ps[:, b, 0:D], ACT.Copy, scale=-1.0).then_inc(S("vf_sb"), 1)
            if n == 3:
                act.wait_ge(S("nmax_ready"), 1)
                act.wait_ge(S("corr_sb"), 16)
                act.activation(e_row[0:1, :], c_row[0:1, :], ACT.Exp, bias=nmax[0:1, :]).then_inc(S("e_ready"), 1)
        act.wait_ge(S("hf_sb"), 2)
        for n, f in enumerate(F_ORDER):
            if n >= 2:
                act.wait_ge(S("g_ready"), 2 * (n - 1))
            act.activation(gtmp[:, n % 2, :, :], tab_inv[:, f, :, :], ACT.Copy, scale=hf[:, f, 0:1])\
               .then_inc(S("g_tmp"), 1)

        def norm2(k, first, last):
            act.wait_ge(S("nbias2_ready"), k + 1)
            for n in range(4 * k + first, 4 * k + last):
                act.activation(x2[:, n, :], x2[:, n, :], ACT.Identity, bias=nbias[:, n:n + 1],
                               scale=rstd[:, n:n + 1]).then_inc(S("x2_ready"), 1)

        norm2(0, 0, 4)
        for k in range(GROUPS):
            g = slice(4 * k, 4 * k + 4)
            act.wait_ge(S("xinv_ready"), k + 1)
            for n in range(4 * k, 4 * k + 4):
                act.activation(xq[:, n % 4, :], x2[:, n, :], ACT.Copy, bias=ROUND, scale=xinv[:, n:n + 1])\
                   .then_inc(S("xq_ready"), 1)
            if k + 1 < GROUPS:
                norm2(k + 1, 0, 2)
            act.wait_ge(S("xqc_ready"), k + 1)
            act.activation(xqb[:, g, :], xqc[:, :, :], ACT.Copy, bias=-ROUND).then_inc(S("xqb_ready"), 1)
            if k + 1 < GROUPS - 1:
                norm2(k + 1, 2, 4)
            act.wait_ge(S("xqT_ps"), k + 1)
            act.activation(xqT[:, g, :], ps[:, k % 2, :].bitcast(BF16).rearrange("p (n c) -> p n c", n=4),
                           ACT.Copy).then_inc(S("xqT_sb"), 1)
        for n in range(NT - 2):
            if n % 4 == 0:
                act.wait_ge(S("nbias3_ready"), n // 4 + 1)
            act.activation(x3[:, TILE_OF[n], :], y3[:, n, :], ACT.Identity, bias=nbias[:, n:n + 1],
                           scale=rstd[:, n:n + 1]).then_inc(S("x3_ready"), 1)

    @block.gpsimd
    def _(pool):
        chain = [0]

        def link(ins):
            chain[0] += 1
            ins.then_inc(S("pool_chain"), 1)
            pool.wait_ge(S("pool_chain"), chain[0])

        def tt(o, a, b, op):
            return pool.tensor_tensor(o, a, b, op)

        def scaled(o, a, by):
            return pool.tensor_scalar(o, a, by, None, ALU.mult)

        pool.memset(ones_row[:, :], 1.0).then_inc(S("ones_set"), 1)
        pool.memset(kv[:, NCT - 1:NT, :], 0.0).then_inc(S("kv_zero"), 1)
        for n in (0, 2):
            r = PIECES[n][2]
            pool.wait_ge(S("part2_ready"), n + 1)
            tt(parts[2][:, 0, r], full[0][:, r], parts[1][:, 0, r], ALU.subtract).then_inc(S("part3_q"), 1)
        pool.wait_ge(S("part3_q"), 2)
        link(pool.memset(k_ring[2][ROWS:KROWS, :], 1.0))
        pool.sem_inc(S("k_ones"), 1)
        pool.wait_ge(S("full_ready"), 6)
        for b in range(RING):
            pool.memset(v_ring[b][:, :, 16:17], 1.0)
            pool.memset(v_ring[b][:, :, 17:32], 0.0).then_inc(S("v_set"), 1)
        for n in (4, 5):
            kq, c, r = PIECES[n]
            pool.wait_ge(S("part1_ready"), n + 1)
            tt(full[kq][:, r], full[kq][:, r], parts[3 * kq][:, c, r], ALU.subtract).then_inc(S("rest_late"), 1)
        for n in (4, 5):
            kq, c, r = PIECES[n]
            pool.wait_ge(S("rest_late"), n - 3)
            pool.wait_ge(S("part2_ready"), n + 1)
            tt(parts[3 * kq + 2][:, c, r], full[kq][:, r], parts[3 * kq + 1][:, c, r], ALU.subtract)\
                .then_inc(S("part3_late"), 1)
        pool.wait_ge(S("x_in"), 64)

        def take_values(h):
            if h >= RING:
                pool.wait_ge(S("quads_done"), (h - RING + 1) * UNITS + 2)
            pool.tensor_copy(v_ring[h % RING][:, :, 0:DH], x_sb[:, :, h * DH:(h + 1) * DH]).then_inc(S("v_ready"), 1)

        def residual(h):
            pool.wait_ge(S("attn_ready"), h + 2)
            tt(y_sb[:, :, h * DH:(h + 1) * DH], attn[h % RING][:, :, :], x_sb[:, :, h * DH:(h + 1) * DH], ALU.add)\
                .then_inc(S("attn_used"), 1)

        def even_side(x, y, s):
            link(tt(s[:, 0:4, :], y[:, 0:4, :], y[:, 4:8, :], ALU.add))
            link(tt(s[:, 4:8, :], y[:, 0:4, :], y[:, 4:8, :], ALU.subtract))
            link(tt(s[:, 8:10, :], s[:, 0:2, :], s[:, 2:4, :], ALU.add))
            link(tt(y[:, 2:4, :], s[:, 0:2, :], s[:, 2:4, :], ALU.subtract))
            link(tt(y[:, 0, :], s[:, 8, :], s[:, 9, :], ALU.add))
            link(tt(y[:, 1, :], s[:, 8, :], s[:, 9, :], ALU.subtract))
            link(tt(s[:, 8, :], s[:, 5, :], s[:, 7, :], ALU.subtract))
            link(tt(s[:, 9, :], s[:, 5, :], s[:, 7, :], ALU.add))

        def kv_dft():
            x, y, s = kv, kvy, kv
            for c in range(CT):
                pool.wait_ge(parts_out[c], 96)
            link(tt(y[:, 0:8, :], x[:, 0:8, :], x[:, 8:16, :], ALU.add))
            yield
            link(tt(y[:, 8:16, :], x[:, 0:8, :], x[:, 8:16, :], ALU.subtract))
            yield
            even_side(x, y, s)
            link(scaled(s[:, 8:10, :], s[:, 8:10, :], R2))
            link(tt(y[:, 4, :], s[:, 4, :], s[:, 8, :], ALU.add))
            link(tt(y[:, 5, :], s[:, 4, :], s[:, 8, :], ALU.subtract))
            link(tt(y[:, 6, :], s[:, 9, :], s[:, 6, :], ALU.add))
            link(tt(y[:, 7, :], s[:, 9, :], s[:, 6, :], ALU.subtract))
            yield
            for t in range(3):
                link(tt(s[:, t, :], y[:, 9 + t, :], y[:, 15 - t, :], ALU.subtract))
                link(tt(s[:, 3 + t, :], y[:, 9 + t, :], y[:, 15 - t, :], ALU.add))
            link(pool.tensor_copy(s[:, 14, :], y[:, 8, :]))
            link(pool.tensor_copy(s[:, 15, :], y[:, 12, :]))
            yield
            for side, b0, p in ((0, 14, 0), (1, 15, 3)):
                link(scaled(s[:, 6, :], s[:, p + 1, :], R2))
                link(tt(s[:, 7, :], s[:, b0, :], s[:, 6, :], ALU.add))
                if side == 0:
                    link(tt(s[:, 8, :], s[:, b0, :], s[:, 6, :], ALU.subtract))
                else:
                    link(tt(s[:, 8, :], s[:, 6, :], s[:, b0, :], ALU.subtract))
                ca, cb = (C1, S1) if side == 0 else (S1, C1)
                link(scaled(s[:, 9, :], s[:, p, :], ca))
                link(scaled(s[:, 10, :], s[:, p + 2, :], cb))
                link(tt(s[:, 9, :], s[:, 9, :], s[:, 10, :], ALU.add))
                link(scaled(s[:, 10, :], s[:, p, :], cb))
                link(scaled(s[:, 11, :], s[:, p + 2, :], ca))
                link(tt(s[:, 10, :], s[:, 10, :], s[:, 11, :], ALU.subtract))
                o = 8 + 4 * side
                link(tt(y[:, o, :], s[:, 7, :], s[:, 9, :], ALU.add))
                link(tt(y[:, o + 2, :], s[:, 8, :], s[:, 10, :], ALU.add))
                if side == 0:
                    link(tt(y[:, o + 1, :], s[:, 7, :], s[:, 9, :], ALU.subtract))
                    link(tt(y[:, o + 3, :], s[:, 8, :], s[:, 10, :], ALU.subtract))
                else:
                    link(tt(y[:, o + 1, :], s[:, 9, :], s[:, 7, :], ALU.subtract))
                    link(tt(y[:, o + 3, :], s[:, 10, :], s[:, 8, :], ALU.subtract))
                yield
            pool.memset(expo[:, :], -0.5).then_inc(S("kvy_ready"), 1)

        for h in range(RING):
            take_values(h)
        pool.wait_ge(S("v_ready"), RING)
        link(pool.memset(k_ring[3][ROWS:KROWS, :], 1.0))
        pool.sem_inc(S("k_ones"), 1)
        pool.wait_ge(S("kv_sb"), NCT)
        for t in range(NCT):
            n = min(P, LC - t * P)
            ins = tt(kv[0:n, t, :], kv[0:n, t, :], bias_b[0:n, :], ALU.add)
        link(ins)
        pool.sem_inc(S("attn_used"), RING)
        work = kv_dft()
        for h in range(H):
            next(work, None)
            residual(h)
            if h + RING < H:
                take_values(h + RING)
        for _ in work:
            pass

        pairs = lambda a: a.rearrange("p (s t) -> p s t", s=2)

        def difference(g):
            a, b = slice(2 * g, 2 * g + 2), slice(8 + 2 * g, 10 + 2 * g)
            pool.wait_ge(S("x1_dve"), g + 1)
            pool.wait_ge(S("x1_act"), 2 * g + 2)
            tt(y1[:, b, :], x1[:, a, :], x1[:, b, :], ALU.subtract).then_inc(S("y1_diff"), 1)

        for g in range(4):
            r = pairs(rstd[:, :])[:, :, 2 * g:2 * g + 2]
            pool.wait_ge(S("var1"), g + 1)
            v = mv[:, :, 1:2].rearrange("p (s t) m -> p s (t m)", s=2)[:, :, 2 * g:2 * g + 2]
            link(pool.tensor_scalar(r, v, EPS, None, ALU.add))
            tt(r, r, pairs(expo[:, :])[:, :, 2 * g:2 * g + 2], ALU.pow).then_inc(S("var1_root"), 1)
            if g >= 2:
                difference(g - 2)
        difference(2)
        difference(3)
        s, y = scr1, y1
        pool.wait_ge(S("cd_ready"), 2)
        link(tt(s[:, 8:10, :], s[:, 0:2, :], s[:, 2:4, :], ALU.add))
        tt(y[:, 0, :], s[:, 8, :], s[:, 9, :], ALU.add)
        tt(y[:, 1, :], s[:, 8, :], s[:, 9, :], ALU.subtract).then_inc(S("y1_first"), 1)
        tt(y[:, 2:4, :], s[:, 0:2, :], s[:, 2:4, :], ALU.subtract).then_inc(S("y1_four"), 1)
        pool.wait_ge(S("late_in"), 16 * LATE_LOADS)
        pool.wait_ge(S("x1f_ps"), 1)
        link(scaled(bo_b[:, :], bo_b[:, :], 16.0))
        tt(y[:, 0, :], y[:, 0, :], bo_b[:, :], ALU.add).then_inc(S("bo_in"), 1)
        Z = lambda f: z[:, f, 1, :]
        pool.wait_ge(S("z_sb"), 5)
        link(tt(F1, Z(2), Z(6), ALU.add))
        link(tt(F2, Z(2), Z(6), ALU.subtract))
        link(scaled(F1, F1, R2))
        link(tt(G1, F1, Z(4), ALU.add))
        link(tt(G3, F1, Z(4), ALU.subtract))
        pool.wait_ge(S("z_sb"), 7)
        link(tt(SA1, Z(1), Z(7), ALU.add))
        link(tt(SA2, Z(1), Z(7), ALU.subtract))
        pool.wait_ge(S("z_sb"), 9)
        link(tt(SB1, Z(3), Z(5), ALU.add))
        link(tt(SB2, Z(3), Z(5), ALU.subtract))
        link(tt(SD, SA2, SB2, ALU.add))
        link(tt(O[4], SA2, SB2, ALU.subtract))
        pool.sem_inc(S("sines_ready"), 1)

        def inverse_roots(k, name):
            g = slice(4 * k, 4 * k + 4)
            pool.wait_ge(S(name), k + 1)
            link(pool.tensor_scalar(rstd[:, g], mv[:, g, 1], EPS, None, ALU.add))
            tt(rstd[:, g], rstd[:, g], expo[:, g], ALU.pow).then_inc(S(name + "_root"), 1)

        inverse_roots(0, "var2")
        inverse_roots(1, "var2")

        def with_bias(k):
            g = slice(4 * k, 4 * k + 4)
            pool.wait_ge(S("x2_ready"), min(4 * k + 4, NT - 2))
            if k == GROUPS - 1:
                pool.wait_ge(S("x2_last"), 2)
            tt(x2b[:, g, :], x2[:, g, :], fb_b[:, :].unsqueeze(1).broadcast_to([P, 4, D]), ALU.add)\
                .then_inc(S("x2b_ready"), 1)

        def add_x2(k):
            g = slice(4 * k, 4 * k + 4)
            pool.wait_ge(S("x2b_ready"), k + 1)
            pool.wait_ge(S("y3_made"), 4 * k + 4)
            tt(y3[:, g, :], y3[:, g, :], x2b[:, g, :], ALU.add).then_inc(S("y3_ready"), 1)

        for k in range(GROUPS):
            with_bias(k)
            if k >= 2:
                add_x2(k - 2)
            if k + 2 < GROUPS:
                inverse_roots(k + 2, "var2")
        inverse_roots(0, "var3")
        add_x2(2)
        for k in range(1, GROUPS):
            inverse_roots(k, "var3")

    @block.vector
    def _(dve):
        chain = [0]

        def link(ins):
            chain[0] += 1
            ins.then_inc(S("dve_chain"), 1)
            dve.wait_ge(S("dve_chain"), chain[0])

        dve.sem_inc(S("mx_free"), 2)
        dve.sem_inc(S("attn_ready"), 1)
        dve.memset(msplit[:, 3:8, :], 0.0)
        for b in range(2):
            dve.memset(k_ring[b][ROWS:KROWS, :], 1.0).then_inc(S("k_ones"), 1)
        dve.wait_ge(S("cols_in"), 16)

        def full_piece(n):
            kq, c, r = PIECES[n]
            if kq:
                ins = dve.tensor_scalar(full[1][:, r], xT[:, c, r], entc[:, c:c + 1], None, ALU.mult)
            else:
                dve.wait_ge(S(f"xT_in{n // 2}"), 16)
                ins = dve.tensor_scalar(full[0][:, r], xT[:, c, r], rotc[:, c:c + 1], float(DH) ** -0.5, ALU.mult, ALU.mult)
            ins.then_inc(S("full_ready"), 1)

        for n in range(4):
            full_piece(n)
        for n in range(4):
            kq, _, r = PIECES[n]
            dve.wait_ge(S("part1_ready"), n + 1)
            dve.wait_ge(S("full_ready"), n + 1)
            dve.tensor_tensor(full[kq][:, r], full[kq][:, r], parts[3 * kq][:, 0, r], ALU.subtract)\
               .then_inc(S("rest_ready"), 1)
        for n in (1, 3):
            r = PIECES[n][2]
            dve.wait_ge(S("part2_ready"), n + 1)
            dve.wait_ge(S("rest_ready"), n + 1)
            dve.tensor_tensor(parts[5][:, 0, r], full[1][:, r], parts[4][:, 0, r], ALU.subtract).then_inc(S("part3_k"), 1)

        def reduce_max(half, g, use):
            dve.wait_ge(S("mx_ready"), use + 1)
            dve.tensor_reduce(mx[:, g // UNITS % 2, g % UNITS, half:half + 1], mx_ps[half], AX.XY, ALU.max).then_inc(S("mx_free"), 1)

        def split(h, parity, step, first=False):
            def then(ins, n):
                ins.then_inc(S("split_chain"), 1)
                dve.wait_ge(S("split_chain"), h * 4 + n)
            if step == 0:
                dve.wait_ge(S("mx_free"), (h + 1) * (2 * UNITS) + 2)
                then(dve.tensor_reduce(negm[:, :], mx[:, parity, :, :], AX.X, ALU.max, negate=True), 1)
                if not first:
                    dve.wait_ge(S("mT_ready"), h)
                then(dve.tensor_copy(msplit[:, 0, :], negm[:, :]), 2)
                dve.tensor_tensor(mrest[:, :], negm[:, :], msplit[:, 0, :], ALU.subtract).then_inc(S("split_chain"), 1)
            else:
                dve.wait_ge(S("split_chain"), h * 4 + 3)
                then(dve.tensor_copy(msplit[:, 1, :], mrest[:, :]), 4)
                dve.tensor_tensor(msplit[:, 2, :], mrest[:, :], msplit[:, 1, :], ALU.subtract)\
                   .then_inc(S("split_ready"), 1)

        def normalise(b, h, bank):
            dve.wait_ge(S("outt_ready"), h + 1)
            dve.reciprocal(recip[:, bank, :, :], out_t[bank][:, :, :, 16]).then_inc(S("recip_ready"), 1)
            dve.wait_ge(S("recip_ready"), h + 1)
            dve.wait_ge(S("attn_used"), h + 1)
            dve.tensor_tensor(attn[b][:, :, :].rearrange("p (c s) d -> p s c d", s=4), out_t[bank][:, :, :, 0:DH],
                              recip[:, bank, :, :].unsqueeze(3).broadcast_to([P, 4, 4, DH]), ALU.mult)\
               .then_inc(S("attn_ready"), 1)

        for g in range(AHEAD):
            if g == 3:
                dve.wait_ge(S("part3_k"), 2)
                dve.wait_ge(S("part3_q"), 2)
                full_piece(4)
                full_piece(5)
            for half in range(2):
                reduce_max(half, g, 2 * g + half)
                if g == UNITS and half == 0:
                    split(0, 0, 1, True)
            if g == UNITS - 1:
                split(0, 0, 0, True)

        def heads(it, count, last):
            for n in range(count * UNITS):
                g = n + AHEAD
                h_max = it * RING + g // UNITS
                for half in range(2):
                    if not last or g < count * UNITS:
                        reduce_max(half, g, (it * (RING * UNITS) + g) * 2 + half)
                    if half == 0 and g % UNITS == 0 and (not last or g <= count * UNITS):
                        split(h_max - 1, None, 1)
                if g % UNITS == UNITS - 1 and (not last or g < count * UNITS):
                    split(h_max, g // UNITS % 2, 0)
                if last and n == (count - 1) * UNITS + 4:
                    dve.wait_ge(S("attn_used"), H - 1 + RING)
                    for t in range(NT):
                        ins = dve.bn_stats(stats[:, t, 0, :], y_sb[:, t, 0:D - DH])
                    link(ins)
                if n % UNITS == UNITS - 1:
                    hb = n // UNITS
                    normalise(hb % RING, it * RING + hb, hb % 2)

        with dve.Fori(0, LOOPS) as it:
            heads(it, RING, False)
        heads(LOOPS, H - LOOPS * RING, True)

        def moments(src, tiles, name):
            for t in tiles:
                last = dve.bn_stats(stats[:, t, 0, :], src[:, t, :])
            link(last)
            for t in tiles:
                last = dve.bn_aggr(mv[:, t, :], stats[:, t, 0, :])
            last.then_inc(S(name), 1)

        def norm(dst, src, t):
            return dve.tensor_scalar(dst[:, t, :], src[:, t, :], mv[:, t, 0:1], rstd[:, t:t + 1],
                                     ALU.subtract, ALU.mult)

        dve.wait_ge(S("attn_used"), H + RING)
        y, s = y1, scr1

        def ln1_moments(g):
            tiles = (2 * g, 2 * g + 1, 2 * g + 8, 2 * g + 9)
            for t in tiles:
                last = dve.bn_stats(stats[:, t, 1, :], y_sb[:, t, D - DH:D])
            link(last)
            for t in tiles:
                last = dve.bn_aggr(mv[:, t, :], stats[:, t, :, :].rearrange("p a b -> p (a b)"))
            last.then_inc(S("var1"), 1)

        def ln1_norm(g):
            dve.wait_ge(S("var1_root"), g + 1)
            dve.wait_ge(S("var1"), g + 1)
            r = slice(8 + 2 * g, 10 + 2 * g)
            dve.scalar_tensor_tensor(nbias[:, r], mv[:, r, 0], -1.0, rstd[:, r], ALU.mult, ALU.mult)\
               .then_inc(S("nbias_ready"), 1)
            norm(x1, y_sb, 2 * g)
            norm(x1, y_sb, 2 * g + 1).then_inc(S("x1_dve"), 1)

        def ln1_sums(g):
            dve.wait_ge(S("x1_dve"), g + 1)
            dve.wait_ge(S("x1_act"), 2 * g + 2)
            a, b = slice(2 * g, 2 * g + 2), slice(8 + 2 * g, 10 + 2 * g)
            dve.tensor_tensor(y[:, a, :], x1[:, a, :], x1[:, b, :], ALU.add).then_inc(S("y1_sum"), 1)

        def second_stage(n):
            a, b = slice(2 * n, 2 * n + 2), slice(4 + 2 * n, 6 + 2 * n)
            dve.wait_ge(S("y1_sum"), 3 + n)
            dve.tensor_tensor(s[:, a, :], y[:, a, :], y[:, b, :], ALU.add)
            dve.tensor_tensor(s[:, b, :], y[:, a, :], y[:, b, :], ALU.subtract).then_inc(S("cd_ready"), 1)

        ln1_moments(0)
        ln1_moments(1)
        ln1_norm(0)
        ln1_moments(2)
        ln1_norm(1)
        ln1_sums(0)
        ln1_moments(3)
        ln1_norm(2)
        ln1_sums(1)
        ln1_norm(3)
        ln1_sums(2)
        second_stage(0)
        ln1_sums(3)
        second_stage(1)
        dve.wait_ge(S("y1_diff"), 4)
        for t in range(3):
            dve.tensor_tensor(s[:, 10 + t, :], y[:, 9 + t, :], y[:, 15 - t, :], ALU.subtract)
            last = dve.tensor_tensor(s[:, 13 + t, :], y[:, 9 + t, :], y[:, 15 - t, :], ALU.add)
        link(last)

        def stt(o, a, by, b, op):
            return dve.scalar_tensor_tensor(o, a, by, b, ALU.mult, op)

        g0 = junk[:, 0, :]
        g1 = junk[:, 1, :]
        v0, v1, v2, v3 = (c_big[:, n, :] for n in range(4))
        for side in range(2):
            b0, p = y[:, 8 + 4 * side, :], 10 + 3 * side
            ca, cb = (C1, S1) if side == 0 else (S1, C1)
            stt(v0, s[:, p + 1, :], R2, b0, ALU.add)
            if side == 0:
                stt(v1, s[:, p + 1, :], -R2, b0, ALU.add)
            else:
                stt(v1, s[:, p + 1, :], R2, b0, ALU.subtract)
            dve.tensor_scalar(g0, s[:, p + 2, :], cb, None, ALU.mult)
            link(dve.tensor_scalar(g1, s[:, p + 2, :], ca, None, ALU.mult))
            stt(v2, s[:, p, :], ca, g0, ALU.add)
            link(stt(v3, s[:, p, :], cb, g1, ALU.subtract))
            o = 8 + 4 * side
            dve.tensor_tensor(y[:, o, :], v0, v2, ALU.add)
            dve.tensor_tensor(y[:, o + 2, :], v1, v3, ALU.add)
            if side == 0:
                dve.tensor_tensor(y[:, o + 1, :], v0, v2, ALU.subtract)
                last = dve.tensor_tensor(y[:, o + 3, :], v1, v3, ALU.subtract)
            else:
                dve.tensor_tensor(y[:, o + 1, :], v2, v0, ALU.subtract)
                last = dve.tensor_tensor(y[:, o + 3, :], v3, v1, ALU.subtract)
            link(last)
        dve.sem_inc(S("y1_odd"), 1)
        dve.wait_ge(S("cd_ready"), 2)
        d_sub, d_add = c_big[:, 4, :], c_big[:, 5, :]
        dve.tensor_tensor(d_sub, s[:, 5, :], s[:, 7, :], ALU.subtract)
        link(dve.tensor_tensor(d_add, s[:, 5, :], s[:, 7, :], ALU.add))
        stt(y[:, 4, :], d_sub, R2, s[:, 4, :], ALU.add)
        stt(y[:, 5, :], d_sub, -R2, s[:, 4, :], ALU.add)
        stt(y[:, 6, :], d_add, R2, s[:, 6, :], ALU.add)
        stt(y[:, 7, :], d_add, R2, s[:, 6, :], ALU.subtract).then_inc(S("y1_two"), 1)
        for n, f in enumerate(X_ORDER):
            dve.wait_ge(S("kf_sb"), n + 1)
            dve.wait_ge(S("x1f_ps"), n + 1)
            b = (4 + n) % 8
            for m in range(2):
                if n:
                    dve.wait_ge(S("prod_done"), 2 * n - 1 + m)
                dve.tensor_tensor_reduce(out=junk[:, m, :], in0=ps[:, b, m * D:(m + 1) * D], in1=spec[:, f, m, :],
                                         scale=1.0, scalar=0.0, op0=ALU.mult, op1=ALU.add,
                                         accum_out=ri[:, f, m:m + 1]).then_inc(S("prod_done"), 1)
        dve.wait_ge(S("prod_done"), 2 * NF)
        dve.wait_ge(S("fold_sb"), 7)
        link(dve.scalar_tensor_tensor(extra[:, :], bb[:, :], float(LC), extra[:, :], ALU.mult, ALU.add))
        link(dve.scalar_tensor_tensor(ri[0:1, 0, 0:1], extra[:, :], float(L), ri[0:1, 0, 0:1], ALU.mult, ALU.add))
        dve.wait_ge(S("late_in"), 16 * LATE_LOADS)
        dve.tensor_copy(rj[:, :, 0], ri[:, :, 0]).then_inc(S("rj_ready"), 1)
        dve.tensor_scalar(rj[:, :, 1], ri[:, :, 1], sign[:, 1:2], None, ALU.mult).then_inc(S("rj_ready"), 1)
        dve.tensor_scalar(rj[:, :, 2], ri[:, :, 1], sign[:, 0:1], None, ALU.mult).then_inc(S("rj_ready"), 1)
        dve.tensor_copy(rj[:, :, 3], ri[:, :, 0]).then_inc(S("rj_ready"), 1)
        dve.tensor_copy(wffn[:, :, :], wffn_int8[:, :, :]).then_inc(S("wffn_ready"), 1)
        cos_t, sin_t = (tab_fwd[:, :, m, 0:1].broadcast_to([P, NF, 2]) for m in range(2))
        dve.wait_ge(S("u_ps"), 1)
        up = ps[:, 0, 0:18].rearrange("p (f m) -> p f m", m=2)
        uv = u_sb[:, :].rearrange("p (f m) -> p f m", m=2)
        dve.tensor_tensor(by_cos[:, :, :], up, cos_t, ALU.mult)
        link(dve.tensor_tensor(by_sin[:, :, :], up, sin_t, ALU.mult))
        dve.tensor_tensor(uv[:, :, 0], by_cos[:, :, 0], by_sin[:, :, 1], ALU.subtract)
        dve.tensor_tensor(uv[:, :, 1], by_cos[:, :, 1], by_sin[:, :, 0], ALU.add).then_inc(S("u_sb"), 1)
        dve.wait_ge(S("corr_sb"), 16)
        link(dve.max(top[:, 0:8], c_row[:, :]))
        dve.tensor_scalar(nmax[:, :], top[:, 0:1], -1.0, None, ALU.mult).then_inc(S("nmax_ready"), 1)
        link(dve.match_replace(c2_row[:, :], top[:, 0:8], c_row[:, :], NEG))
        link(dve.max(top[:, 8:16], c2_row[:, :]))
        link(dve.memset(top[:, TOPK:16], NEG))
        link(dve.match_replace(w_row[:, :], top[:, 8:16], c2_row[:, :], NEG))
        dve.wait_ge(S("e_ready"), 1)
        dve.scalar_tensor_tensor(w_row[:, :], w_row[:, :], NEG, e_row[:, :], ALU.is_equal, ALU.mult,
                                 accum_out=wsum[:, :]).then_inc(S("w_ready"), 1)
        dve.wait_ge(S("w_ready"), 1)
        dve.reciprocal(wrec[:, :], wsum[:, :]).then_inc(S("wrec_ready"), 1)
        dve.wait_ge(S("wrec_ps"), 1)
        link(dve.tensor_copy(wrec_b[:, :], ps[:, 7, 0:1]))
        hp = ps[:, 0, 0:18].rearrange("p (f m) -> p f m", m=2)
        dve.wait_ge(S("h_ps"), 1)
        dve.scalar_tensor_tensor(by_cos[:, :, :], hp, wrec_b[:, 0:1], cos_t, ALU.mult, ALU.mult)
        link(dve.scalar_tensor_tensor(by_sin[:, :, :], hp, wrec_b[:, 0:1], sin_t, ALU.mult, ALU.mult))
        dve.tensor_tensor(hh[:, :, 0], by_cos[:, :, 0], by_sin[:, :, 1], ALU.subtract).then_inc(S("h_sb"), 1)
        dve.tensor_tensor(hh[:, :, 1], by_cos[:, :, 1], by_sin[:, :, 0], ALU.add).then_inc(S("h_sb"), 1)
        stt(hh[:, :, 2], by_sin[:, :, 0], -1.0, by_cos[:, :, 1], ALU.subtract).then_inc(S("h_sb"), 1)
        dve.tensor_tensor(hh[:, :, 3], by_cos[:, :, 0], by_sin[:, :, 1], ALU.subtract).then_inc(S("h_sb"), 1)
        hp2 = ps[:, 1, 0:18].rearrange("p (f m) -> p f m", m=2)
        dve.wait_ge(S("h_ps"), 2)
        dve.tensor_copy(hf[:, :, 0:2], hp2).then_inc(S("hf_sb"), 1)
        dve.tensor_scalar(hf[:, :, 2], hp2[:, :, 1], -1.0, None, ALU.mult).then_inc(S("hf_sb"), 1)
        dve.wait_ge(S("hf_sb"), 2)
        for n, f in enumerate(F_ORDER):
            dve.wait_ge(S("g_tmp"), n + 1)
            stt(gtab[:, f, 0, :], tab_inv[:, f, 1, :], hf[:, f, 2:3], gtmp[:, n % 2, 0, :], ALU.add).then_inc(S("g_ready"), 1)
            stt(gtab[:, f, 1, :], tab_inv[:, f, 0, :], hf[:, f, 1:2], gtmp[:, n % 2, 1, :], ALU.add).then_inc(S("g_ready"), 1)
        def take(n):
            f = F_ORDER[n]
            dve.wait_ge(S("z_ps"), n + 1)
            r, i = SLOT_R[f], SLOT_I.get(f)
            o = ps[:, 2 + n % 6, :]
            if i is None:
                ins = stt(z[:, f, 0, :], y1[:, r, :], 1.0 / 16, o[:, 0:D], ALU.add)
            else:
                ins = stt(z[:, f, :, :], y1[:, r:i + 1:i - r, :], 1.0 / 8, o.rearrange("p (a c) -> p a c", a=2), ALU.add)
            ins.then_inc(S("z_sb"), 1)

        C = lambda f: z[:, f, 0, :]
        tt = lambda o, a, b, op: dve.tensor_tensor(o, a, b, op)
        E = slot[0:9]
        A1, A2, B1, B2, P1, P2, Q1, Q2, E0, V0, V1, V2, V3 = slot[9:22]
        dve.wait_ge(S("bo_in"), 1)
        take(0)
        take(1)
        dve.wait_ge(S("z_sb"), 2)
        tt(A1, C(0), C(8), ALU.add)
        link(tt(A2, C(0), C(8), ALU.subtract))
        take(2)
        dve.wait_ge(S("z_sb"), 3)
        tt(E0, A1, C(4), ALU.add)
        tt(E[2], A1, C(4), ALU.subtract)
        take(3)
        take(4)
        dve.wait_ge(S("z_sb"), 5)
        tt(B1, C(2), C(6), ALU.add)
        link(tt(B2, C(2), C(6), ALU.subtract))
        stt(E[1], B2, R2, A2, ALU.add)
        stt(E[3], B2, -R2, A2, ALU.add)
        tt(E[0], E0, B1, ALU.add)
        tt(E[4], E0, B1, ALU.subtract)
        take(5)
        take(6)
        dve.wait_ge(S("z_sb"), 7)
        tt(P1, C(1), C(7), ALU.add)
        tt(P2, C(1), C(7), ALU.subtract)
        take(7)
        take(8)
        dve.wait_ge(S("z_sb"), 9)
        tt(Q1, C(3), C(5), ALU.add)
        link(tt(Q2, C(3), C(5), ALU.subtract))
        tt(V0, P1, Q1, ALU.subtract)
        tt(V1, P1, Q1, ALU.add)
        dve.tensor_scalar(V2, Q2, S1, None, ALU.mult)
        link(dve.tensor_scalar(V3, Q2, C1, None, ALU.mult))
        stt(A1, P2, C1, V2, ALU.add)
        stt(A2, P2, S1, V3, ALU.subtract)
        stt(E[6], V0, -R2, E[2], ALU.add)
        link(tt(E[8], E[0], V1, ALU.subtract))
        stt(E[2], V0, R2, E[2], ALU.add)
        tt(E[0], E[0], V1, ALU.add)
        tt(E[7], E[1], A1, ALU.subtract)
        link(tt(E[5], E[3], A2, ALU.subtract))
        tt(E[1], E[1], A1, ALU.add)
        tt(E[3], E[3], A2, ALU.add)
        dve.wait_ge(S("sines_ready"), 1)
        W1, W2, H1, H3 = (y1[:, n, :] for n in range(4))
        dve.tensor_scalar(W1, SB1, C1, None, ALU.mult)
        dve.tensor_scalar(W2, SB1, S1, None, ALU.mult)
        stt(O[2], SD, R2, F2, ALU.add)
        link(stt(O[6], SD, R2, F2, ALU.subtract))
        stt(H1, SA1, S1, W1, ALU.add)
        link(stt(H3, SA1, C1, W2, ALU.subtract))
        tt(O[1], H1, G1, ALU.add)
        tt(O[7], H1, G1, ALU.subtract)
        tt(O[3], H3, G3, ALU.add)
        link(tt(O[5], H3, G3, ALU.subtract))

        def group_out(k):
            for n in range(2 * k, 2 * k + 2):
                if n == 0:
                    dve.tensor_copy(x2[:, 0, :], E[0])
                    last = dve.tensor_copy(x2[:, 1, :], E[8])
                else:
                    tt(x2[:, 2 * n, :], E[n], O[n], ALU.add)
                    last = tt(x2[:, 2 * n + 1, :], E[n], O[n], ALU.subtract)
            link(last)
            moments(x2, range(4 * k, 4 * k + 4), "var2")

        def negated_mean(k, name, done):
            g = slice(4 * k, 4 * k + 4)
            dve.wait_ge(S(name), k + 1)
            dve.wait_ge(S(name + "_root"), k + 1)
            dve.scalar_tensor_tensor(nbias[:, g], mv[:, g, 0], -1.0, rstd[:, g], ALU.mult, ALU.mult)\
               .then_inc(S(done), 1)

        def scale_out(k):
            dve.wait_ge(S("ffn_ps"), k + 1)
            for n in range(4):
                t = 4 * k + n
                dve.scalar_tensor_tensor(y3[:, t, :], ps[:, 4 + 2 * (k % 2) + n // 2, n % 2 * D:(n % 2 + 1) * D],
                                         xscale[:, t:t + 1], ws_b[:, :], ALU.mult, ALU.mult)\
                   .then_inc(S("y3_made"), 1)

        def moments3(k):
            dve.wait_ge(S("y3_ready"), k + 1)
            moments(y3, range(4 * k, 4 * k + 4), "var3")

        group_out(0)
        group_out(1)
        negated_mean(0, "var2", "nbias2_ready")
        for k in range(GROUPS):
            g = slice(4 * k, 4 * k + 4)
            if k + 1 < GROUPS:
                negated_mean(k + 1, "var2", "nbias2_ready")
            if k + 1 == GROUPS - 1:
                for n in (NT - 2, NT - 1):
                    norm(x2, x2, n).then_inc(S("x2_last"), 1)
            dve.wait_ge(S("x2_ready"), min(4 * k + 4, NT - 2))
            if k == GROUPS - 1:
                dve.wait_ge(S("x2_last"), 2)
            link(dve.tensor_reduce(amax[:, g], x2[:, g, :], AX.X, ALU.max, apply_absolute_value=True))
            link(dve.tensor_scalar(xscale[:, g], amax[:, g], 1e-6, 1.0 / 127.0, ALU.max, ALU.mult))
            dve.reciprocal(xinv[:, g], xscale[:, g]).then_inc(S("xinv_ready"), 1)
            if k >= 2:
                scale_out(k - 2)
            if k + 2 < GROUPS:
                group_out(k + 2)
            if k == 3:
                moments3(0)
            dve.wait_ge(S("xq_ready"), 4 * k + 4)
            if k:
                dve.wait_ge(S("xqb_ready"), k)
            dve.tensor_scalar(xqc[:, :, :], xq[:, :, :], ROUND - 128.0, ROUND + 127.0, ALU.max, ALU.min)\
               .then_inc(S("xqc_ready"), 1)
        scale_out(2)
        moments3(1)
        negated_mean(0, "var3", "nbias3_ready")
        moments3(2)
        negated_mean(1, "var3", "nbias3_ready")
        scale_out(3)
        dve.wait_ge(S("x2b_ready"), 4)
        dve.wait_ge(S("y3_made"), NT)
        dve.tensor_tensor(y3[:, 12:16, :], y3[:, 12:16, :], x2b[:, 12:16, :], ALU.add).then_inc(S("y3_ready"), 1)
        negated_mean(2, "var3", "nbias3_ready")
        moments3(3)
        negated_mean(3, "var3", "nbias3_ready")
        for n in (NT - 2, NT - 1):
            dve.tensor_scalar(x3[:, TILE_OF[n], :], y3[:, n, :], mv[:, n, 0:1], rstd[:, n:n + 1],
                              ALU.subtract, ALU.mult).then_inc(S("x3_last"), 1)


def kernel(**inputs):
    import concourse.bacc as bacc
    from concourse.bass_utils import run_bass_kernel_spmd

    a = {k: np.asarray(v) for k, v in inputs.items()}

    def cols(v):
        return np.ascontiguousarray(v.reshape(CT, P).T)

    def rows_of(v):
        return np.ascontiguousarray(np.broadcast_to(v[None, :], (P, v.shape[0])))

    arrays = {
        "x": a["x"][0], "xT": a["x"][0].T, "ctxT": a["ctx_1024"][0].T,
        "cols": np.concatenate([cols(a[n].reshape(-1)) for n in (
            "L0_attn_rotation_params", "L0_attn_entangle_params", "L0_xattn_bq", "L0_xattn_bk", "L0_xattn_bv")], 1),
        "weights": np.concatenate([a["L0_xattn_Wk"].T, a["L0_xattn_Wq"].T, a["L0_xattn_Wv"].T, a["L0_xattn_Wo"]], 0),
        "bo_b": rows_of(a["L0_xattn_bo"]), "ws_b": rows_of(a["L0_ffn_weight_scale"]), "fb_b": rows_of(a["L0_ffn_bias"]),
        "wffnT_bytes": np.ascontiguousarray(a["L0_ffn_weight_q"].T).view(np.int32),
        **tables(),
    }
    arrays = {k: np.ascontiguousarray(v) for k, v in arrays.items()}
    nc = bacc.Bacc("TRN2", target_bir_lowering=False, num_devices=1)
    handles = {k: nc.dram_tensor(k, v.shape, mybir.dt.from_np(v.dtype), kind="ExternalInput").ap()
               for k, v in arrays.items()}
    result = nc.dram_tensor("layer_out", [L, D], F32, kind="ExternalOutput").ap()
    decoder_layer(nc, handles, result)
    r = run_bass_kernel_spmd(nc, [arrays], core_ids=[0])
    return r.results[0]["layer_out"].reshape(1, L, D)
```
